# Optimizing a Trainium2 kernel written in Bass

```python
import numpy as np
import jax
import jax.numpy as jnp

def _softmax(x, axis=-1):
    return jax.nn.softmax(x, axis=axis)

def _gelu(x):
    return jax.nn.gelu(x, approximate=True)

def _silu(x):
    return jax.nn.silu(x)

def _sigmoid(x):
    return jax.nn.sigmoid(x)

def _layernorm(x, axis=-1, eps=1e-05):
    m = jnp.mean(x, axis=axis, keepdims=True)
    v = jnp.var(x, axis=axis, keepdims=True)
    return (x - m) / jnp.sqrt(v + eps)

def _scatter_add(tgt, idx, src, axis=0):
    return tgt.at[idx].add(src)

def _segment_sum(src, seg, n):
    return jax.ops.segment_sum(src, seg, n)
kernel_name = 'mk_xattn_ffn_d1_seqx_r2_94b504'

def setup_inputs(seed: int=0):
    np.random.seed(seed)
    _w = jnp.asarray

    def _rec_inputs():
        import jax
        import jax.numpy as jnp
        _rk = jax.random.key(seed)
        x = -0.0002928 + 1 * jax.random.normal(jax.random.fold_in(_rk, 1), (32, 256, 512), jnp.float32)
        _lenS = 256 - jax.random.randint(jax.random.fold_in(_rk, 7), (32,), 0, max(1, 256 // 4) + 1, jnp.int32)
        _lenS2 = 256 - jax.random.randint(jax.random.fold_in(_rk, 8), (32,), 0, max(1, 256 // 4) + 1, jnp.int32)
        _ctx_1024P = jax.random.normal(jax.random.fold_in(_rk, 11), (32, 16, 512), jnp.float32)
        _ctx_1024c = jax.random.dirichlet(jax.random.fold_in(_rk, 511), 0.3 * jnp.ones((16,), jnp.float32), (32, 256))
        _ctx_1024t = jnp.einsum('bsk,bkd->bsd', _ctx_1024c, _ctx_1024P)
        _ctx_1024t = _ctx_1024t * jax.lax.rsqrt(jnp.mean(jnp.square(_ctx_1024t)) + 1e-12) * 0.953939
        ctx_1024 = -1.39393e-06 + 0.999914 * (_ctx_1024t + 0.3 * jax.random.normal(jax.random.fold_in(_rk, 611), (32, 256, 512), jnp.float32))
        _validS = jnp.arange(256)[None, :] < _lenS[:, None]
        _validS2 = jnp.arange(256)[None, :] < _lenS2[:, None]
        _causal = jnp.tril(jnp.ones((256, 256), dtype=bool))
        mask_BxS2_bf1 = jnp.ones((32, 256), dtype=bool)
        mask_BxSxS2_bk0 = jnp.logical_not(jnp.broadcast_to(_validS2[:, None, :], (32, 256, 256)))
        return (x, ctx_1024, mask_BxS2_bf1, mask_BxSxS2_bk0)
    x, ctx_1024, mask_BxS2_bf1, mask_BxSxS2_bk0 = _rec_inputs()

    def _L0_xattn_setup():
        import math
        import jax, jax.numpy as jnp
        import numpy as np
        NUM_HEADS = 16
        EMBED_DIM = 512
        HEAD_DIM = EMBED_DIM // NUM_HEADS
        N, S = (2, 1024)

        def _mha(Q, K, V, Wq, Wk, Wv, Wo, padding_mask, attention_mask):
            n, s, e = Q.shape
            q = (Q @ Wq.T).reshape(n, s, NUM_HEADS, HEAD_DIM).transpose(0, 2, 1, 3)
            k = (K @ Wk.T).reshape(n, s, NUM_HEADS, HEAD_DIM).transpose(0, 2, 1, 3)
            v = (V @ Wv.T).reshape(n, s, NUM_HEADS, HEAD_DIM).transpose(0, 2, 1, 3)
            scores = jnp.einsum('nhqd,nhkd->nhqk', q, k) / math.sqrt(HEAD_DIM)
            neg_inf = jnp.float32(-jnp.inf)
            pm = padding_mask[:, None, :, None]
            scores = jnp.where(pm, scores, neg_inf)
            scores = jnp.where(attention_mask[:, None, :, :], scores, neg_inf)
            attn = jax.nn.softmax(scores, axis=-1)
            attn = jnp.where(jnp.isnan(attn), 0.0, attn)
            out = jnp.einsum('nhqk,nhkd->nhqd', attn, v)
            out = out.transpose(0, 2, 1, 3).reshape(n, s, e)
            out = out @ Wo.T
            return out
        key = jax.random.key(seed)
        ks = jax.random.split(key, 7)
        scale = 1.0 / math.sqrt(EMBED_DIM)
        Q = jax.random.normal(ks[0], (N, S, EMBED_DIM), dtype=jnp.float32)
        K = jax.random.normal(ks[1], (N, S, EMBED_DIM), dtype=jnp.float32)
        V = jax.random.normal(ks[2], (N, S, EMBED_DIM), dtype=jnp.float32)
        Wq = jax.random.normal(ks[3], (EMBED_DIM, EMBED_DIM), dtype=jnp.float32) * scale
        Wk = jax.random.normal(ks[4], (EMBED_DIM, EMBED_DIM), dtype=jnp.float32) * scale
        Wv = jax.random.normal(ks[5], (EMBED_DIM, EMBED_DIM), dtype=jnp.float32) * scale
        Wo = jax.random.normal(ks[6], (EMBED_DIM, EMBED_DIM), dtype=jnp.float32) * scale
        padding_mask = jnp.ones((N, S), dtype=bool)
        attention_mask = jnp.broadcast_to(jnp.tril(jnp.ones((S, S), dtype=bool)), (N, S, S))
        return {'Q': Q, 'K': K, 'V': V, 'Wq': Wq, 'Wk': Wk, 'Wv': Wv, 'Wo': Wo, 'padding_mask': padding_mask, 'attention_mask': attention_mask}
    _L0_xattn_all = _L0_xattn_setup()
    _L0_xattn_in = {k: v for k, v in _L0_xattn_all.items() if k in ('Wq', 'Wk', 'Wv', 'Wo')}
    del _L0_xattn_all

    def _L0_ffn_setup():
        import math
        import jax, jax.numpy as jnp
        import numpy as np
        D_CONTENT = 512
        D_POSITION = 32
        NUM_TILES = 8
        BATCH = 8
        SEQ = 1024

        def make_pe(seq_len, d_pos):
            pos = jnp.arange(seq_len, dtype=jnp.float32)[:, None]
            div = jnp.exp(jnp.arange(0, d_pos, 2, dtype=jnp.float32) * (-math.log(10000.0) / d_pos))
            ang = pos * div
            pe = jnp.zeros((seq_len, d_pos), dtype=jnp.float32)
            pe = pe.at[:, 0::2].set(jnp.sin(ang))
            pe = pe.at[:, 1::2].set(jnp.cos(ang))
            return pe
        key = jax.random.key(seed)
        k1, k2, k3, k4 = jax.random.split(key, 4)
        x = jax.random.normal(k1, (BATCH, SEQ, D_CONTENT), dtype=jnp.float32)
        tile_sigs = jax.random.normal(k2, (NUM_TILES, D_POSITION), dtype=jnp.float32)
        lim = 1.0 / math.sqrt(D_CONTENT)
        W = jax.random.uniform(k3, (NUM_TILES, D_CONTENT, D_CONTENT), minval=-lim, maxval=lim, dtype=jnp.float32)
        b = jax.random.uniform(k4, (NUM_TILES, D_CONTENT), minval=-lim, maxval=lim, dtype=jnp.float32)
        return {'x': x, 'tile_sigs': tile_sigs, 'W': W, 'b': b}
    _L0_ffn_all = _L0_ffn_setup()
    _L0_ffn_in = {k: v for k, v in _L0_ffn_all.items() if k in ('tile_sigs', 'W', 'b')}
    del _L0_ffn_all
    return {'x': x, 'ctx_1024': ctx_1024, 'mask_BxS2_bf1': mask_BxS2_bf1, 'mask_BxSxS2_bk0': mask_BxSxS2_bk0, 'L0_xattn_Wq': _L0_xattn_in['Wq'], 'L0_xattn_Wk': _L0_xattn_in['Wk'], 'L0_xattn_Wv': _L0_xattn_in['Wv'], 'L0_xattn_Wo': _L0_xattn_in['Wo'], 'L0_ffn_tile_sigs': _L0_ffn_in['tile_sigs'], 'L0_ffn_W': _L0_ffn_in['W'], 'L0_ffn_b': _L0_ffn_in['b']}

def reference(x, ctx_1024, mask_BxS2_bf1, mask_BxSxS2_bk0, L0_xattn_Wq, L0_xattn_Wk, L0_xattn_Wv, L0_xattn_Wo, L0_ffn_tile_sigs, L0_ffn_W, L0_ffn_b):
    import jax
    import jax.numpy as jnp

    def _L0_xattn_ref(Q, K, V, Wq, Wk, Wv, Wo, padding_mask, attention_mask):
        import math
        import jax, jax.numpy as jnp
        import numpy as np
        NUM_HEADS = 16
        EMBED_DIM = 512
        HEAD_DIM = EMBED_DIM // NUM_HEADS
        N, S = (2, 1024)

        def _mha(Q, K, V, Wq, Wk, Wv, Wo, padding_mask, attention_mask):
            n, s, e = Q.shape
            q = (Q @ Wq.T).reshape(n, s, NUM_HEADS, HEAD_DIM).transpose(0, 2, 1, 3)
            k = (K @ Wk.T).reshape(n, s, NUM_HEADS, HEAD_DIM).transpose(0, 2, 1, 3)
            v = (V @ Wv.T).reshape(n, s, NUM_HEADS, HEAD_DIM).transpose(0, 2, 1, 3)
            scores = jnp.einsum('nhqd,nhkd->nhqk', q, k) / math.sqrt(HEAD_DIM)
            neg_inf = jnp.float32(-jnp.inf)
            pm = padding_mask[:, None, :, None]
            scores = jnp.where(pm, scores, neg_inf)
            scores = jnp.where(attention_mask[:, None, :, :], scores, neg_inf)
            attn = jax.nn.softmax(scores, axis=-1)
            attn = jnp.where(jnp.isnan(attn), 0.0, attn)
            out = jnp.einsum('nhqk,nhkd->nhqd', attn, v)
            out = out.transpose(0, 2, 1, 3).reshape(n, s, e)
            out = out @ Wo.T
            return out
        return _mha(Q, K, V, Wq, Wk, Wv, Wo, padding_mask, attention_mask)

    def _L0_ffn_ref(x, tile_sigs, W, b):
        import math
        import jax, jax.numpy as jnp
        import numpy as np
        D_CONTENT = 512
        D_POSITION = 32
        NUM_TILES = 8
        BATCH = 8
        SEQ = 1024

        def make_pe(seq_len, d_pos):
            pos = jnp.arange(seq_len, dtype=jnp.float32)[:, None]
            div = jnp.exp(jnp.arange(0, d_pos, 2, dtype=jnp.float32) * (-math.log(10000.0) / d_pos))
            ang = pos * div
            pe = jnp.zeros((seq_len, d_pos), dtype=jnp.float32)
            pe = pe.at[:, 0::2].set(jnp.sin(ang))
            pe = pe.at[:, 1::2].set(jnp.cos(ang))
            return pe
        B, S, D = x.shape
        P = tile_sigs.shape[1]
        pe = make_pe(S, P)
        scores = jnp.einsum('sp,tp->st', pe, jnp.sign(tile_sigs))
        idx = jnp.argmax(scores, axis=-1)
        y_all = jnp.einsum('bsd,tod->bsto', x, W) + b
        idx4 = jnp.broadcast_to(idx[None, :, None, None], (B, S, 1, D))
        out = jnp.take_along_axis(y_all, idx4, axis=2)[:, :, 0]
        return out
    x = x + _L0_xattn_ref(_layernorm(x, axis=-1), ctx_1024, ctx_1024, L0_xattn_Wq, L0_xattn_Wk, L0_xattn_Wv, L0_xattn_Wo, mask_BxS2_bf1, mask_BxSxS2_bk0)
    x = x + _L0_ffn_ref(_layernorm(x, axis=-1), L0_ffn_tile_sigs, L0_ffn_W, L0_ffn_b)
    return x

_drawn_inputs = setup_inputs


def setup_inputs(seed=0):
    import zlib

    import numpy as np

    out = dict(_drawn_inputs(seed))
    spreads = {}
    factors = {'L0_ffn_b': 2.862}
    for name, (base, spread) in spreads.items():
        noise = np.random.default_rng([zlib.crc32(name.encode()), seed]).standard_normal(out[name].shape)
        drawn = base * np.exp(spread * noise) if base else spread * noise
        out[name] = jnp.asarray(drawn.astype(out[name].dtype))
    for name, factor in factors.items():
        out[name] = (out[name] * factor).astype(out[name].dtype)
    return out
```

```python
from contextlib import ExitStack

import numpy as np

import concourse.bass as bass
from concourse import mybir

F32 = mybir.dt.float32
F32R = mybir.dt.float32r
I32 = mybir.dt.int32
U32 = mybir.dt.uint32
U8 = mybir.dt.uint8
ALU = mybir.AluOpType
ACT = mybir.ActivationFunctionType
AX = mybir.AxisListType

P = 128
B, S, DM = 32, 256, 512
H, DH = 16, 32
KC = DM // P
HG = P // DH
BK = 64
NBLKS = S // BK
SCALE = float(DH) ** -0.5
EPS = 1e-5
BIG = 3e38
FLOOR = -1e38
TINY = 1e-30
NE, DP = 8, 32
PB = P // B
NR = (S + NE * (PB - 1)) // PB - 0
NR = 70 if NR > 70 else NR
OOB = 1 << 20


def wait_alone(eng, sem, value, passed):
    wait(eng, sem, value)
    if not isinstance(value, int):
        eng.sem_inc(passed, 1)


def wait(eng, sem, value):
    if isinstance(value, int) and value <= 0:
        return
    eng.wait_ge(sem, value)


class Drains:

    def __init__(self, prologue, step, last, bank_of, signals):
        self.prologue, self.step, self.last = prologue, step, last
        self.bank_of, self.signals = bank_of, signals

    def uses(self, names, bank):
        return sum(bank in self.bank_of(n) for n in names)

    def before(self, kind, i, name, bank):
        names = {"prologue": self.prologue, "step": self.step, "last": self.last}[kind]
        here = self.uses(names[:names.index(name)], bank)
        if kind == "prologue":
            return self.signals * here
        first = self.uses(self.prologue, bank)
        return i * (self.signals * self.uses(self.step, bank)) + self.signals * (first + here)

    def after(self, kind, i, name, bank):
        return self.before(kind, i, name, bank) + self.signals


def t_banks(name):
    if name.startswith("PT"):
        return (0, 1)
    if name.startswith(("XT", "OT")):
        return (int(name[2]) % 2,)
    return ()


A_BANK = {"K": 0, "V": 0, "PV0": 1, "Q0": 1, "OP0": 0, "PV1": 1, "Q1": 0, "OP1": 1, "PV2": 0, "Q2": 1,
          "OP2": 0, "PV3": 1, "Q3": 0, "OP3": 1}


def a_banks(name):
    key = name[0] if name[0] in "KV" else name
    return (A_BANK[key],) if key in A_BANK else ()


class Form:

    def __init__(self, nb, nbk, depth):
        self.nb, self.nbk, self.depth = nb, nbk, depth
        self.groups = B // nb
        self.c = 2 * nb
        self.slots = nb * nbk
        self.nt = self.slots // 2
        self.first_block = NBLKS - nbk
        c, nt, nbk = self.c, self.nt, self.nbk
        pt = lambda q: [f"PT{q}.{n}" for n in range(nbk)]
        sc = lambda q: [f"S{q}.{n}" for n in range(nbk)]
        kt, vt = [f"K{t}" for t in range(nt)], [f"V{t}" for t in range(nt)]
        if depth == 2:
            self.prologue = kt + ["XT0", "XT1"] + vt + ["XT2", "XT3", "Q0", "Q1", "Q2", "Q3"] + sc(0)
            self.step = (sc(1) + pt(0) + kt + ["XT0", "XT1", "PV0"] + vt + ["XT2", "XT3"] + sc(2)
                         + ["Q0", "OT0"] + pt(1) + ["OP0", "PV1"] + sc(3)
                         + ["Q1", "OT1"] + pt(2) + ["OP1", "PV2", "Q2", "OT2"] + pt(3)
                         + ["OP2", "PV3", "Q3", "OT3"] + sc(0) + ["OP3"])
            self.last = (sc(1) + pt(0) + ["PV0"] + sc(2) + ["OT0"] + pt(1) + ["OP0", "PV1"] + sc(3)
                         + ["OT1"] + pt(2) + ["OP1", "PV2", "OT2"] + pt(3) + ["OP2", "PV3", "OT3", "OP3"])
        else:
            self.prologue = []
            self.step = kt + vt + ["XT0", "XT1", "Q0", "Q1", "Q2", "Q3"]
            for q in range(c):
                self.step += sc(q) + pt(q) + [f"PV{q}", f"OT{q}", f"OP{q}"]
            self.last = self.step
        self.t = Drains(self.prologue, self.step, self.last, t_banks, 2)
        self.a = Drains(self.prologue, self.step, self.last, a_banks, 1)


def kernel_program(nc, x, ctx_t, mask, pad, wq, wk, wv, wo, sigs_t, wf, bf, ident_d, route_d, pe_t, out):
    x1 = nc.dram_tensor("x1_scratch", (B * S, DM), F32, kind="Internal").ap()
    top = ExitStack()
    with top:
        def sb(name, shape, dt=F32, stack=top):
            return stack.enter_context(nc.sbuf_tensor(name, shape, dt))

        def sem(name):
            return top.enter_context(nc.semaphore(name))

        pS = top.enter_context(nc.psum_tensor("pS", [P, 2, 2 * 512], F32))
        pT = top.enter_context(nc.psum_tensor("pT", [P, 2, 512], F32))
        pA = top.enter_context(nc.psum_tensor("pA", [P, 2, 512], F32))

        ident = sb("ident", [P, P])
        neg_half = sb("neg_half", [P, 1])
        gather_rows = sb("gather_rows", [P, NR], I32)
        scatter_rows = sb("scatter_rows", [P, NR], I32)
        expert_of = sb("expert_of", [1, NR], I32)
        short_flag = sb("short_flag", [1, 1], I32)

        attn_stack = ExitStack()
        w_hi = {n: sb(f"w{n}_hi", [P, KC, DM], F32R, attn_stack) for n in "qkvo"}
        w_lo = {n: sb(f"w{n}_lo", [P, KC, DM], F32R, attn_stack) for n in "qkvo"}

        prep = ExitStack()
        w_raw = sb("w_raw", [P, 4, KC * DM], F32, prep)
        mask_early = sb("mask_early", [P, NBLKS - 1, B * 2 * BK], U8, prep)
        NROUTE = route_d.shape[1]
        route = sb("route", [P, NROUTE], F32, prep)
        pe_sb = sb("pe_sb", [DP, S], F32, prep)
        sig = sb("sig", [DP, NE], F32, prep)
        sgn = sb("sgn", [DP, 3, NE], F32, prep)
        rt = sb("rt", [P, 2, 8, NE], F32, prep)
        cnt = sb("cnt", [P, 4, NE + 1], F32, prep)
        cnt_i = sb("cnt_i", [P, 2, NE], I32, prep)
        r1 = sb("r1", [P, 2, 4], F32, prep)
        match = sb("match", [P, 2, PB * NR], F32, prep)
        rows_f = sb("rows_f", [P, 2, NR], F32, prep)
        expert_f = sb("expert_f", [1, NE, NR], F32, prep)
        early = sb("early", [P, 1], F32, prep)
        early2 = sb("early2", [1, 1], F32, prep)

        o = 0
        def part(n, o=o):
            nonlocal_offset[0] += n
            return route[:, nonlocal_offset[0] - n:nonlocal_offset[0]]
        nonlocal_offset = [0]
        c_before = part(P)
        c_ones = part(P)
        c_slot = part(PB * NR)
        c_pos = part(2 * PB * P)
        c_place = part(PB * P)
        c_expert = part(NE)
        c_batch = part(1)
        c_block = part(NR)

        mask_loaded = sem("mask_loaded")
        consts_loaded = sem("consts_loaded")
        w_loaded = [sem(f"w_loaded_{n}") for n in "qkvo"]
        w_hi_ready = sem("w_hi_ready")
        w_lo_ready = sem("w_lo_ready")
        half_set = sem("half_set")
        pool_passed, dve_passed, sync_passed = sem("pool_passed"), sem("dve_passed"), sem("sync_passed")
        early_max = sem("early_max")
        early_sum = sem("early_sum")
        flag_ready = sem("flag_ready")
        rv = sem("route_vector")
        rp = sem("route_product")

        with nc.Block() as block:
            @block.sync
            def _(sp):
                sp.dma_start(mask_early[:], mask[0:NBLKS - 1].rearrange("k p b q j -> p k (b q j)")).then_inc(mask_loaded, 16)
                sp.dma_start(ident[:], ident_d).then_inc(consts_loaded, 16)
                sp.dma_start(route[:], route_d).then_inc(consts_loaded, 16)
                sp.dma_start(pe_sb[:], pe_t).then_inc(consts_loaded, 16)
                sp.dma_start(sig[:], sigs_t).then_inc(consts_loaded, 16)
                for n, w in enumerate((wq, wk, wv, wo)):
                    sp.dma_start(w_raw[:, n, :].rearrange("p (c n) -> p c n", c=KC),
                                 w.rearrange("(c p) n -> p c n", p=P)).then_inc(w_loaded[n], 16)

            @block.gpsimd
            def _(pool):
                pool.memset(neg_half[:], -0.5).then_inc(half_set, 1)
                pool.wait_ge(half_set, 1)

            @block.scalar
            def _(act):
                for n, k in enumerate("qkvo"):
                    act.wait_ge(w_loaded[n], 16)
                    act.copy(w_hi[k][:].rearrange("p c n -> p (c n)"), w_raw[:, n, :]).then_inc(w_hi_ready, 1)
                act.wait_ge(w_hi_ready, 4)

            @block.vector
            def _(dve):
                step = [0]

                def done(ins):
                    step[0] += 1
                    ins.then_inc(rv, 1)
                    dve.wait_ge(rv, step[0])

                dve.wait_ge(consts_loaded, 64)
                done(dve.tensor_scalar(sgn[:, 0, :], sig[:], 0.0, None, ALU.is_gt))
                done(dve.tensor_scalar(sgn[:, 1, :], sig[:], 0.0, None, ALU.is_lt))
                done(dve.tensor_tensor(sgn[:, 2, :], sgn[:, 0, :], sgn[:, 1, :], ALU.subtract))
                dve.wait_ge(mask_loaded, 16)
                dve.tensor_reduce(early[:], mask_early[:].rearrange("p k n -> p (k n)").bitcast(U32), AX.X, ALU.max)\
                    .then_inc(early_max, 1)
                dve.wait_ge(rp, 1)
                for h in range(2):
                    sc = pA[:, h, 0:NE]
                    done(dve.tensor_reduce(r1[:, h, 0:1], sc, AX.X, ALU.max))
                    done(dve.tensor_scalar(rt[:, h, 0, :], sc, r1[:, h, 0:1], None, ALU.is_equal))
                    done(dve.scalar_tensor_tensor(rt[:, h, 1, :], rt[:, h, 0, :], -float(NE), c_expert, ALU.mult, ALU.add))
                    done(dve.tensor_scalar(rt[:, h, 6, :], c_expert, float(NE), None, ALU.add))
                    done(dve.tensor_scalar(rt[:, h, 1, :], rt[:, h, 1, :], float(NE), None, ALU.add))
                    done(dve.tensor_reduce(r1[:, h, 1:2], rt[:, h, 1, :], AX.X, ALU.min))
                    done(dve.tensor_scalar(rt[:, h, 2, :], c_expert, r1[:, h, 1:2], None, ALU.is_equal))
                dve.wait_ge(rp, 2)
                done(dve.tensor_scalar(cnt_i[:, 0, :], pA[:, 0, 256:256 + NE], float(PB - 1), None, ALU.add))
                done(dve.tensor_scalar(cnt_i[:, 1, :], cnt_i[:, 0, :], 2, None, ALU.arith_shift_right))
                done(dve.tensor_copy(cnt[:, 0, 0:NE], cnt_i[:, 1, :]))
                done(dve.memset(cnt[:, 1, 0:1], 0.0))
                for t in range(NE):
                    done(dve.tensor_tensor(cnt[:, 1, t + 1:t + 2], cnt[:, 1, t:t + 1], cnt[:, 0, t:t + 1], ALU.add))
                for h in range(2):
                    done(dve.scalar_tensor_tensor(rt[:, h, 3, :], cnt[:, 1, 0:NE], float(PB),
                                                  pA[:, 1, 64 + 64 * h:64 + 64 * h + NE], ALU.mult, ALU.add))
                    done(dve.tensor_tensor(rt[:, h, 4, :], rt[:, h, 3, :], rt[:, h, 2, :], ALU.mult))
                    done(dve.tensor_reduce(r1[:, h, 2:3], rt[:, h, 4, :], AX.X, ALU.add))
                    done(dve.tensor_scalar(match[:, h, :], c_slot, r1[:, h, 2:3], None, ALU.is_equal))
                dve.wait_ge(rp, 3)
                done(dve.tensor_scalar(rows_f[:, 0, :], pT[:, 0, 0:NR], c_batch, None, ALU.add))
                done(dve.tensor_scalar(rows_f[:, 1, :], pT[:, 1, 0:NR], -float(OOB), float(OOB), ALU.mult, ALU.add))
                done(dve.tensor_copy(gather_rows[:], rows_f[:, 0, :]))
                done(dve.tensor_tensor(scatter_rows[:], rows_f[:, 0, :], rows_f[:, 1, :], ALU.add))
                done(dve.tensor_scalar(expert_f[0:1, 0, :], c_block[0:1, :], 0.0, None, ALU.mult))
                for t in range(1, NE):
                    done(dve.scalar_tensor_tensor(expert_f[0:1, t, :], c_block[0:1, :], cnt[0:1, 1, t:t + 1],
                                                  expert_f[0:1, t - 1, :], ALU.is_ge, ALU.add))
                done(dve.tensor_copy(expert_of[:], expert_f[0:1, NE - 1, :]))
                dve.wait_ge(early_sum, 1)
                dve.tensor_scalar(short_flag[:], pS[0:1, 0, 0:1], 0.0, None, ALU.is_equal).then_inc(flag_ready, 1)
                for n, k in enumerate("qkvo"):
                    dve.wait_ge(w_hi_ready, n + 1)
                    dve.tensor_tensor(w_lo[k][:].rearrange("p c n -> p (c n)"), w_raw[:, n, :],
                                      w_hi[k][:].rearrange("p c n -> p (c n)").bitcast(F32), ALU.subtract)\
                        .then_inc(w_lo_ready, 1)
                dve.wait_ge(w_lo_ready, 4)
                dve.wait_ge(flag_ready, 1)

            @block.tensor
            def _(pe):
                pe.wait_ge(rv, 3)
                pe.wait_ge(consts_loaded, 64)
                for h in range(2):
                    mm = pe.matmul(pA[:, h, 0:NE], pe_sb[:, h * P:(h + 1) * P], sgn[:, 2, :], start=True, stop=True)
                mm.then_inc(rp, 1)
                pe.wait_ge(early_max, 1)
                pe.matmul(pS[0:1, 0, 0:1], early[:], c_ones[:, 0:1], start=True, stop=True).then_inc(early_sum, 1)
                pe.wait_ge(rv, 17)
                oh = [rt[:, h, 2, :] for h in range(2)]
                pe.matmul(pA[:, 0, 256:256 + NE], c_ones, oh[0], start=True, stop=False)
                pe.matmul(pA[:, 0, 256:256 + NE], c_ones, oh[1], start=False, stop=True)
                pe.matmul(pA[:, 1, 64:64 + NE], c_before, oh[0], start=True, stop=True)
                pe.matmul(pA[:, 1, 128:128 + NE], c_ones, oh[0], start=True, stop=False)
                pe.matmul(pA[:, 1, 128:128 + NE], c_before, oh[1], start=False, stop=True).then_inc(rp, 1)
                pe.wait_ge(rv, 17 + 4 + NE + 8)
                for k in range(2 * PB):
                    h, i = divmod(k, PB)
                    m = match[:, h, i * NR:(i + 1) * NR]
                    pe.matmul(pT[:, 0, 0:NR], c_pos[:, (h * PB + i) * P:(h * PB + i + 1) * P], m,
                              start=(k == 0), stop=(k == 2 * PB - 1))
                for k in range(2 * PB):
                    h, i = divmod(k, PB)
                    mm = pe.matmul(pT[:, 1, 0:NR], c_place[:, i * P:(i + 1) * P], match[:, h, i * NR:(i + 1) * NR],
                                   start=(k == 0), stop=(k == 2 * PB - 1))
                mm.then_inc(rp, 1)
        prep.close()

        SHORT, FULL = Form(2, 1, 2), Form(1, NBLKS, 1)
        for f, tag in ((SHORT, "s"), (FULL, "f")):
            st = ExitStack()
            d = f.depth
            f.x_sb = sb(f"x_{tag}", [P, d, f.c, DM], F32, st)
            f.ctx_raw = sb(f"ctx_raw_{tag}", [P, f.slots, KC, BK], F32, st)
            f.ctx_hi = sb(f"ctx_hi_{tag}", [P, KC, f.slots, BK], F32R, st)
            f.ctx_lo = sb(f"ctx_lo_{tag}", [P, KC, f.slots, BK], F32R, st)
            f.mask_u8 = sb(f"mask_u8_{tag}", [P, f.c, f.nbk, BK], U8, st)
            f.pad_u8 = sb(f"pad_u8_{tag}", [P, f.c], U8, st)
            f.pad_big = sb(f"pad_big_{tag}", [P, f.c], F32, st)
            f.bias = sb(f"bias_{tag}", [P, d, f.c, f.nbk, BK], F32, st)
            f.stat = sb(f"stat_{tag}", [P, f.c, 6], F32, st)
            f.mom = sb(f"mom_{tag}", [P, f.c, 2], F32, st)
            f.rstd = sb(f"rstd_{tag}", [P, f.c, 2], F32, st)
            f.xn = sb(f"xn_{tag}", [P, f.c, DM], F32, st)
            f.xt_hi = sb(f"xt_hi_{tag}", [P, KC, f.c * P], F32R, st)
            f.xt_lo = sb(f"xt_lo_{tag}", [P, KC, f.c * P], F32R, st)
            f.qt = sb(f"qt_{tag}", [P, d, KC, f.c * P], F32, st)
            f.kd = sb(f"kd_{tag}", [P, d, f.slots, KC, HG * BK], F32, st)
            f.vd = sb(f"vd_{tag}", [P, d, f.slots, H // 2, 2 * DH], F32, st)
            f.s_sb = sb(f"s_{tag}", [P, d, f.nbk, H * BK], F32, st)
            f.row = sb(f"row_{tag}", [P, 2, 4, H], F32, st)
            f.pt = sb(f"pt_{tag}", [P, f.nbk, H // 2, P], F32, st)
            f.o_sb = sb(f"o_{tag}", [P, DM], F32, st)
            f.ot_hi = sb(f"ot_hi_{tag}", [P, KC, P], F32R, st)
            f.ot_lo = sb(f"ot_lo_{tag}", [P, KC, P], F32R, st)
            f.y_sb = sb(f"y_{tag}", [P, 2, DM], F32, st)
            st.close()
        attn_stack.close()

        zeroed = sem("zeroed")
        x_loaded = [[sem(f"x_loaded_{d}{q}") for q in range(SHORT.c)] for d in range(2)]
        ctx_loaded = sem("ctx_loaded")
        mask_in = sem("mask_in")
        ctx_hi_ready = sem("ctx_hi_ready")
        ctx_lo_ready = sem("ctx_lo_ready")
        stat_ready = sem("stat_ready")
        mom_ready = sem("mom_ready")
        var_ready = sem("var_ready")
        rstd_ready = sem("rstd_ready")
        xn_ready = sem("xn_ready")
        pad_ready = sem("pad_ready")
        bias_ready = sem("bias_ready")
        xt_done = sem("xt_done")
        k_done = sem("k_done")
        v_done = sem("v_done")
        q_done = sem("q_done")
        s_done = sem("s_done")
        s_drained = sem("s_drained")
        max_ready = sem("max_ready")
        shifted = sem("shifted")
        exp_ready = sem("exp_ready")
        sum_ready = sem("sum_ready")
        floored = sem("floored")
        inv_ready = sem("inv_ready")
        pt_done = sem("pt_done")
        pv_done = sem("pv_done")
        ot_done = sem("ot_done")
        ot_hi_ready = sem("ot_hi_ready")
        op_done = sem("op_done")
        xt_hi_ready = sem("xt_hi_ready")
        t_drained = [sem(f"t_drained_{b}") for b in range(2)]
        a_drained = [sem(f"a_drained_{b}") for b in range(2)]
        y_stored = [sem(f"y_stored_{b}") for b in range(2)]

        def sync_part(sp, f):
            c = f.c

            def load_x(g, d, q):
                row = sp.snap(g * (c * P) + q * P) if not isinstance(g, int) else g * c * P + q * P
                if not (isinstance(g, int) and g < f.depth):
                    i = g - f.depth
                    name = f"OP{q}"
                    wait(sp, a_drained[a_banks(name)[0]], f.a.after("step", i, name, a_banks(name)[0]))
                sp.dma_start(f.x_sb[:, d, q, :], x[bass.ds(row, P), :]).then_inc(x_loaded[d][q], 16)

            def first_batch(g):
                return g * f.nb if isinstance(g, int) else sp.snap(g * f.nb)

            def load_ctx(g):
                b0 = first_batch(g)
                wait(sp, ctx_lo_ready, g)
                for b in range(f.nb):
                    for n in range(f.nbk):
                        sp.dma_start(f.ctx_raw[:, b * f.nbk + n, :, :],
                                     ctx_t[bass.ds(b0 + b, 1), f.first_block + n].rearrange("a p c k -> (a p) c k"))\
                            .then_inc(ctx_loaded, 16)

            def load_mask(g):
                b0 = first_batch(g)
                wait_alone(sp, bias_ready, g * c, sync_passed)
                for n in range(f.nbk):
                    sp.dma_start(f.mask_u8[:, :, n, :],
                                 mask[f.first_block + n, :, bass.ds(b0, f.nb)].rearrange("p b q k -> p (b q) k"))\
                        .then_inc(mask_in, 16)
                sp.dma_start(f.pad_u8[:], pad[:, bass.ds(b0, f.nb)].rearrange("p b q -> p (b q)")).then_inc(mask_in, 16)

            def store_y(kind, i, q):
                name = f"OP{q}"
                b = a_banks(name)[0]
                row = sp.snap(i * (c * P) + q * P) if not isinstance(i, int) else i * c * P + q * P
                wait(sp, a_drained[b], f.a.after(kind, i, name, b))
                sp.dma_start(x1[bass.ds(row, P), :], f.y_sb[:, q % 2, :]).then_inc(y_stored[q % 2], 16)

            def loads(g, d):
                load_ctx(g)
                load_mask(g)
                for q in range(c):
                    load_x(g, d, q)

            def step(kind, i, d, ahead):
                g = i + f.depth
                if ahead:
                    load_ctx(g)
                    load_mask(g)
                for q in range(c):
                    store_y(kind, i, q)
                    if ahead:
                        load_x(g, d, q)

            if f.depth == 2:
                loads(0, 0)
                loads(1, 1)
                step("step", 0, 0, True)
                step("step", 1, 1, True)
                with sp.Fori(1, f.groups // 2 - 1) as j:
                    step("step", 2 * j, 0, True)
                    step("step", 2 * j + 1, 1, True)
                step("step", f.groups - 2, 0, False)
                step("last", f.groups - 1, 1, False)
            else:
                loads(0, 0)
                step("step", 0, 0, True)
                with sp.Fori(1, f.groups - 1) as i:
                    step("step", i, 0, True)
                step("last", f.groups - 1, 0, False)
            for b in range(2):
                sp.wait_ge(y_stored[b], 16 * f.groups * c // 2)

        def gpsimd_part(pool, f):
            c = f.c
            for d in range(f.depth):
                pool.memset(f.kd[:, d], 0.0).then_inc(zeroed, 1)
                pool.memset(f.vd[:, d], 0.0).then_inc(zeroed, 1)

            def ctx_low(g):
                wait(pool, ctx_hi_ready, g + 1)
                pool.tensor_tensor(f.ctx_lo[:].rearrange("p c s k -> p s c k"), f.ctx_raw[:],
                                   f.ctx_hi[:].bitcast(F32).rearrange("p c s k -> p s c k"), ALU.subtract)\
                    .then_inc(ctx_lo_ready, 1)

            def normalise(g, d):
                for q in range(c):
                    n = g * c + q
                    wait_alone(pool, mom_ready, n + 1, pool_passed)
                    pool.tensor_scalar(f.rstd[:, q, 0:1], f.mom[:, q, 1:2], EPS, None, ALU.add).then_inc(var_ready, 1)
                    pool.wait_ge(var_ready, n + 1)
                    pool.tensor_tensor(f.rstd[:, q, 1:2], f.rstd[:, q, 0:1], neg_half[:], ALU.pow).then_inc(rstd_ready, 1)
                    wait(pool, xt_done, n + 1 - c)
                    wait_alone(pool, rstd_ready, n + 1, pool_passed)
                    pool.tensor_scalar(f.xn[:, q, :], f.x_sb[:, d, q, :], f.mom[:, q, 0:1], f.rstd[:, q, 1:2],
                                       ALU.subtract, ALU.mult).then_inc(xn_ready, 1)

            def mask_bias(g, d):
                wait_alone(pool, mask_in, 16 * (f.nbk + 1) * (g + 1), pool_passed)
                pool.tensor_scalar(f.pad_big[:], f.pad_u8[:], BIG, None, ALU.mult).then_inc(pad_ready, 1)
                wait(pool, s_drained, (g + 1 - f.depth) * (c * f.nbk))
                wait_alone(pool, pad_ready, g + 1, pool_passed)
                for q in range(c):
                    pool.tensor_scalar(f.bias[:, d, q].rearrange("p n k -> p (n k)"),
                                       f.mask_u8[:, q].rearrange("p n k -> p (n k)"),
                                       f.pad_big[:, q:q + 1], -BIG, ALU.mult, ALU.add).then_inc(bias_ready, 1)

            if f.depth == 2:
                ctx_low(0)
                normalise(0, 0)
                mask_bias(0, 0)
                ctx_low(1)

                def step(i, d, ctx_next):
                    normalise(i + 1, 1 - d)
                    mask_bias(i + 1, 1 - d)
                    if ctx_next:
                        ctx_low(i + 2)

                step(0, 0, True)
                step(1, 1, True)
                with pool.Fori(1, f.groups // 2 - 1) as j:
                    step(2 * j, 0, True)
                    step(2 * j + 1, 1, True)
                step(f.groups - 2, 0, False)
            else:
                def group(i):
                    ctx_low(i)
                    normalise(i, 0)
                    mask_bias(i, 0)

                group(0)
                with pool.Fori(1, f.groups) as i:
                    group(i)

        def scalar_part(act, f):
            c = f.c

            def ctx_high(g):
                act.wait_ge(ctx_loaded, 16 * f.slots * (g + 1))
                wait(act, v_done, f.nt * g)
                act.copy(f.ctx_hi[:].rearrange("p c s k -> p s c k"), f.ctx_raw[:]).then_inc(ctx_hi_ready, 1)

            def xt_high(g, q):
                act.wait_ge(xt_done, g * c + q + 1)
                act.copy(f.xt_hi[:, :, q * P:(q + 1) * P], pT[:, q % 2, :].rearrange("p (c n) -> p c n", c=KC))\
                    .then_inc(xt_hi_ready, 1)

            def k_copy(g, d):
                if isinstance(g, int) and g == 0:
                    act.wait_ge(zeroed, 2 * f.depth)
                for t in range(f.nt):
                    act.wait_ge(k_done, g * f.nt + t + 1)
                    for h in range(HG):
                        r = slice(h * DH, (h + 1) * DH)
                        ins = None
                        src = pA[r, a_banks("K0")[0], :].rearrange("p (c s k) -> p c s k", c=KC, s=2)
                        for s in range(2):
                            ins = act.copy(f.kd[r, d, 2 * t + s, :, h * BK:(h + 1) * BK], src[:, :, s, :])
                    ins.then_inc(a_drained[a_banks("K0")[0]], 1)

            def v_copy(g, d):
                for t in range(f.nt):
                    act.wait_ge(v_done, g * f.nt + t + 1)
                    src = pA[:, a_banks("V0")[0], :].rearrange("p (r e c) -> p r e c", r=H // 2, e=2)
                    for s in range(2):
                        for e in range(2):
                            ins = act.copy(f.vd[e * BK:(e + 1) * BK, d, 2 * t + s, :, e * DH:(e + 1) * DH],
                                           src[s * BK:(s + 1) * BK, :, e, :])
                    ins.then_inc(a_drained[a_banks("V0")[0]], 1)

            def q_copy(g, d, m):
                act.wait_ge(q_done, g * KC + m + 1)
                b = a_banks(f"Q{m}")[0]
                act.copy(f.qt[:, d, m, :], pA[:, b, 0:c * P]).then_inc(a_drained[b], 1)

            def exps(i, q):
                act.wait_ge(shifted, (i * c + q + 1) * f.nbk)
                t = f.s_sb[:, q % f.depth]
                act.activation(t, t, ACT.Exp, scale=-SCALE).then_inc(exp_ready, 1)

            def pt_copy(i, q):
                for n in range(f.nbk):
                    act.wait_ge(pt_done, (i * c + q) * f.nbk + n + 1)
                    act.copy(f.pt[:, n, 0:4, :].rearrange("p r n -> p (r n)"), pT[:, 0, :]).then_inc(t_drained[0], 2)

            def ot_high(i, q):
                act.wait_ge(ot_done, i * c + q + 1)
                wait(act, op_done, i * c + q)
                act.copy(f.ot_hi[:].rearrange("p c n -> p (c n)"), pT[:, q % 2, :]).then_inc(ot_hi_ready, 1)

            if f.depth == 2:
                def first():
                    ctx_high(0)
                    k_copy(0, 0)
                    xt_high(0, 0)
                    xt_high(0, 1)
                    v_copy(0, 0)
                    ctx_high(1)
                    xt_high(0, 2)
                    xt_high(0, 3)
                    for m in range(KC):
                        q_copy(0, 0, m)
                    exps(0, 0)

                def step(i, d, nxt, ctx_next):
                    g, e = i + 1, 1 - d
                    pt_copy(i, 0)
                    if nxt:
                        k_copy(g, e)
                    if nxt:
                        xt_high(g, 0)
                        xt_high(g, 1)
                    exps(i, 1)
                    if nxt:
                        v_copy(g, e)
                        xt_high(g, 2)
                        xt_high(g, 3)
                        if ctx_next:
                            ctx_high(i + 2)
                        q_copy(g, e, 0)
                    ot_high(i, 0)
                    exps(i, 2)
                    pt_copy(i, 1)
                    if nxt:
                        q_copy(g, e, 1)
                    ot_high(i, 1)
                    exps(i, 3)
                    pt_copy(i, 2)
                    if nxt:
                        q_copy(g, e, 2)
                    ot_high(i, 2)
                    pt_copy(i, 3)
                    if nxt:
                        q_copy(g, e, 3)
                    ot_high(i, 3)
                    if nxt:
                        exps(g, 0)

                first()
                step(0, 0, True, True)
                step(1, 1, True, True)
                with act.Fori(1, f.groups // 2 - 1) as j:
                    step(2 * j, 0, True, True)
                    step(2 * j + 1, 1, True, True)
                step(f.groups - 2, 0, True, False)
                step(f.groups - 1, 1, False, False)
            else:
                def group(i):
                    ctx_high(i)
                    k_copy(i, 0)
                    v_copy(i, 0)
                    for q in range(c):
                        xt_high(i, q)
                    for m in range(KC):
                        q_copy(i, 0, m)
                    for q in range(c):
                        exps(i, q)
                        pt_copy(i, q)
                        ot_high(i, q)

                group(0)
                with act.Fori(1, f.groups) as i:
                    group(i)

        def vector_part(dve, f):
            c = f.c

            def moments(g, d, q):
                n = g * c + q
                dve.wait_ge(x_loaded[d][q], (16 // f.depth) * (g - d) + 16)
                dve.bn_stats(f.stat[:, q, :], f.x_sb[:, d, q, :]).then_inc(stat_ready, 1)
                wait(dve, xn_ready, n + 1 - c)
                wait_alone(dve, stat_ready, n + 1, dve_passed)
                dve.bn_aggr(f.mom[:, q, :], f.stat[:, q, :]).then_inc(mom_ready, 1)

            def xt_low(g, q):
                dve.wait_ge(xt_hi_ready, g * c + q + 1)
                t = slice(q * P, (q + 1) * P)
                dve.tensor_tensor(f.xt_lo[:, :, t], pT[:, q % 2, :].rearrange("p (c n) -> p c n", c=KC),
                                  f.xt_hi[:, :, t].bitcast(F32), ALU.subtract).then_inc(t_drained[q % 2], 2)

            def mask_scores(i, d, q):
                n = i * c + q
                dve.wait_ge(bias_ready, n + 1)
                for k in range(f.nbk):
                    u = n * f.nbk + k
                    dve.wait_ge(s_done, u + 1)
                    ring = (q * f.nbk + k) % 2
                    dve.tensor_tensor(f.s_sb[:, q % f.depth, k, :].rearrange("p (h k) -> p h k", h=H),
                                      pS[:, ring, :].rearrange("p (h k) -> p h k", h=H),
                                      f.bias[:, d, q, k:k + 1, :].broadcast_to([P, H, BK]), ALU.add).then_inc(s_drained, 1)
                dve.wait_ge(s_drained, (n + 1) * f.nbk)
                t = f.s_sb[:, q % f.depth].rearrange("p n (h k) -> p h n k", h=H)
                dve.tensor_reduce(f.row[:, q % 2, 0, :], t, AX.XY, ALU.max).then_inc(max_ready, 1)
                dve.wait_ge(max_ready, n + 1)
                for k in range(f.nbk):
                    t = f.s_sb[:, q % f.depth, k, :].rearrange("p (h k) -> p h k", h=H)
                    dve.scalar_tensor_tensor(t, f.row[:, q % 2, 0, :].unsqueeze(2).broadcast_to([P, H, BK]), FLOOR, t,
                                             ALU.max, ALU.subtract).then_inc(shifted, 1)

            def pt_copy(i, q):
                for n in range(f.nbk):
                    dve.wait_ge(pt_done, (i * c + q) * f.nbk + n + 1)
                    dve.tensor_copy(f.pt[:, n, 4:8, :].rearrange("p r n -> p (r n)"), pT[:, 1, :]).then_inc(t_drained[1], 2)

            def row_sums(i, q):
                n = i * c + q
                dve.wait_ge(exp_ready, n + 1)
                t = f.s_sb[:, q % f.depth].rearrange("p n (h k) -> p h n k", h=H)
                dve.tensor_reduce(f.row[:, q % 2, 1, :], t, AX.XY, ALU.add).then_inc(sum_ready, 1)
                dve.wait_ge(sum_ready, n + 1)
                dve.tensor_scalar(f.row[:, q % 2, 2, :], f.row[:, q % 2, 1, :], TINY, None, ALU.max).then_inc(floored, 1)
                dve.wait_ge(floored, n + 1)
                dve.reciprocal(f.row[:, q % 2, 3, :], f.row[:, q % 2, 2, :]).then_inc(inv_ready, 1)

            def o_scale(i, q):
                n = i * c + q
                b = a_banks(f"PV{q}")[0]
                dve.wait_ge(inv_ready, n + 1)
                dve.wait_ge(pv_done, n + 1)
                wait(dve, ot_done, n)
                dve.tensor_tensor(f.o_sb[:].rearrange("p (h e) -> p h e", h=H),
                                  pA[:, b, :].rearrange("p (h e) -> p h e", h=H),
                                  f.row[:, q % 2, 3, :].unsqueeze(2).broadcast_to([P, H, DH]), ALU.mult)\
                    .then_inc(a_drained[b], 1)

            def ot_low(i, q):
                dve.wait_ge(ot_hi_ready, i * c + q + 1)
                dve.tensor_tensor(f.ot_lo[:].rearrange("p c n -> p (c n)"), pT[:, q % 2, :],
                                  f.ot_hi[:].rearrange("p c n -> p (c n)").bitcast(F32), ALU.subtract)\
                    .then_inc(t_drained[q % 2], 2)

            def residual(i, d, q):
                b = a_banks(f"OP{q}")[0]
                dve.wait_ge(op_done, i * c + q + 1)
                wait(dve, y_stored[q % 2], 16 * (i * (c // 2) + q // 2))
                dve.tensor_tensor(f.y_sb[:, q % 2, :], pA[:, b, :], f.x_sb[:, d, q, :], ALU.add).then_inc(a_drained[b], 1)

            if f.depth == 2:
                def first():
                    for q in range(c):
                        moments(0, 0, q)
                    for q in range(c):
                        xt_low(0, q)
                    mask_scores(0, 0, 0)

                def step(i, d, nxt):
                    g, e = i + 1, 1 - d
                    if nxt:
                        for q in range(3):
                            moments(g, e, q)
                    pt_copy(i, 0)
                    mask_scores(i, d, 1)
                    if nxt:
                        moments(g, e, 3)
                        xt_low(g, 0)
                        xt_low(g, 1)
                    row_sums(i, 0)
                    o_scale(i, 0)
                    if nxt:
                        xt_low(g, 2)
                        xt_low(g, 3)
                    mask_scores(i, d, 2)
                    ot_low(i, 0)
                    pt_copy(i, 1)
                    residual(i, d, 0)
                    row_sums(i, 1)
                    o_scale(i, 1)
                    mask_scores(i, d, 3)
                    ot_low(i, 1)
                    pt_copy(i, 2)
                    residual(i, d, 1)
                    row_sums(i, 2)
                    o_scale(i, 2)
                    ot_low(i, 2)
                    pt_copy(i, 3)
                    residual(i, d, 2)
                    row_sums(i, 3)
                    o_scale(i, 3)
                    ot_low(i, 3)
                    if nxt:
                        mask_scores(g, e, 0)
                    residual(i, d, 3)

                first()
                step(0, 0, True)
                step(1, 1, True)
                with dve.Fori(1, f.groups // 2 - 1) as j:
                    step(2 * j, 0, True)
                    step(2 * j + 1, 1, True)
                step(f.groups - 2, 0, True)
                step(f.groups - 1, 1, False)
            else:
                def group(i):
                    for q in range(c):
                        moments(i, 0, q)
                    for q in range(c):
                        xt_low(i, q)
                    for q in range(c):
                        mask_scores(i, 0, q)
                        row_sums(i, q)
                        pt_copy(i, q)
                        o_scale(i, q)
                        ot_low(i, q)
                        residual(i, 0, q)

                group(0)
                with dve.Fori(1, f.groups) as i:
                    group(i)

        def tensor_part(pe, f):
            c = f.c

            def t_free(kind, i, name, b):
                wait(pe, t_drained[b], f.t.before(kind, i, name, b))

            def a_free(kind, i, name):
                b = a_banks(name)[0]
                wait(pe, a_drained[b], f.a.before(kind, i, name, b))
                return b

            def a_copied(kind, i, name):
                b = a_banks(name)[0]
                pe.wait_ge(a_drained[b], f.a.after(kind, i, name, b))

            def three(dst, lhs, rhs, k, last):
                for n, (a, b) in enumerate(((0, 0), (0, 1), (1, 0))):
                    mm = pe.matmul(dst, lhs[a], rhs[b], start=(k == 0 and n == 0), stop=(last and n == 2))
                return mm

            def transpose_x(kind, i, g, q):
                b = q % 2
                pe.wait_ge(xn_ready, g * c + q + 1)
                t_free(kind, i, f"XT{q}", b)
                for k in range(KC):
                    mm = pe.transpose(pT[:, b, k * P:(k + 1) * P], f.xn[:, q, k * P:(k + 1) * P], ident[:])
                mm.then_inc(xt_done, 1)

            def project_k(kind, i, g):
                pe.wait_ge(ctx_lo_ready, g + 1)
                for t in range(f.nt):
                    b = a_free(kind, i, f"K{t}")
                    for m in range(KC):
                        for k in range(KC):
                            s = slice(2 * t, 2 * t + 2)
                            mm = three(pA[:, b, m * P:(m + 1) * P],
                                       (w_hi["k"][:, k, m * P:(m + 1) * P], w_lo["k"][:, k, m * P:(m + 1) * P]),
                                       (f.ctx_hi[:, k, s, :].rearrange("p s k -> p (s k)"),
                                        f.ctx_lo[:, k, s, :].rearrange("p s k -> p (s k)")), k, k == KC - 1)
                    mm.then_inc(k_done, 1)

            def project_v(kind, i, g):
                for t in range(f.nt):
                    b = a_free(kind, i, f"V{t}")
                    s = slice(2 * t, 2 * t + 2)
                    for k in range(KC):
                        mm = three(pA[:, b, :], (f.ctx_hi[:, k, s, :].rearrange("p s k -> p (s k)"),
                                                 f.ctx_lo[:, k, s, :].rearrange("p s k -> p (s k)")),
                                   (w_hi["v"][:, k, :], w_lo["v"][:, k, :]), k, k == KC - 1)
                    mm.then_inc(v_done, 1)

            def project_q(kind, i, m):
                if m == 0:
                    for q in range(c):
                        if q >= c - 2:
                            pe.wait_ge(t_drained[q % 2], f.t.after(kind, i, f"XT{q}", q % 2))
                b = a_free(kind, i, f"Q{m}")
                for k in range(KC):
                    mm = three(pA[:, b, 0:c * P], (w_hi["q"][:, k, m * P:(m + 1) * P], w_lo["q"][:, k, m * P:(m + 1) * P]),
                               (f.xt_hi[:, k, :], f.xt_lo[:, k, :]), k, k == KC - 1)
                mm.then_inc(q_done, 1)

            def scores(kind, i, g, d, q):
                for n in range(f.nbk):
                    u = (g * c + q) * f.nbk + n
                    ring = (q * f.nbk + n) % 2
                    wait(pe, s_drained, u - 1)
                    for m in range(KC):
                        if q == 0 and n == 0:
                            a_copied(kind, i, f"Q{m}")
                        if q == 0 and n == 0 and m == 0:
                            a_copied(kind, i, f"K{f.nt - 1}")
                        mm = pe.matmul(pS[:, ring, m * 256:(m + 1) * 256], f.qt[:, d, m, q * P:(q + 1) * P],
                                       f.kd[:, d, (q // 2) * f.nbk + n, m, :], start=True, stop=True)
                    mm.then_inc(s_done, 1)

            def transpose_p(kind, i, q):
                pe.wait_ge(exp_ready, i * c + q + 1)
                for n in range(f.nbk):
                    for b in range(2):
                        t_free(kind, i, f"PT{q}.{n}", b)
                        for r in range(4):
                            k = 4 * b + r
                            mm = pe.transpose(pT[:, b, r * P:(r + 1) * P], f.s_sb[:, q % f.depth, n, k * P:(k + 1) * P], ident[:])
                    mm.then_inc(pt_done, 1)

            def weigh_v(kind, i, d, q):
                b = a_free(kind, i, f"PV{q}")
                if q == 0 and f.depth == 1:
                    a_copied(kind, i, f"V{f.nt - 1}")
                for h in range(2):
                    pe.wait_ge(t_drained[h], f.t.after(kind, i, f"PT{q}.{f.nbk - 1}", h))
                for r in range(H // 2):
                    for n in range(f.nbk):
                        mm = pe.matmul(pA[:, b, r * 2 * DH:(r + 1) * 2 * DH], f.pt[:, n, r, :],
                                       f.vd[:, d, (q // 2) * f.nbk + n, r, :], start=(n == 0), stop=(n == f.nbk - 1))
                mm.then_inc(pv_done, 1)

            def transpose_o(kind, i, q):
                b = q % 2
                t_free(kind, i, f"OT{q}", b)
                v = a_banks(f"PV{q}")[0]
                pe.wait_ge(a_drained[v], f.a.after(kind, i, f"PV{q}", v))
                for k in range(KC):
                    mm = pe.transpose(pT[:, b, k * P:(k + 1) * P], f.o_sb[:, k * P:(k + 1) * P], ident[:])
                mm.then_inc(ot_done, 1)

            def project_o(kind, i, q):
                b = a_free(kind, i, f"OP{q}")
                pe.wait_ge(t_drained[q % 2], f.t.after(kind, i, f"OT{q}", q % 2))
                for k in range(KC):
                    mm = three(pA[:, b, :], (f.ot_hi[:, k, :], f.ot_lo[:, k, :]), (w_hi["o"][:, k, :], w_lo["o"][:, k, :]),
                               k, k == KC - 1)
                mm.then_inc(op_done, 1)

            if f.depth == 2:
                def first():
                    k = "prologue"
                    project_k(k, 0, 0)
                    transpose_x(k, 0, 0, 0)
                    transpose_x(k, 0, 0, 1)
                    project_v(k, 0, 0)
                    transpose_x(k, 0, 0, 2)
                    transpose_x(k, 0, 0, 3)
                    for m in range(KC):
                        project_q(k, 0, m)
                    scores(k, 0, 0, 0, 0)

                def step(k, i, d):
                    nxt = k == "step"
                    g, e = i + 1, 1 - d
                    scores(k, i, i, d, 1)
                    transpose_p(k, i, 0)
                    if nxt:
                        project_k(k, i, g)
                        transpose_x(k, i, g, 0)
                        transpose_x(k, i, g, 1)
                    weigh_v(k, i, d, 0)
                    if nxt:
                        project_v(k, i, g)
                        transpose_x(k, i, g, 2)
                        transpose_x(k, i, g, 3)
                    scores(k, i, i, d, 2)
                    if nxt:
                        project_q(k, i, 0)
                    transpose_o(k, i, 0)
                    transpose_p(k, i, 1)
                    project_o(k, i, 0)
                    weigh_v(k, i, d, 1)
                    scores(k, i, i, d, 3)
                    if nxt:
                        project_q(k, i, 1)
                    transpose_o(k, i, 1)
                    transpose_p(k, i, 2)
                    project_o(k, i, 1)
                    weigh_v(k, i, d, 2)
                    if nxt:
                        project_q(k, i, 2)
                    transpose_o(k, i, 2)
                    transpose_p(k, i, 3)
                    project_o(k, i, 2)
                    weigh_v(k, i, d, 3)
                    if nxt:
                        project_q(k, i, 3)
                    transpose_o(k, i, 3)
                    if nxt:
                        scores(k, i, g, e, 0)
                    project_o(k, i, 3)

                first()
                step("step", 0, 0)
                step("step", 1, 1)
                with pe.Fori(1, f.groups // 2 - 1) as j:
                    step("step", 2 * j, 0)
                    step("step", 2 * j + 1, 1)
                step("step", f.groups - 2, 0)
                step("last", f.groups - 1, 1)
            else:
                def group(i):
                    k = "step"
                    project_k(k, i, i)
                    project_v(k, i, i)
                    for q in range(c):
                        transpose_x(k, i, i, q)
                    for m in range(KC):
                        project_q(k, i, m)
                    for q in range(c):
                        scores(k, i, i, 0, q)
                        transpose_p(k, i, q)
                        weigh_v(k, i, 0, q)
                        transpose_o(k, i, q)
                        project_o(k, i, q)

                group(0)
                with pe.Fori(1, f.groups) as i:
                    group(i)

        with nc.Block() as block:
            def either(eng, part):
                short = eng.value_load(short_flag[0:1, 0:1], min_val=0, max_val=1)
                with eng.If(short == 1):
                    part(eng, SHORT)
                with eng.Else():
                    part(eng, FULL)

            @block.sync
            def _(sp):
                either(sp, sync_part)

            @block.gpsimd
            def _(pool):
                either(pool, gpsimd_part)

            @block.scalar
            def _(act):
                either(act, scalar_part)

            @block.vector
            def _(dve):
                either(dve, vector_part)

            @block.tensor
            def _(pe):
                either(pe, tensor_part)

        R = 4
        wf_hi = sb("wf_hi", [P, NE, KC * DM], F32R)
        wf_lo = sb("wf_lo", [P, NE, KC * DM], F32R)
        wf_raw = sb("wf_raw", [P, 2, KC * DM])
        bias_all = sb("bias_all", [P, NE, DM])
        g_row = sb("g_row", [P, R], I32)
        s_row = sb("s_row", [P, R], I32)
        xg = sb("xg", [P, R, DM])
        xb = sb("xb", [P, 2, DM])
        stat2 = sb("stat2", [P, R, 6])
        mom2 = sb("mom2", [P, R, 2])
        rstd2 = sb("rstd2", [P, R, 2])
        xn2 = sb("xn2", [P, 2, DM])
        x2_hi = sb("x2_hi", [P, 2, DM], F32R)
        x2_lo = sb("x2_lo", [P, 2, DM], F32R)
        y2 = sb("y2", [P, 2, DM])

        wf_loaded = [sem(f"wf_loaded_{b}") for b in range(2)]
        bias_loaded = sem("bias_loaded")
        wf_hi_ready = sem("wf_hi_ready")
        wf_lo_ready = sem("wf_lo_ready")
        g_row_ready = sem("g_row_ready")
        s_row_ready = sem("s_row_ready")
        gathered = [sem(f"gathered_{r}") for r in range(R)]
        stat2_ready = sem("stat2_ready")
        mom2_ready = sem("mom2_ready")
        var2_ready = sem("var2_ready")
        rstd2_ready = sem("rstd2_ready")
        xn2_ready = sem("xn2_ready")
        x2t_done = sem("x2t_done")
        x2_hi_ready = sem("x2_hi_ready")
        x2_lo_ready = sem("x2_lo_ready")
        xb_ready = sem("xb_ready")
        f_done = sem("f_done")
        y2_ready = sem("y2_ready")
        scattered = [sem(f"scattered_{r}") for r in range(R)]

        def blocks(eng, body, before, after):
            turns = (NR - before - 1) // R
            for j in range(-before, R):
                body(j, j % R)
            with eng.Fori(1, turns) as k:
                for r in range(R):
                    body(R * k + r, r)
            for j in range(R * turns, NR + after):
                body(j, j % R)

        def is_block(j):
            return not isinstance(j, int) or 0 <= j < NR

        with nc.Block() as block:
            @block.sync
            def _(sp):
                sp.dma_start(bias_all[:].rearrange("p t n -> p (t n)"),
                             bf.rearrange("(a t) n -> a (t n)", a=1).broadcast_to([P, NE * DM])).then_inc(bias_loaded, 16)
                for t in range(NE):
                    wait(sp, wf_lo_ready, t - 1)
                    sp.dma_start(wf_raw[:, t % 2, :].rearrange("p (c n) -> p c n", c=KC),
                                 wf[t].rearrange("(c p) n -> p c n", p=P)).then_inc(wf_loaded[t % 2], 16)

            @block.gpsimd
            def _(pool):
                last_row = pool.to_reg(B * S - 1)

                def gather(j, r):
                    wait(pool, xb_ready, j + 1 - R)
                    pool.tensor_copy(g_row[:, r:r + 1], gather_rows[:, bass.ds(j, 1)]).then_inc(g_row_ready, 1)
                    wait_alone(pool, g_row_ready, j + 1, pool_passed)
                    pool.indirect_dma_start(xg[:, r, :], None, x1, bass.IndirectOffsetOnAxis(ap=g_row[:, r:r + 1], axis=0))\
                        .then_inc(gathered[r], 16)

                def rstd(j, r):
                    wait_alone(pool, mom2_ready, j + 1, pool_passed)
                    pool.tensor_scalar(rstd2[:, r, 0:1], mom2[:, r, 1:2], EPS, None, ALU.add).then_inc(var2_ready, 1)
                    pool.wait_ge(var2_ready, j + 1)
                    pool.tensor_tensor(rstd2[:, r, 1:2], rstd2[:, r, 0:1], neg_half[:], ALU.pow).then_inc(rstd2_ready, 1)

                def add_bias(j, r):
                    e = pool.value_load(expert_of[0:1, bass.ds(j, 1)], min_val=0, max_val=NE - 1)
                    pool.wait_ge(xn2_ready, j + 1)
                    wait(pool, y2_ready, j - 1)
                    pool.tensor_tensor(xb[:, r % 2, :], xg[:, r, :],
                                       bias_all[:, bass.ds(e, 1), :].rearrange("p a n -> p (a n)"), ALU.add)\
                        .then_inc(xb_ready, 1)

                def scatter(j, r):
                    pool.wait_ge(y2_ready, j + 1)
                    pool.tensor_copy(s_row[:, r:r + 1], scatter_rows[:, bass.ds(j, 1)]).then_inc(s_row_ready, 1)
                    wait_alone(pool, s_row_ready, j + 1, pool_passed)
                    pool.indirect_dma_start(out, bass.IndirectOffsetOnAxis(ap=s_row[:, r:r + 1], axis=0), y2[:, r % 2, :], None,
                                            bounds_check=last_row, oob_is_err=False).then_inc(scattered[r], 16)

                def body(j, r):
                    if is_block(j - 1):
                        scatter(j - 1, (r - 1) % R)
                    if is_block(j + 1):
                        if not isinstance(j, int) or j + 1 > 0:
                            pass
                        else:
                            pool.wait_ge(bias_loaded, 16)
                        add_bias(j + 1, (r + 1) % R)
                    if is_block(j + 5):
                        gather(j + 5, (r + 5) % R)
                    if is_block(j + 3):
                        rstd(j + 3, (r + 3) % R)

                blocks(pool, body, 5, 1)
                for r in range(R):
                    pool.wait_ge(scattered[r], 16 * len(range(r, NR, R)))

            @block.scalar
            def _(act):
                for t in range(NE):
                    act.wait_ge(wf_loaded[t % 2], 16 * (t // 2 + 1))
                    act.copy(wf_hi[:, t, :], wf_raw[:, t % 2, :]).then_inc(wf_hi_ready, 1)

                def body(j, r):
                    if is_block(j + 1):
                        act.wait_ge(x2t_done, j + 2)
                        wait(act, f_done, j)
                        act.copy(x2_hi[:, (r + 1) % 2, :], pT[:, (r + 1) % 2, :]).then_inc(x2_hi_ready, 1)

                blocks(act, body, 5, 1)

            @block.vector
            def _(dve):
                for t in range(NE):
                    dve.wait_ge(wf_hi_ready, t + 1)
                    dve.tensor_tensor(wf_lo[:, t, :], wf_raw[:, t % 2, :], wf_hi[:, t, :].bitcast(F32), ALU.subtract)\
                        .then_inc(wf_lo_ready, 1)

                def low(j, r):
                    dve.wait_ge(x2_hi_ready, j + 1)
                    dve.tensor_tensor(x2_lo[:, r % 2, :], pT[:, r % 2, :], x2_hi[:, r % 2, :].bitcast(F32), ALU.subtract)\
                        .then_inc(x2_lo_ready, 1)

                def normalise(j, r):
                    dve.wait_ge(rstd2_ready, j + 1)
                    wait(dve, x2t_done, j - 1)
                    dve.tensor_scalar(xn2[:, r % 2, :], xg[:, r, :], mom2[:, r, 0:1], rstd2[:, r, 1:2],
                                      ALU.subtract, ALU.mult).then_inc(xn2_ready, 1)

                def moments(j, r):
                    dve.wait_ge(gathered[r], (j - r) * (16 // R) + 16)
                    dve.bn_stats(stat2[:, r, :], xg[:, r, :]).then_inc(stat2_ready, 1)
                    wait_alone(dve, stat2_ready, j + 1, dve_passed)
                    dve.bn_aggr(mom2[:, r, :], stat2[:, r, :]).then_inc(mom2_ready, 1)

                def finish(j, r):
                    dve.wait_ge(f_done, j + 1)
                    dve.wait_ge(xb_ready, j + 1)
                    if not isinstance(j, int) or j >= 2:
                        dve.wait_ge(scattered[(r - 2) % R], (j - 2 - (r - 2) % R) * (16 // R) + 16)
                    dve.tensor_tensor(y2[:, r % 2, :], pA[:, r % 2, :], xb[:, r % 2, :], ALU.add).then_inc(y2_ready, 1)

                def body(j, r):
                    if is_block(j + 1):
                        low(j + 1, (r + 1) % R)
                    if is_block(j + 2):
                        normalise(j + 2, (r + 2) % R)
                    if is_block(j + 3):
                        moments(j + 3, (r + 3) % R)
                    if is_block(j):
                        finish(j, r)

                blocks(dve, body, 5, 1)

            @block.tensor
            def _(pe):
                def transpose(j, r):
                    pe.wait_ge(xn2_ready, j + 1)
                    wait(pe, x2_lo_ready, j - 1)
                    for k in range(KC):
                        mm = pe.transpose(pT[:, r % 2, k * P:(k + 1) * P], xn2[:, r % 2, k * P:(k + 1) * P], ident[:])
                    mm.then_inc(x2t_done, 1)

                def product(j, r):
                    e = pe.value_load(expert_of[0:1, bass.ds(j, 1)], min_val=0, max_val=NE - 1)
                    pe.wait_ge(wf_lo_ready, e + 1)
                    wait(pe, y2_ready, j - 1)
                    pe.wait_ge(x2_lo_ready, j + 1)
                    hi, lo = x2_hi[:, r % 2, :], x2_lo[:, r % 2, :]
                    for k in range(KC):
                        for n, (a, w) in enumerate(((hi, wf_hi), (hi, wf_lo), (lo, wf_hi))):
                            mm = pe.matmul(pA[:, r % 2, :], a[:, k * P:(k + 1) * P],
                                           w[:, bass.ds(e, 1), k * DM:(k + 1) * DM].rearrange("p a n -> p (a n)"),
                                           start=(k == 0 and n == 0), stop=(k == KC - 1 and n == 2))
                    mm.then_inc(f_done, 1)

                def body(j, r):
                    if is_block(j + 1):
                        transpose(j + 1, (r + 1) % R)
                    if is_block(j):
                        product(j, r)

                blocks(pe, body, 5, 1)


def position_table():
    pos = np.arange(S, dtype=np.float32)[:, None]
    div = np.exp(np.arange(0, DP, 2, dtype=np.float32) * np.float32(-np.log(10000.0) / DP))
    ang = (pos * div).astype(np.float32)
    pe = np.zeros((S, DP), np.float32)
    pe[:, 0::2] = np.sin(ang)
    pe[:, 1::2] = np.cos(ang)
    return np.ascontiguousarray(pe.T)


def route_table():
    p = np.arange(P)
    before = (p[:, None] < p[None, :]).astype(np.float32)
    slot = np.concatenate([PB * np.arange(NR) + i for i in range(PB)])
    place = np.stack([(p // B == i) for i in range(PB)]).astype(np.float32)
    pos = np.concatenate([(h * P + p)[:, None] * place[i][None, :] for h in range(2) for i in range(PB)], axis=1)
    rows = lambda v: np.broadcast_to(np.asarray(v, np.float32)[None, :], (P, len(v)))
    return np.ascontiguousarray(np.concatenate([
        before, np.ones((P, P)), rows(slot), pos, rows(place.reshape(-1)), rows(np.arange(NE) - NE),
        (S * (p % B))[:, None], rows(np.arange(NR))], axis=1), dtype=np.float32)


def kernel(**inputs):
    import concourse.bacc as _bacc
    from concourse.bass_utils import run_bass_kernel_spmd as _run

    a = {k: np.asarray(v) for k, v in inputs.items()}
    c = np.ascontiguousarray
    ctx_t = a["ctx_1024"].reshape(B, NBLKS, BK, KC, P).transpose(0, 1, 4, 3, 2)
    mask = a["mask_BxSxS2_bk0"].reshape(B, 2, P, NBLKS, BK).transpose(3, 2, 0, 1, 4)
    pad = a["mask_BxS2_bf1"].reshape(B, 2, P).transpose(2, 0, 1)
    arrays = {
        "x": a["x"].reshape(B * S, DM),
        "ctx_t": ctx_t,
        "mask": mask,
        "pad": pad,
        "wq": a["L0_xattn_Wq"].T, "wk": a["L0_xattn_Wk"].T, "wv": a["L0_xattn_Wv"].T, "wo": a["L0_xattn_Wo"].T,
        "sigs_t": a["L0_ffn_tile_sigs"].T,
        "wf": a["L0_ffn_W"].transpose(0, 2, 1),
        "bf": a["L0_ffn_b"],
        "ident": np.eye(P, dtype=np.float32),
        "route": route_table(),
        "pe_t": position_table(),
    }
    nc = _bacc.Bacc("TRN2", target_bir_lowering=False, num_devices=1)
    feeds, args = {}, []
    for name, v in arrays.items():
        v = c(v)
        feeds[f"in_{name}"] = v
        args.append(nc.dram_tensor(f"in_{name}", v.shape, mybir.dt.from_np(v.dtype), kind="ExternalInput").ap())
    out = nc.dram_tensor("out_0_dram", (B * S, DM), F32, kind="ExternalOutput").ap()
    kernel_program(nc, *args, out)
    r = _run(nc, [feeds], core_ids=[0])
    return r.results[0]["out_0_dram"].reshape(B, S, DM)
```

```python
from contextlib import ExitStack

import numpy as np

import concourse.bass as bass
from concourse import mybir

F32 = mybir.dt.float32
F32R = mybir.dt.float32r
I32 = mybir.dt.int32
U32 = mybir.dt.uint32
U8 = mybir.dt.uint8
ALU = mybir.AluOpType
ACT = mybir.ActivationFunctionType
AX = mybir.AxisListType

P = 128
B, S, DM = 32, 256, 512
H, DH = 16, 32
KC = DM // P
HG = P // DH
BK = 64
NBLKS = S // BK
SCALE = float(DH) ** -0.5
EPS = 1e-5
BIG = 3e38
FLOOR = -1e38
TINY = 1e-30
NE, DP = 8, 32
PB = P // B
NR = (S + NE * (PB - 1)) // PB
OOB = 1 << 20


def wait_alone(eng, sem, value, passed):
    wait(eng, sem, value)
    if not isinstance(value, int):
        eng.sem_inc(passed, 1)


def wait(eng, sem, value):
    if isinstance(value, int) and value <= 0:
        return
    eng.wait_ge(sem, value)


class Drains:

    def __init__(self, lists, bank_of, signals):
        self.lists, self.bank_of, self.signals = lists, bank_of, signals

    def uses(self, names, bank):
        return self.signals * sum(bank in self.bank_of(n) for n in names)

    def before(self, kind, i, name, bank):
        names = self.lists[kind]
        first = self.uses(names[:names.index(name)], bank)
        if kind == "prologue":
            return first
        first = first + self.uses(self.lists["prologue"], bank)
        if kind == "zero":
            return first
        first = first + self.uses(self.lists["zero"], bank)
        return (i - 1) * self.uses(self.lists["step"], bank) + first

    def after(self, kind, i, name, bank):
        return self.before(kind, i, name, bank) + self.signals


def t_banks(name):
    if name.startswith("PT"):
        return (0, 1)
    if name.startswith(("XT", "OT")):
        return (int(name[2]) % 2,)
    return ()


A_BANK = {"PV0": 0, "OP3": 1, "K": 0, "PV1": 1, "OP0": 0, "KT": 1, "Q0": 0, "PV2": 1, "OP1": 0, "Q1": 1,
          "Q2": 0, "Q3": 1, "PV3": 0, "OP2": 1, "V": 0, "OP3z": 0}


def a_banks(name):
    key = name.rstrip("0123456789") if name[0] in "KV" else name
    return (A_BANK[key],) if key in A_BANK else ()


class Form:

    def __init__(self, nb, nbk, depth):
        self.nb, self.nbk, self.depth = nb, nbk, depth
        self.groups = B // nb
        self.c = 2 * nb
        self.slots = nb * nbk
        self.nt = self.slots // 2
        self.first_block = NBLKS - nbk
        c, nt, nbk = self.c, self.nt, self.nbk
        pt = lambda q: [f"PT{q}.{n}" for n in range(nbk)]
        sc = lambda q: [f"S{q}.{n}" for n in range(nbk)]
        kt, vt = [f"K{t}" for t in range(nt)], [f"V{t}" for t in range(nt)]
        ktt = [f"KT{t}" for t in range(nt)]
        if depth == 2:
            lists = {"prologue": kt + ktt + ["XT0", "XT1", "XT2", "XT3", "Q0", "Q1", "Q2", "Q3"] + sc(0) + vt}
            for kind in ("zero", "step", "last"):
                nxt = kind != "last"
                o3 = ["OP3"] if kind != "zero" else []
                lists[kind] = (
                    pt(0) + sc(1) + (["XT0"] if nxt else []) + ["PV0"] + (["XT1"] if nxt else []) + o3 + ["OT0"] + (kt if nxt else [])
                    + pt(1) + sc(2) + (["XT2"] if nxt else []) + ["PV1"] + (["XT3"] if nxt else []) + ["OP0"]
                    + (ktt if nxt else []) + ["OT1"] + (["Q0"] if nxt else [])
                    + pt(2) + sc(3) + ["PV2", "OP1", "OT2"] + (["Q1", "Q2"] if nxt else [])
                    + pt(3) + (["Q3"] + sc(0) if nxt else []) + ["PV3", "OP2", "OT3"] + (vt if nxt else ["OP3z"]))
        else:
            names = [n for pair in zip(kt, ktt) for n in pair] + vt + ["XT0", "XT1", "Q0", "Q1", "Q2", "Q3"]
            for q in range(c):
                names += sc(q) + pt(q) + [f"PV{q}", f"OT{q}", f"OP{q}"]
            lists = {"prologue": [], "zero": names, "step": names, "last": names}
        self.t = Drains(lists, t_banks, 2)
        self.a = Drains(lists, a_banks, 1)

    def kind(self, i):
        if isinstance(i, int) and i in (0, self.groups - 1):
            return "zero" if i == 0 else "last"
        return "step"

    def output_at(self, i, q):
        if q < 3:
            return i, f"OP{q}"
        return (i, "OP3z") if isinstance(i, int) and i == self.groups - 1 else (i + 1, "OP3")

    def output_read(self, i, q):
        at, name = self.output_at(i, q)
        b = a_banks(name)[0]
        return b, self.a.after(self.kind(at), at, name, b)


def kernel_program(nc, x, ctx_t, mask, pad, wq, wk, wv, wo, sigs_t, wf, bf, ident_d, route_d, pe_t, pick_d, out):
    x1 = nc.dram_tensor("x1_scratch", (B * S, DM + 2), F32, kind="Internal").ap()
    top = ExitStack()
    with top:
        def sb(name, shape, dt=F32, stack=top):
            return stack.enter_context(nc.sbuf_tensor(name, shape, dt))

        def sem(name):
            return top.enter_context(nc.semaphore(name))

        pS = top.enter_context(nc.psum_tensor("pS", [P, 2, 2 * 512], F32))
        pT = top.enter_context(nc.psum_tensor("pT", [P, 2, 512], F32))
        pA = top.enter_context(nc.psum_tensor("pA", [P, 2, 512], F32))

        ident = sb("ident", [P, P])
        neg_half = sb("neg_half", [P, 1])
        gather_rows = sb("gather_rows", [P, NR], I32)
        scatter_rows = sb("scatter_rows", [P, NR], I32)
        expert_of = sb("expert_of", [1, NR], I32)
        short_flag = sb("short_flag", [1, 1], I32)
        bias_rows = sb("bias_rows", [64, NE, DM], F32R)
        ones_rows = sb("ones_rows", [64, P], F32R)

        attn_stack = ExitStack()
        w_hi = {n: sb(f"w{n}_hi", [P, KC, DM], F32R, attn_stack) for n in "qkvo"}
        w_lo = {n: sb(f"w{n}_lo", [P, KC, DM], F32R, attn_stack) for n in "qkvo"}

        prep = ExitStack()
        w_raw = sb("w_raw", [P, 4, KC * DM], F32, prep)
        mask_early = sb("mask_early", [P, NBLKS - 1, B * 2 * BK], U8, prep)
        NROUTE = route_d.shape[1]
        route = sb("route", [P, NROUTE], F32, prep)
        pe_sb = sb("pe_sb", [DP, S], F32, prep)
        sig = sb("sig", [DP, NE], F32, prep)
        sgn = sb("sgn", [DP, 3, NE], F32, prep)
        rt = sb("rt", [P, 2, 8, NE], F32, prep)
        cnt = sb("cnt", [P, 4, NE + 1], F32, prep)
        cnt_i = sb("cnt_i", [P, 2, NE], I32, prep)
        r1 = sb("r1", [P, 2, 4], F32, prep)
        match = sb("match", [P, 2, PB * NR], F32, prep)
        rows_f = sb("rows_f", [P, 2, NR], F32, prep)
        expert_f = sb("expert_f", [1, NE, NR], F32, prep)
        early = sb("early", [P, 1], F32, prep)
        bias_raw = sb("bias_raw", [64, DM], F32, prep)
        bias_hl = sb("bias_hl", [64, DM], F32R, prep)
        pick = sb("pick", [64, NE], F32, prep)

        ends = np.cumsum([P, P, PB * NR, 2 * PB * P, PB * P, NE, 1, NR])
        c_before, c_ones, c_slot, c_pos, c_place, c_expert, c_batch, c_block = (
            route[:, int(b) - n:int(b)] for b, n in zip(ends, (P, P, PB * NR, 2 * PB * P, PB * P, NE, 1, NR)))

        mask_loaded = sem("mask_loaded")
        consts_loaded = sem("consts_loaded")
        w_loaded = [sem(f"w_loaded_{n}") for n in "qkvo"]
        w_hi_ready = sem("w_hi_ready")
        w_lo_ready = sem("w_lo_ready")
        half_set = sem("half_set")
        bias_loaded = sem("bias_loaded")
        bias_hi_ready = sem("bias_hi_ready")
        bias_split = sem("bias_split")
        bias_cleared = sem("bias_cleared")
        picked = sem("picked")
        ones_set = sem("ones_set")
        pool_passed, dve_passed, sync_passed = sem("pool_passed"), sem("dve_passed"), sem("sync_passed")
        early_max = sem("early_max")
        early_sum = sem("early_sum")
        flag_ready = sem("flag_ready")
        rv = sem("route_vector")
        rp = sem("route_product")

        with nc.Block() as block:
            @block.sync
            def _(sp):
                sp.dma_start(mask_early[:], mask[0:NBLKS - 1].rearrange("k p b q j -> p k (b q j)")).then_inc(mask_loaded, 16)
                sp.dma_start(ident[:], ident_d).then_inc(consts_loaded, 16)
                sp.dma_start(route[:], route_d).then_inc(consts_loaded, 16)
                sp.dma_start(pe_sb[:], pe_t).then_inc(consts_loaded, 16)
                sp.dma_start(sig[:], sigs_t).then_inc(consts_loaded, 16)
                sp.wait_ge(bias_cleared, 1)
                sp.dma_start(bias_raw[0:NE, :], bf).then_inc(bias_loaded, 16)
                sp.dma_start(bias_raw[32:32 + NE, :], bf).then_inc(bias_loaded, 16)
                sp.dma_start(pick[:], pick_d).then_inc(bias_loaded, 16)
                for n, w in enumerate((wq, wk, wv, wo)):
                    sp.dma_start(w_raw[:, n, :].rearrange("p (c n) -> p c n", c=KC),
                                 w.rearrange("(c p) n -> p c n", p=P)).then_inc(w_loaded[n], 16)

            @block.gpsimd
            def _(pool):
                pool.memset(neg_half[:], -0.5).then_inc(half_set, 1)
                pool.memset(bias_raw[:], 0.0).then_inc(bias_cleared, 1)
                pool.memset(ones_rows[:].bitcast(F32), 1.0).then_inc(ones_set, 1)
                pool.wait_ge(bias_loaded, 48)
                pool.tensor_copy(bias_hl[:], bias_raw[:]).then_inc(bias_hi_ready, 1)
                pool.wait_ge(bias_hi_ready, 1)
                pool.tensor_tensor(bias_hl[32:64, :], bias_raw[32:64, :], bias_hl[32:64, :].bitcast(F32), ALU.subtract)\
                    .then_inc(bias_split, 1)
                pool.wait_ge(bias_split, 1)
                pool.wait_ge(ones_set, 1)
                pool.wait_ge(half_set, 1)

            @block.scalar
            def _(act):
                for n, k in enumerate("qkvo"):
                    act.wait_ge(w_loaded[n], 16)
                    act.copy(w_hi[k][:].rearrange("p c n -> p (c n)"), w_raw[:, n, :]).then_inc(w_hi_ready, 1)
                act.wait_ge(bias_loaded, 48)
                act.wait_ge(bias_split, 1)
                for t in range(NE):
                    act.activation(bias_rows[:, t, :], bias_hl[:].bitcast(F32), ACT.Copy, scale=pick[:, t:t + 1])\
                        .then_inc(picked, 1)
                act.wait_ge(w_hi_ready, 4)
                act.wait_ge(picked, NE)

            @block.vector
            def _(dve):
                step = [0]

                def done(ins):
                    step[0] += 1
                    ins.then_inc(rv, 1)
                    dve.wait_ge(rv, step[0])

                def low(n):
                    k = "qkvo"[n]
                    dve.wait_ge(w_hi_ready, n + 1)
                    dve.tensor_tensor(w_lo[k][:].rearrange("p c n -> p (c n)"), w_raw[:, n, :],
                                      w_hi[k][:].rearrange("p c n -> p (c n)").bitcast(F32), ALU.subtract)\
                        .then_inc(w_lo_ready, 1)

                dve.wait_ge(consts_loaded, 64)
                done(dve.tensor_scalar(sgn[:, 0, :], sig[:], 0.0, None, ALU.is_gt))
                done(dve.tensor_scalar(sgn[:, 1, :], sig[:], 0.0, None, ALU.is_lt))
                done(dve.tensor_tensor(sgn[:, 2, :], sgn[:, 0, :], sgn[:, 1, :], ALU.subtract))
                dve.wait_ge(mask_loaded, 16)
                dve.tensor_reduce(early[:], mask_early[:].rearrange("p k n -> p (k n)").bitcast(U32), AX.X, ALU.max)\
                    .then_inc(early_max, 1)
                dve.wait_ge(rp, 1)
                for h in range(2):
                    sc = pA[:, h, 0:NE]
                    done(dve.tensor_reduce(r1[:, h, 0:1], sc, AX.X, ALU.max))
                    done(dve.tensor_scalar(rt[:, h, 0, :], sc, r1[:, h, 0:1], None, ALU.is_equal))
                    done(dve.scalar_tensor_tensor(rt[:, h, 1, :], rt[:, h, 0, :], -float(NE), c_expert, ALU.mult, ALU.add))
                    done(dve.tensor_scalar(rt[:, h, 6, :], c_expert, float(NE), None, ALU.add))
                    done(dve.tensor_scalar(rt[:, h, 1, :], rt[:, h, 1, :], float(NE), None, ALU.add))
                    done(dve.tensor_reduce(r1[:, h, 1:2], rt[:, h, 1, :], AX.X, ALU.min))
                    done(dve.tensor_scalar(rt[:, h, 2, :], c_expert, r1[:, h, 1:2], None, ALU.is_equal))
                low(0)
                dve.wait_ge(rp, 2)
                done(dve.tensor_scalar(cnt_i[:, 0, :], pA[:, 0, 256:256 + NE], float(PB - 1), None, ALU.add))
                done(dve.tensor_scalar(cnt_i[:, 1, :], cnt_i[:, 0, :], 2, None, ALU.arith_shift_right))
                done(dve.tensor_copy(cnt[:, 0, 0:NE], cnt_i[:, 1, :]))
                done(dve.memset(cnt[:, 1, 0:1], 0.0))
                for t in range(NE):
                    done(dve.tensor_tensor(cnt[:, 1, t + 1:t + 2], cnt[:, 1, t:t + 1], cnt[:, 0, t:t + 1], ALU.add))
                for h in range(2):
                    done(dve.scalar_tensor_tensor(rt[:, h, 3, :], cnt[:, 1, 0:NE], float(PB),
                                                  pA[:, 1, 64 + 64 * h:64 + 64 * h + NE], ALU.mult, ALU.add))
                    done(dve.tensor_tensor(rt[:, h, 4, :], rt[:, h, 3, :], rt[:, h, 2, :], ALU.mult))
                    done(dve.tensor_reduce(r1[:, h, 2:3], rt[:, h, 4, :], AX.X, ALU.add))
                    done(dve.tensor_scalar(match[:, h, :], c_slot, r1[:, h, 2:3], None, ALU.is_equal))
                low(1)
                low(2)
                dve.wait_ge(rp, 3)
                done(dve.tensor_scalar(rows_f[:, 0, :], pT[:, 0, 0:NR], c_batch, None, ALU.add))
                done(dve.tensor_scalar(rows_f[:, 1, :], pT[:, 1, 0:NR], -float(OOB), float(OOB), ALU.mult, ALU.add))
                done(dve.tensor_copy(gather_rows[:], rows_f[:, 0, :]))
                done(dve.tensor_tensor(scatter_rows[:], rows_f[:, 0, :], rows_f[:, 1, :], ALU.add))
                done(dve.tensor_scalar(expert_f[0:1, 0, :], c_block[0:1, :], 0.0, None, ALU.mult))
                for t in range(1, NE):
                    done(dve.scalar_tensor_tensor(expert_f[0:1, t, :], c_block[0:1, :], cnt[0:1, 1, t:t + 1],
                                                  expert_f[0:1, t - 1, :], ALU.is_ge, ALU.add))
                done(dve.tensor_copy(expert_of[:], expert_f[0:1, NE - 1, :]))
                dve.wait_ge(early_sum, 1)
                dve.tensor_scalar(short_flag[:], pS[0:1, 0, 0:1], 0.0, None, ALU.is_equal).then_inc(flag_ready, 1)
                low(3)
                dve.wait_ge(w_lo_ready, 4)
                dve.wait_ge(flag_ready, 1)

            @block.tensor
            def _(pe):
                pe.wait_ge(rv, 3)
                pe.wait_ge(consts_loaded, 64)
                for h in range(2):
                    mm = pe.matmul(pA[:, h, 0:NE], pe_sb[:, h * P:(h + 1) * P], sgn[:, 2, :], start=True, stop=True)
                mm.then_inc(rp, 1)
                pe.wait_ge(early_max, 1)
                pe.matmul(pS[0:1, 0, 0:1], early[:], c_ones[:, 0:1], start=True, stop=True).then_inc(early_sum, 1)
                pe.wait_ge(rv, 17)
                oh = [rt[:, h, 2, :] for h in range(2)]
                pe.matmul(pA[:, 0, 256:256 + NE], c_ones, oh[0], start=True, stop=False)
                pe.matmul(pA[:, 0, 256:256 + NE], c_ones, oh[1], start=False, stop=True)
                pe.matmul(pA[:, 1, 64:64 + NE], c_before, oh[0], start=True, stop=True)
                pe.matmul(pA[:, 1, 128:128 + NE], c_ones, oh[0], start=True, stop=False)
                pe.matmul(pA[:, 1, 128:128 + NE], c_before, oh[1], start=False, stop=True).then_inc(rp, 1)
                pe.wait_ge(rv, 17 + 4 + NE + 8)
                for k in range(2 * PB):
                    h, i = divmod(k, PB)
                    m = match[:, h, i * NR:(i + 1) * NR]
                    pe.matmul(pT[:, 0, 0:NR], c_pos[:, (h * PB + i) * P:(h * PB + i + 1) * P], m,
                              start=(k == 0), stop=(k == 2 * PB - 1))
                for k in range(2 * PB):
                    h, i = divmod(k, PB)
                    mm = pe.matmul(pT[:, 1, 0:NR], c_place[:, i * P:(i + 1) * P], match[:, h, i * NR:(i + 1) * NR],
                                   start=(k == 0), stop=(k == 2 * PB - 1))
                mm.then_inc(rp, 1)
        prep.close()

        SHORT, FULL = Form(2, 1, 2), Form(1, NBLKS, 1)
        for f, tag in ((SHORT, "s"), (FULL, "f")):
            st = ExitStack()
            d = f.depth
            f.x_sb = sb(f"x_{tag}", [P, d, f.c, DM], F32, st)
            f.ctx_raw = sb(f"ctx_raw_{tag}", [P, f.slots, KC, BK], F32, st)
            f.ctx_hi = sb(f"ctx_hi_{tag}", [P, KC, f.slots, BK], F32R, st)
            f.ctx_lo = sb(f"ctx_lo_{tag}", [P, KC, f.slots, BK], F32R, st)
            f.mask_u8 = sb(f"mask_u8_{tag}", [P, f.c, f.nbk, BK], U8, st)
            f.pad_u8 = sb(f"pad_u8_{tag}", [P, f.c], U8, st)
            f.pad_big = sb(f"pad_big_{tag}", [P, f.c], F32, st)
            f.bias = sb(f"bias_{tag}", [P, d, f.c, f.nbk, BK], F32, st)
            f.stat = sb(f"stat_{tag}", [P, f.c, 6], F32, st)
            f.mom = sb(f"mom_{tag}", [P, f.c, 2], F32, st)
            f.rstd = sb(f"rstd_{tag}", [P, f.c, 3], F32, st)
            f.xn = sb(f"xn_{tag}", [P, f.c, DM], F32, st)
            f.xt_hi = sb(f"xt_hi_{tag}", [P, KC, f.c * P], F32R, st)
            f.xt_lo = sb(f"xt_lo_{tag}", [P, KC, f.c * P], F32R, st)
            f.qt = sb(f"qt_{tag}", [P, d, KC, f.c * P], F32, st)
            f.k_sb = sb(f"k_{tag}", [P, DM], F32, st)
            f.kd = sb(f"kd_{tag}", [P, d, f.slots, KC, HG * BK], F32, st)
            f.vd = sb(f"vd_{tag}", [P, d, f.slots, H // 2, 2 * DH], F32, st)
            f.s_sb = sb(f"s_{tag}", [P, d, f.nbk, H * BK], F32, st)
            f.row = sb(f"row_{tag}", [P, 2, 4, H], F32, st)
            f.pt = sb(f"pt_{tag}", [P, f.nbk, H // 2, P], F32, st)
            f.o_sb = sb(f"o_{tag}", [P, DM], F32, st)
            f.ot_hi = sb(f"ot_hi_{tag}", [P, KC, P], F32R, st)
            f.ot_lo = sb(f"ot_lo_{tag}", [P, KC, P], F32R, st)
            f.y_sb = sb(f"y_{tag}", [P, 2, DM + 2], F32, st)
            f.y_stat = sb(f"y_stat_{tag}", [P, 2, 6], F32, st)
            f.y_mom = sb(f"y_mom_{tag}", [P, 2, 2], F32, st)
            st.close()
        attn_stack.close()
        wf_lo = sb("wf_lo", [P, NE, KC * DM], F32R)
        WO_PLACES = (3, 7)
        wf_loaded = [sem(f"wf_loaded_{t}") for t in range(NE)]

        def load_expert(sp, t):
            sp.dma_start(wf_lo[:, t, :].bitcast(F32).rearrange("p (c n) -> p c n", c=KC),
                         wf[t].rearrange("(c p) n -> p c n", p=P)).then_inc(wf_loaded[t], 16)

        zeroed = sem("zeroed")
        x_loaded = [[sem(f"x_loaded_{d}{q}") for q in range(SHORT.c)] for d in range(2)]
        ctx_loaded = sem("ctx_loaded")
        mask_in = sem("mask_in")
        ctx_hi_ready = sem("ctx_hi_ready")
        ctx_lo_ready = sem("ctx_lo_ready")
        stat_ready = sem("stat_ready")
        mom_ready = sem("mom_ready")
        var_ready = sem("var_ready")
        rstd_ready = sem("rstd_ready")
        shift_ready = sem("shift_ready")
        xn_ready = sem("xn_ready")
        pad_ready = sem("pad_ready")
        bias_ready = sem("bias_ready")
        xt_done = sem("xt_done")
        k_done = sem("k_done")
        kt_done = sem("kt_done")
        v_done = sem("v_done")
        q_done = sem("q_done")
        s_done = sem("s_done")
        s_drained = sem("s_drained")
        max_ready = sem("max_ready")
        shifted = sem("shifted")
        exp_ready = sem("exp_ready")
        sum_ready = sem("sum_ready")
        floored = sem("floored")
        inv_ready = sem("inv_ready")
        pt_done = sem("pt_done")
        pv_done = sem("pv_done")
        ot_done = sem("ot_done")
        ot_hi_ready = sem("ot_hi_ready")
        op_done = sem("op_done")
        y_stat_ready = sem("y_stat_ready")
        y_mom_ready = sem("y_mom_ready")
        y_var_ready = sem("y_var_ready")
        y_ready = sem("y_ready")
        xt_hi_ready = sem("xt_hi_ready")
        t_drained = [sem(f"t_drained_{b}") for b in range(2)]
        a_drained = [sem(f"a_drained_{b}") for b in range(2)]
        y_stored = [sem(f"y_stored_{b}") for b in range(2)]

        def sync_part(sp, f):
            c = f.c

            def load_x(g, d, q):
                row = sp.snap(g * (c * P) + q * P) if not isinstance(g, int) else g * c * P + q * P
                if not (isinstance(g, int) and g < f.depth):
                    b, count = f.output_read(g - f.depth, q)
                    wait(sp, a_drained[b], count)
                sp.dma_start(f.x_sb[:, d, q, :], x[bass.ds(row, P), :]).then_inc(x_loaded[d][q], 16)

            def first_batch(g):
                return g * f.nb if isinstance(g, int) else sp.snap(g * f.nb)

            def load_ctx(g):
                b0 = first_batch(g)
                wait(sp, ctx_lo_ready, g)
                for b in range(f.nb):
                    for n in range(f.nbk):
                        sp.dma_start(f.ctx_raw[:, b * f.nbk + n, :, :],
                                     ctx_t[bass.ds(b0 + b, 1), f.first_block + n].rearrange("a p c k -> (a p) c k"))\
                            .then_inc(ctx_loaded, 16)

            def load_mask(g):
                b0 = first_batch(g)
                wait_alone(sp, bias_ready, g * c, sync_passed)
                for n in range(f.nbk):
                    sp.dma_start(f.mask_u8[:, :, n, :],
                                 mask[f.first_block + n, :, bass.ds(b0, f.nb)].rearrange("p b q k -> p (b q) k"))\
                        .then_inc(mask_in, 16)
                sp.dma_start(f.pad_u8[:], pad[:, bass.ds(b0, f.nb)].rearrange("p b q -> p (b q)")).then_inc(mask_in, 16)

            def store_y(i, q):
                row = sp.snap(i * (c * P) + q * P) if not isinstance(i, int) else i * c * P + q * P
                sp.wait_ge(y_ready, i * c + q + 1)
                sp.dma_start(x1[bass.ds(row, P), :], f.y_sb[:, q % 2, :]).then_inc(y_stored[q % 2], 16)

            def load_experts():
                sp.wait_ge(k_done, f.groups * f.nt)
                sp.wait_ge(q_done, f.groups * KC)
                sp.wait_ge(v_done, f.groups * f.nt)
                for t in range(NE):
                    if t not in WO_PLACES:
                        load_expert(sp, t)

            def step(i, d, ahead=True, last=False):
                if last:
                    load_experts()
                if not (isinstance(i, int) and i == 0):
                    if not last:
                        load_x(i + 1, 1 - d, 3)
                    store_y(i - 1, 3)
                if ahead:
                    load_ctx(i + 2)
                for q in range(3):
                    if ahead:
                        load_x(i + 2, d, q)
                    store_y(i, q)
                    if ahead and q == 0:
                        load_mask(i + 2)
                if last:
                    store_y(i, 3)

            if f.depth == 2:
                load_ctx(0)
                for q in range(c):
                    load_x(0, 0, q)
                load_mask(0)
                for q in range(c):
                    load_x(1, 1, q)
                load_ctx(1)
                load_mask(1)
                step(0, 0)
                step(1, 1)
                with sp.Fori(1, f.groups // 2 - 1) as j:
                    step(2 * j, 0)
                    step(2 * j + 1, 1)
                step(f.groups - 2, 0, ahead=False)
                step(f.groups - 1, 1, ahead=False, last=True)
            else:
                def group(i):
                    load_ctx(i)
                    load_mask(i)
                    for q in range(c):
                        load_x(i, 0, q)
                    for q in range(c):
                        store_y(i, q)

                group(0)
                with sp.Fori(1, f.groups) as i:
                    group(i)
                load_experts()
            for b in range(2):
                sp.wait_ge(y_stored[b], 16 * f.groups * c // 2)

        def gpsimd_part(pool, f):
            c = f.c
            for d in range(f.depth):
                pool.memset(f.kd[:, d], 0.0).then_inc(zeroed, 1)
                pool.memset(f.vd[:, d], 0.0).then_inc(zeroed, 1)

            def ctx_low(g):
                wait(pool, ctx_hi_ready, g + 1)
                pool.tensor_tensor(f.ctx_lo[:].rearrange("p c s k -> p s c k"), f.ctx_raw[:],
                                   f.ctx_hi[:].bitcast(F32).rearrange("p c s k -> p s c k"), ALU.subtract)\
                    .then_inc(ctx_lo_ready, 1)

            def rstd(g, q):
                n = g * c + q
                wait_alone(pool, mom_ready, n + 1, pool_passed)
                pool.tensor_scalar(f.rstd[:, q, 0:1], f.mom[:, q, 1:2], EPS, None, ALU.add).then_inc(var_ready, 1)
                pool.wait_ge(var_ready, n + 1)
                pool.tensor_tensor(f.rstd[:, q, 1:2], f.rstd[:, q, 0:1], neg_half[:], ALU.pow).then_inc(rstd_ready, 1)
                wait_alone(pool, rstd_ready, n + 1, pool_passed)
                pool.tensor_scalar(f.rstd[:, q, 2:3], f.mom[:, q, 0:1], f.rstd[:, q, 1:2], -1.0,
                                   ALU.mult, ALU.mult).then_inc(shift_ready, 1)

            def y_rstd(i, q):
                n = i * c + q
                y = f.y_sb[:, q % 2, :]
                wait_alone(pool, y_mom_ready, n + 1, pool_passed)
                pool.tensor_copy(y[:, DM:DM + 1], f.y_mom[:, q % 2, 0:1])
                pool.tensor_scalar(f.y_mom[:, q % 2, 1:2], f.y_mom[:, q % 2, 1:2], EPS, None, ALU.add).then_inc(y_var_ready, 1)
                pool.wait_ge(y_var_ready, n + 1)
                pool.tensor_tensor(y[:, DM + 1:DM + 2], f.y_mom[:, q % 2, 1:2], neg_half[:], ALU.pow).then_inc(y_ready, 1)

            def mask_bias(g, d):
                wait_alone(pool, mask_in, 16 * (f.nbk + 1) * (g + 1), pool_passed)
                pool.tensor_scalar(f.pad_big[:], f.pad_u8[:], BIG, None, ALU.mult).then_inc(pad_ready, 1)
                wait(pool, s_drained, (g + 1 - f.depth) * (c * f.nbk))
                wait_alone(pool, pad_ready, g + 1, pool_passed)
                for q in range(c):
                    pool.tensor_scalar(f.bias[:, d, q].rearrange("p n k -> p (n k)"),
                                       f.mask_u8[:, q].rearrange("p n k -> p (n k)"),
                                       f.pad_big[:, q:q + 1], -BIG, ALU.mult, ALU.add).then_inc(bias_ready, 1)

            if f.depth == 2:
                def step(i, d, nxt=True, ahead=True):
                    g = i + 1
                    if nxt:
                        ctx_low(g)
                        rstd(g, 2)
                    if not (isinstance(i, int) and i == 0):
                        y_rstd(i - 1, 3)
                    if nxt:
                        rstd(g, 3)
                        mask_bias(g, 1 - d)
                    y_rstd(i, 0)
                    y_rstd(i, 1)
                    if ahead:
                        rstd(g + 1, 0)
                    y_rstd(i, 2)
                    if ahead:
                        rstd(g + 1, 1)

                ctx_low(0)
                for q in range(c):
                    rstd(0, q)
                mask_bias(0, 0)
                rstd(1, 0)
                rstd(1, 1)
                step(0, 0)
                step(1, 1)
                with pool.Fori(1, f.groups // 2 - 1) as j:
                    step(2 * j, 0)
                    step(2 * j + 1, 1)
                step(f.groups - 2, 0, ahead=False)
                step(f.groups - 1, 1, nxt=False, ahead=False)
                y_rstd(f.groups - 1, 3)
            else:
                def group(i):
                    ctx_low(i)
                    for q in range(c):
                        rstd(i, q)
                    mask_bias(i, 0)
                    for q in range(c):
                        y_rstd(i, q)

                group(0)
                with pool.Fori(1, f.groups) as i:
                    group(i)

        def scalar_part(act, f):
            c = f.c

            def ctx_high(g):
                act.wait_ge(ctx_loaded, 16 * f.slots * (g + 1))
                wait(act, v_done, f.nt * g)
                act.copy(f.ctx_hi[:].rearrange("p c s k -> p s c k"), f.ctx_raw[:]).then_inc(ctx_hi_ready, 1)

            def xt_high(g, q):
                act.wait_ge(xt_done, g * c + q + 1)
                act.copy(f.xt_hi[:, :, q * P:(q + 1) * P], pT[:, q % 2, :].rearrange("p (c n) -> p c n", c=KC))\
                    .then_inc(xt_hi_ready, 1)

            def k_copy(g, t):
                act.wait_ge(k_done, g * f.nt + t + 1)
                act.copy(f.k_sb[:], pA[:, a_banks("K0")[0], :]).then_inc(a_drained[a_banks("K0")[0]], 1)

            def kt_copy(g, d, t):
                if isinstance(g, int) and g == 0:
                    act.wait_ge(zeroed, 2 * f.depth)
                b = a_banks("KT0")[0]
                act.wait_ge(kt_done, g * f.nt + t + 1)
                for h in range(HG):
                    r = slice(h * DH, (h + 1) * DH)
                    src = pA[r, b, :].rearrange("p (c s k) -> p c s k", c=KC, s=2)
                    for s in range(2):
                        ins = act.copy(f.kd[r, d, 2 * t + s, :, h * BK:(h + 1) * BK], src[:, :, s, :])
                ins.then_inc(a_drained[b], 1)

            def v_copy(g, d):
                for t in range(f.nt):
                    act.wait_ge(v_done, g * f.nt + t + 1)
                    src = pA[:, a_banks("V0")[0], :].rearrange("p (r e c) -> p r e c", r=H // 2, e=2)
                    for s in range(2):
                        for e in range(2):
                            ins = act.copy(f.vd[e * BK:(e + 1) * BK, d, 2 * t + s, :, e * DH:(e + 1) * DH],
                                           src[s * BK:(s + 1) * BK, :, e, :])
                    ins.then_inc(a_drained[a_banks("V0")[0]], 1)

            def q_copy(g, d, m):
                act.wait_ge(q_done, g * KC + m + 1)
                b = a_banks(f"Q{m}")[0]
                act.copy(f.qt[:, d, m, :], pA[:, b, 0:c * P]).then_inc(a_drained[b], 1)

            def exps(i, q):
                act.wait_ge(shifted, (i * c + q + 1) * f.nbk)
                t = f.s_sb[:, q % f.depth]
                act.activation(t, t, ACT.Exp, scale=-SCALE).then_inc(exp_ready, 1)

            def pt_copy(i, q):
                for n in range(f.nbk):
                    act.wait_ge(pt_done, (i * c + q) * f.nbk + n + 1)
                    for b in range(2):
                        act.copy(f.pt[:, n, 4 * b:4 * b + 4, :].rearrange("p r n -> p (r n)"), pT[:, b, :])\
                            .then_inc(t_drained[b], 2)

            def normalise(g, d, q):
                n = g * c + q
                wait(act, shift_ready, n + 1)
                wait(act, xt_done, n + 1 - c)
                act.activation(f.xn[:, q, :], f.x_sb[:, d, q, :], ACT.Identity, bias=f.rstd[:, q, 2:3],
                               scale=f.rstd[:, q, 1:2]).then_inc(xn_ready, 1)

            def ot_high(i, q):
                act.wait_ge(ot_done, i * c + q + 1)
                wait(act, op_done, i * c + q)
                act.copy(f.ot_hi[:].rearrange("p c n -> p (c n)"), pT[:, q % 2, :]).then_inc(ot_hi_ready, 1)

            if f.depth == 2:
                def first():
                    ctx_high(0)
                    for q in range(c):
                        normalise(0, 0, q)
                    k_copy(0, 0)
                    kt_copy(0, 0, 0)
                    for q in range(c):
                        xt_high(0, q)
                    normalise(1, 1, 0)
                    for m in range(KC):
                        q_copy(0, 0, m)
                    exps(0, 0)
                    v_copy(0, 0)

                def step(i, d, nxt=True, ahead=True):
                    g, e = i + 1, 1 - d
                    pt_copy(i, 0)
                    if nxt:
                        normalise(g, e, 1)
                        ctx_high(g)
                        xt_high(g, 0)
                        xt_high(g, 1)
                    exps(i, 1)
                    ot_high(i, 0)
                    if nxt:
                        normalise(g, e, 2)
                        k_copy(g, 0)
                    pt_copy(i, 1)
                    if nxt:
                        normalise(g, e, 3)
                        xt_high(g, 2)
                        xt_high(g, 3)
                    exps(i, 2)
                    ot_high(i, 1)
                    if nxt:
                        kt_copy(g, e, 0)
                        q_copy(g, e, 0)
                    pt_copy(i, 2)
                    exps(i, 3)
                    ot_high(i, 2)
                    if nxt:
                        q_copy(g, e, 1)
                    if ahead:
                        normalise(g + 1, d, 0)
                    if nxt:
                        q_copy(g, e, 2)
                    pt_copy(i, 3)
                    if nxt:
                        q_copy(g, e, 3)
                        exps(g, 0)
                    ot_high(i, 3)
                    if nxt:
                        v_copy(g, e)

                first()
                step(0, 0)
                step(1, 1)
                with act.Fori(1, f.groups // 2 - 1) as j:
                    step(2 * j, 0)
                    step(2 * j + 1, 1)
                step(f.groups - 2, 0, ahead=False)
                step(f.groups - 1, 1, nxt=False, ahead=False)
            else:
                def group(i):
                    ctx_high(i)
                    for q in range(c):
                        normalise(i, 0, q)
                    for t in range(f.nt):
                        k_copy(i, t)
                        kt_copy(i, 0, t)
                    v_copy(i, 0)
                    for q in range(c):
                        xt_high(i, q)
                    for m in range(KC):
                        q_copy(i, 0, m)
                    for q in range(c):
                        exps(i, q)
                        pt_copy(i, q)
                        ot_high(i, q)

                group(0)
                with act.Fori(1, f.groups) as i:
                    group(i)

        def vector_part(dve, f):
            c = f.c

            def moments(g, d, q):
                n = g * c + q
                dve.wait_ge(x_loaded[d][q], (16 // f.depth) * (g - d) + 16)
                dve.bn_stats(f.stat[:, q, :], f.x_sb[:, d, q, :]).then_inc(stat_ready, 1)
                wait(dve, xn_ready, n + 1 - c)
                wait_alone(dve, stat_ready, n + 1, dve_passed)
                dve.bn_aggr(f.mom[:, q, :], f.stat[:, q, :]).then_inc(mom_ready, 1)

            def xt_low(g, q):
                dve.wait_ge(xt_hi_ready, g * c + q + 1)
                t = slice(q * P, (q + 1) * P)
                dve.tensor_tensor(f.xt_lo[:, :, t], pT[:, q % 2, :].rearrange("p (c n) -> p c n", c=KC),
                                  f.xt_hi[:, :, t].bitcast(F32), ALU.subtract).then_inc(t_drained[q % 2], 2)

            def mask_scores(i, d, q):
                n = i * c + q
                dve.wait_ge(bias_ready, n + 1)
                wait(dve, pt_done, (n + 1 - f.depth) * f.nbk)
                for k in range(f.nbk):
                    u = n * f.nbk + k
                    dve.wait_ge(s_done, u + 1)
                    ring = (q * f.nbk + k) % 2
                    dve.tensor_tensor(f.s_sb[:, q % f.depth, k, :].rearrange("p (h k) -> p h k", h=H),
                                      pS[:, ring, :].rearrange("p (h k) -> p h k", h=H),
                                      f.bias[:, d, q, k:k + 1, :].broadcast_to([P, H, BK]), ALU.add).then_inc(s_drained, 1)
                dve.wait_ge(s_drained, (n + 1) * f.nbk)
                t = f.s_sb[:, q % f.depth].rearrange("p n (h k) -> p h n k", h=H)
                dve.tensor_reduce(f.row[:, q % 2, 0, :], t, AX.XY, ALU.max).then_inc(max_ready, 1)

            def shift_scores(i, q):
                dve.wait_ge(max_ready, i * c + q + 1)
                for k in range(f.nbk):
                    t = f.s_sb[:, q % f.depth, k, :].rearrange("p (h k) -> p h k", h=H)
                    dve.scalar_tensor_tensor(t, f.row[:, q % 2, 0, :].unsqueeze(2).broadcast_to([P, H, BK]), FLOOR, t,
                                             ALU.max, ALU.subtract).then_inc(shifted, 1)

            def row_sums(i, q):
                n = i * c + q
                dve.wait_ge(exp_ready, n + 1)
                t = f.s_sb[:, q % f.depth].rearrange("p n (h k) -> p h n k", h=H)
                dve.tensor_reduce(f.row[:, q % 2, 1, :], t, AX.XY, ALU.add).then_inc(sum_ready, 1)
                dve.wait_ge(sum_ready, n + 1)
                dve.tensor_scalar(f.row[:, q % 2, 2, :], f.row[:, q % 2, 1, :], TINY, None, ALU.max).then_inc(floored, 1)
                dve.wait_ge(floored, n + 1)
                dve.reciprocal(f.row[:, q % 2, 3, :], f.row[:, q % 2, 2, :]).then_inc(inv_ready, 1)

            def o_scale(i, q):
                n = i * c + q
                b = a_banks(f"PV{q}")[0]
                dve.wait_ge(inv_ready, n + 1)
                dve.wait_ge(pv_done, n + 1)
                wait(dve, ot_done, n)
                dve.tensor_tensor(f.o_sb[:].rearrange("p (h e) -> p h e", h=H),
                                  pA[:, b, :].rearrange("p (h e) -> p h e", h=H),
                                  f.row[:, q % 2, 3, :].unsqueeze(2).broadcast_to([P, H, DH]), ALU.mult)\
                    .then_inc(a_drained[b], 1)

            def ot_low(i, q):
                dve.wait_ge(ot_hi_ready, i * c + q + 1)
                dve.tensor_tensor(f.ot_lo[:].rearrange("p c n -> p (c n)"), pT[:, q % 2, :],
                                  f.ot_hi[:].rearrange("p c n -> p (c n)").bitcast(F32), ALU.subtract)\
                    .then_inc(t_drained[q % 2], 2)

            def residual(i, d, q):
                b, _ = f.output_read(i, q)
                dve.wait_ge(op_done, i * c + q + 1)
                wait(dve, y_stored[q % 2], 16 * (i * (c // 2) + q // 2))
                dve.tensor_tensor(f.y_sb[:, q % 2, 0:DM], pA[:, b, :], f.x_sb[:, d, q, :], ALU.add).then_inc(a_drained[b], 1)

            def y_moments(i, q):
                n = i * c + q
                b, count = f.output_read(i, q)
                dve.wait_ge(a_drained[b], count)
                dve.bn_stats(f.y_stat[:, q % 2, :], f.y_sb[:, q % 2, 0:DM]).then_inc(y_stat_ready, 1)
                wait(dve, y_ready, n - 1)
                wait_alone(dve, y_stat_ready, n + 1, dve_passed)
                dve.bn_aggr(f.y_mom[:, q % 2, :], f.y_stat[:, q % 2, :]).then_inc(y_mom_ready, 1)

            if f.depth == 2:
                def step(i, d, nxt=True, ahead=True):
                    g, e = i + 1, 1 - d
                    row_sums(i, 0)
                    mask_scores(i, d, 1)
                    o_scale(i, 0)
                    shift_scores(i, 1)
                    if nxt:
                        xt_low(g, 0)
                        xt_low(g, 1)
                        moments(g, e, 2)
                    if not (isinstance(i, int) and i == 0):
                        residual(i - 1, e, 3)
                    ot_low(i, 0)
                    if not (isinstance(i, int) and i == 0):
                        y_moments(i - 1, 3)
                    row_sums(i, 1)
                    if nxt:
                        moments(g, e, 3)
                    mask_scores(i, d, 2)
                    o_scale(i, 1)
                    shift_scores(i, 2)
                    if nxt:
                        xt_low(g, 2)
                        xt_low(g, 3)
                    residual(i, d, 0)
                    ot_low(i, 1)
                    y_moments(i, 0)
                    row_sums(i, 2)
                    mask_scores(i, d, 3)
                    o_scale(i, 2)
                    shift_scores(i, 3)
                    residual(i, d, 1)
                    ot_low(i, 2)
                    y_moments(i, 1)
                    if ahead:
                        moments(g + 1, d, 0)
                    row_sums(i, 3)
                    if nxt:
                        mask_scores(g, e, 0)
                    o_scale(i, 3)
                    if nxt:
                        shift_scores(g, 0)
                    residual(i, d, 2)
                    ot_low(i, 3)
                    y_moments(i, 2)
                    if ahead:
                        moments(g + 1, d, 1)

                for q in range(c):
                    moments(0, 0, q)
                moments(1, 1, 0)
                moments(1, 1, 1)
                for q in range(c):
                    xt_low(0, q)
                mask_scores(0, 0, 0)
                shift_scores(0, 0)
                step(0, 0)
                step(1, 1)
                with dve.Fori(1, f.groups // 2 - 1) as j:
                    step(2 * j, 0)
                    step(2 * j + 1, 1)
                step(f.groups - 2, 0, ahead=False)
                step(f.groups - 1, 1, nxt=False, ahead=False)
                residual(f.groups - 1, 1, 3)
                y_moments(f.groups - 1, 3)
            else:
                def group(i):
                    for q in range(c):
                        moments(i, 0, q)
                    for q in range(c):
                        xt_low(i, q)
                    for q in range(c):
                        mask_scores(i, 0, q)
                        shift_scores(i, q)
                        row_sums(i, q)
                        o_scale(i, q)
                        ot_low(i, q)
                        residual(i, 0, q)
                        y_moments(i, q)

                group(0)
                with dve.Fori(1, f.groups) as i:
                    group(i)

        def tensor_part(pe, f):
            c = f.c

            def t_free(kind, i, name, b):
                wait(pe, t_drained[b], f.t.before(kind, i, name, b))

            def a_free(kind, i, name):
                b = a_banks(name)[0]
                wait(pe, a_drained[b], f.a.before(kind, i, name, b))
                return b

            def a_copied(kind, i, name):
                b = a_banks(name)[0]
                pe.wait_ge(a_drained[b], f.a.after(kind, i, name, b))

            def three(dst, lhs, rhs, k, last):
                for n, (a, b) in enumerate(((0, 0), (0, 1), (1, 0))):
                    mm = pe.matmul(dst, lhs[a], rhs[b], start=(k == 0 and n == 0), stop=(last and n == 2))
                return mm

            def transpose_x(kind, i, g, q):
                b = q % 2
                pe.wait_ge(xn_ready, g * c + q + 1)
                t_free(kind, i, f"XT{q}", b)
                for k in range(KC):
                    mm = pe.transpose(pT[:, b, k * P:(k + 1) * P], f.xn[:, q, k * P:(k + 1) * P], ident[:])
                mm.then_inc(xt_done, 1)

            def project_k(kind, i, g, t):
                pe.wait_ge(ctx_lo_ready, g + 1)
                b = a_free(kind, i, f"K{t}")
                s = slice(2 * t, 2 * t + 2)
                for k in range(KC):
                    mm = three(pA[:, b, :], (f.ctx_hi[:, k, s, :].rearrange("p s k -> p (s k)"),
                                             f.ctx_lo[:, k, s, :].rearrange("p s k -> p (s k)")),
                               (w_hi["k"][:, k, :], w_lo["k"][:, k, :]), k, k == KC - 1)
                mm.then_inc(k_done, 1)

            def transpose_k(kind, i, g, t):
                b = a_free(kind, i, f"KT{t}")
                a_copied(kind, i, f"K{t}")
                for m in range(KC):
                    mm = pe.transpose(pA[:, b, m * P:(m + 1) * P], f.k_sb[:, m * P:(m + 1) * P], ident[:])
                mm.then_inc(kt_done, 1)

            def project_v(kind, i, g):
                for t in range(f.nt):
                    b = a_free(kind, i, f"V{t}")
                    s = slice(2 * t, 2 * t + 2)
                    for k in range(KC):
                        mm = three(pA[:, b, :], (f.ctx_hi[:, k, s, :].rearrange("p s k -> p (s k)"),
                                                 f.ctx_lo[:, k, s, :].rearrange("p s k -> p (s k)")),
                                   (w_hi["v"][:, k, :], w_lo["v"][:, k, :]), k, k == KC - 1)
                    mm.then_inc(v_done, 1)

            def project_q(kind, i, m):
                if m == 0:
                    for q in range(c):
                        if q >= c - 2:
                            pe.wait_ge(t_drained[q % 2], f.t.after(kind, i, f"XT{q}", q % 2))
                b = a_free(kind, i, f"Q{m}")
                for k in range(KC):
                    mm = three(pA[:, b, 0:c * P], (w_hi["q"][:, k, m * P:(m + 1) * P], w_lo["q"][:, k, m * P:(m + 1) * P]),
                               (f.xt_hi[:, k, :], f.xt_lo[:, k, :]), k, k == KC - 1)
                mm.then_inc(q_done, 1)

            def scores(kind, i, g, d, q):
                for n in range(f.nbk):
                    u = (g * c + q) * f.nbk + n
                    ring = (q * f.nbk + n) % 2
                    wait(pe, s_drained, u - 1)
                    for m in range(KC):
                        if q == 0 and n == 0:
                            a_copied(kind, i, f"Q{m}")
                        if q == 0 and n == 0 and m == 0:
                            a_copied(kind, i, f"KT{f.nt - 1}")
                        mm = pe.matmul(pS[:, ring, m * 256:(m + 1) * 256], f.qt[:, d, m, q * P:(q + 1) * P],
                                       f.kd[:, d, (q // 2) * f.nbk + n, m, :], start=True, stop=True)
                    mm.then_inc(s_done, 1)

            def transpose_p(kind, i, q):
                pe.wait_ge(exp_ready, i * c + q + 1)
                for n in range(f.nbk):
                    for b in range(2):
                        t_free(kind, i, f"PT{q}.{n}", b)
                        for r in range(4):
                            k = 4 * b + r
                            mm = pe.transpose(pT[:, b, r * P:(r + 1) * P], f.s_sb[:, q % f.depth, n, k * P:(k + 1) * P], ident[:])
                    mm.then_inc(pt_done, 1)

            def weigh_v(kind, i, d, q):
                b = a_free(kind, i, f"PV{q}")
                if q == 0 and f.depth == 1:
                    a_copied(kind, i, f"V{f.nt - 1}")
                for h in range(2):
                    pe.wait_ge(t_drained[h], f.t.after(kind, i, f"PT{q}.{f.nbk - 1}", h))
                for r in range(H // 2):
                    for n in range(f.nbk):
                        mm = pe.matmul(pA[:, b, r * 2 * DH:(r + 1) * 2 * DH], f.pt[:, n, r, :],
                                       f.vd[:, d, (q // 2) * f.nbk + n, r, :], start=(n == 0), stop=(n == f.nbk - 1))
                mm.then_inc(pv_done, 1)

            def transpose_o(kind, i, q):
                b = q % 2
                t_free(kind, i, f"OT{q}", b)
                v = a_banks(f"PV{q}")[0]
                pe.wait_ge(a_drained[v], f.a.after(kind, i, f"PV{q}", v))
                for k in range(KC):
                    mm = pe.transpose(pT[:, b, k * P:(k + 1) * P], f.o_sb[:, k * P:(k + 1) * P], ident[:])
                mm.then_inc(ot_done, 1)

            def project_o(i, q):
                at, name = f.output_at(i, q)
                b = a_free(f.kind(at), at, name)
                pe.wait_ge(t_drained[q % 2], f.t.after(f.kind(i), i, f"OT{q}", q % 2))
                for k in range(KC):
                    mm = three(pA[:, b, :], (f.ot_hi[:, k, :], f.ot_lo[:, k, :]), (w_hi["o"][:, k, :], w_lo["o"][:, k, :]),
                               k, k == KC - 1)
                mm.then_inc(op_done, 1)

            if f.depth == 2:
                def first():
                    k = "prologue"
                    project_k(k, 0, 0, 0)
                    transpose_k(k, 0, 0, 0)
                    for q in range(c):
                        transpose_x(k, 0, 0, q)
                    for m in range(KC):
                        project_q(k, 0, m)
                    scores(k, 0, 0, 0, 0)
                    project_v(k, 0, 0)

                def step(i, d):
                    k = f.kind(i)
                    nxt = k != "last"
                    g, e = i + 1, 1 - d
                    transpose_p(k, i, 0)
                    scores(k, i, i, d, 1)
                    if nxt:
                        transpose_x(k, i, g, 0)
                    weigh_v(k, i, d, 0)
                    if nxt:
                        transpose_x(k, i, g, 1)
                    if k != "zero":
                        project_o(i - 1, 3)
                    transpose_o(k, i, 0)
                    if nxt:
                        project_k(k, i, g, 0)
                    transpose_p(k, i, 1)
                    scores(k, i, i, d, 2)
                    if nxt:
                        transpose_x(k, i, g, 2)
                    weigh_v(k, i, d, 1)
                    if nxt:
                        transpose_x(k, i, g, 3)
                    project_o(i, 0)
                    if nxt:
                        transpose_k(k, i, g, 0)
                    transpose_o(k, i, 1)
                    if nxt:
                        project_q(k, i, 0)
                    transpose_p(k, i, 2)
                    scores(k, i, i, d, 3)
                    weigh_v(k, i, d, 2)
                    project_o(i, 1)
                    transpose_o(k, i, 2)
                    if nxt:
                        project_q(k, i, 1)
                        project_q(k, i, 2)
                    transpose_p(k, i, 3)
                    if nxt:
                        project_q(k, i, 3)
                        scores(k, i, g, e, 0)
                    weigh_v(k, i, d, 3)
                    project_o(i, 2)
                    transpose_o(k, i, 3)
                    if nxt:
                        project_v(k, i, g)

                first()
                step(0, 0)
                step(1, 1)
                with pe.Fori(1, f.groups // 2 - 1) as j:
                    step(2 * j, 0)
                    step(2 * j + 1, 1)
                step(f.groups - 2, 0)
                step(f.groups - 1, 1)
                project_o(f.groups - 1, 3)
            else:
                def group(i, kind):
                    for t in range(f.nt):
                        project_k(kind, i, i, t)
                        transpose_k(kind, i, i, t)
                    project_v(kind, i, i)
                    for q in range(c):
                        transpose_x(kind, i, i, q)
                    for m in range(KC):
                        project_q(kind, i, m)
                    for q in range(c):
                        scores(kind, i, i, 0, q)
                        transpose_p(kind, i, q)
                        weigh_v(kind, i, 0, q)
                        transpose_o(kind, i, q)
                        project_o(i, q)

                group(0, "zero")
                with pe.Fori(1, f.groups) as i:
                    group(i, "step")

        with nc.Block() as block:
            def either(eng, part):
                short = eng.value_load(short_flag[0:1, 0:1], min_val=0, max_val=1)
                with eng.If(short == 1):
                    part(eng, SHORT)
                with eng.Else():
                    part(eng, FULL)

            @block.sync
            def _(sp):
                either(sp, sync_part)

            @block.gpsimd
            def _(pool):
                either(pool, gpsimd_part)

            @block.scalar
            def _(act):
                either(act, scalar_part)

            @block.vector
            def _(dve):
                either(dve, vector_part)

            @block.tensor
            def _(pe):
                either(pe, tensor_part)

        R = 6
        DVE_SPLITS = 6
        wf_hi = sb("wf_hi", [P, NE, KC * DM], F32R)
        g_row = sb("g_row", [P, R], I32)
        s_row = sb("s_row", [P, R], I32)
        xg = sb("xg", [P, R, DM + 2])
        xn2 = sb("xn2", [P, 2, DM])
        x2_hi = sb("x2_hi", [P, 2, DM], F32R)
        x2_lo = sb("x2_lo", [P, 2, DM], F32R)
        y2 = sb("y2", [P, 3, DM])

        wf_hi_ready = sem("wf_hi_ready")
        wf_lo_ready = sem("wf_lo_ready")
        wf_lo_pool = sem("wf_lo_pool")
        g_row_ready = sem("g_row_ready")
        s_row_ready = sem("s_row_ready")
        gathered = [sem(f"gathered_{r}") for r in range(R)]
        xn2_ready = sem("xn2_ready")
        x2t_done = sem("x2t_done")
        x2_hi_ready = sem("x2_hi_ready")
        x2_lo_ready = sem("x2_lo_ready")
        f_done = sem("f_done")
        y2_ready = sem("y2_ready")
        scattered = [sem(f"scattered_{r}") for r in range(R)]

        def at(k, n):
            return R * k + n, n % R, k + n // R

        def blocks(eng, body, split=None, splits=()):
            turns = (NR - 5 - 1) // R
            t = 0
            for n in range(-5, R):
                for _ in range(splits[n + 5] if n + 5 < len(splits) else 0):
                    split(t)
                    t += 1
                body(0, n)
            with eng.Fori(1, turns) as k:
                for n in range(R):
                    body(k, n)
            for n in range(NR + 1 - R * turns):
                body(turns, n)

        def is_block(k, n):
            return not isinstance(k, int) or 0 <= R * k + n < NR

        def split_low(eng, t):
            eng.wait_ge(wf_hi_ready, t + 1)
            return eng.tensor_tensor(wf_lo[:, t, :], wf_lo[:, t, :].bitcast(F32), wf_hi[:, t, :].bitcast(F32), ALU.subtract)

        with nc.Block() as block:
            @block.sync
            def _(sp):
                for t in WO_PLACES:
                    load_expert(sp, t)

            @block.gpsimd
            def _(pool):
                last_row = pool.to_reg(B * S - 1)

                def gather(k, n):
                    j, r, turn = at(k, n)
                    wait(pool, y2_ready, j + 1 - R)
                    pool.tensor_copy(g_row[:, r:r + 1], gather_rows[:, bass.ds(j, 1)]).then_inc(g_row_ready, 1)
                    wait_alone(pool, g_row_ready, j + 1, pool_passed)
                    pool.indirect_dma_start(xg[:, r, :], None, x1, bass.IndirectOffsetOnAxis(ap=g_row[:, r:r + 1], axis=0))\
                        .then_inc(gathered[r], 16)

                def scatter(k, n):
                    j, r, turn = at(k, n)
                    pool.wait_ge(y2_ready, j + 1)
                    pool.tensor_copy(s_row[:, r:r + 1], scatter_rows[:, bass.ds(j, 1)]).then_inc(s_row_ready, 1)
                    wait_alone(pool, s_row_ready, j + 1, pool_passed)
                    pool.indirect_dma_start(out, bass.IndirectOffsetOnAxis(ap=s_row[:, r:r + 1], axis=0), y2[:, r % 3, :], None,
                                            bounds_check=last_row, oob_is_err=False).then_inc(scattered[r], 16)

                def split(t):
                    split_low(pool, DVE_SPLITS + t).then_inc(wf_lo_pool, 1)

                def body(k, n):
                    if is_block(k, n - 1):
                        scatter(k, n - 1)
                    if is_block(k, n + 5):
                        gather(k, n + 5)

                blocks(pool, body, split, (0, 0, 0, 0, 0, NE - DVE_SPLITS))
                for r in range(R):
                    pool.wait_ge(scattered[r], 16 * len(range(r, NR, R)))

            @block.scalar
            def _(act):
                def split(t):
                    act.wait_ge(wf_loaded[t], 16)
                    act.copy(wf_hi[:, t, :], wf_lo[:, t, :].bitcast(F32)).then_inc(wf_hi_ready, 1)

                def high(k, n):
                    j, r, turn = at(k, n)
                    act.wait_ge(x2t_done, j + 1)
                    wait(act, f_done, j - 1)
                    act.copy(x2_hi[:, r % 2, :], pT[:, r % 2, :]).then_inc(x2_hi_ready, 1)

                def body(k, n):
                    if is_block(k, n + 1):
                        high(k, n + 1)

                blocks(act, body, split, (0, 0, 3, 1, 2, 2))

            @block.vector
            def _(dve):
                def split(t):
                    if t < DVE_SPLITS:
                        split_low(dve, t).then_inc(wf_lo_ready, 1)
                    else:
                        dve.wait_ge(wf_lo_pool, t + 1 - DVE_SPLITS)
                        dve.sem_inc(wf_lo_ready, 1)

                def normalise(k, n):
                    j, r, turn = at(k, n)
                    wait(dve, x2t_done, j - 1)
                    dve.wait_ge(gathered[r], 16 * turn + 16)
                    dve.tensor_scalar(xn2[:, r % 2, :], xg[:, r, 0:DM], xg[:, r, DM:DM + 1], xg[:, r, DM + 1:DM + 2],
                                      ALU.subtract, ALU.mult).then_inc(xn2_ready, 1)

                def low(k, n):
                    j, r, turn = at(k, n)
                    dve.wait_ge(x2_hi_ready, j + 1)
                    dve.tensor_tensor(x2_lo[:, r % 2, :], pT[:, r % 2, :], x2_hi[:, r % 2, :].bitcast(F32), ALU.subtract)\
                        .then_inc(x2_lo_ready, 1)

                def finish(k, n):
                    j, r, turn = at(k, n)
                    dve.wait_ge(f_done, j + 1)
                    if is_block(k, n - 3):
                        _, r3, turn3 = at(k, n - 3)
                        dve.wait_ge(scattered[r3], 16 * turn3 + 16)
                    dve.tensor_tensor(y2[:, r % 3, :], pA[:, r % 2, :], xg[:, r, 0:DM], ALU.add).then_inc(y2_ready, 1)

                def body(k, n):
                    if is_block(k, n + 1):
                        low(k, n + 1)
                    if is_block(k, n + 2):
                        normalise(k, n + 2)
                    if is_block(k, n):
                        finish(k, n)

                blocks(dve, body, split, (0, 0, 2, 1, 1, 4))

            @block.tensor
            def _(pe):
                def transpose(k, n):
                    j, r, turn = at(k, n)
                    pe.wait_ge(xn2_ready, j + 1)
                    wait(pe, x2_lo_ready, j - 1)
                    for c in range(KC):
                        mm = pe.transpose(pT[:, r % 2, c * P:(c + 1) * P], xn2[:, r % 2, c * P:(c + 1) * P], ident[:])
                    mm.then_inc(x2t_done, 1)

                def product(k, n):
                    j, r, turn = at(k, n)
                    e = pe.value_load(expert_of[0:1, bass.ds(j, 1)], min_val=0, max_val=NE - 1)
                    pe.wait_ge(wf_lo_ready, e + 1)
                    wait(pe, y2_ready, j - 1)
                    pe.matmul(pA[:, r % 2, :], ones_rows[:], bias_rows[:, bass.ds(e, 1), :].rearrange("p a n -> p (a n)"),
                              start=True, stop=False)
                    pe.wait_ge(x2_lo_ready, j + 1)
                    hi, lo = x2_hi[:, r % 2, :], x2_lo[:, r % 2, :]
                    for c in range(KC):
                        for a, w in ((hi, wf_hi), (hi, wf_lo), (lo, wf_hi)):
                            mm = pe.matmul(pA[:, r % 2, :], a[:, c * P:(c + 1) * P],
                                           w[:, bass.ds(e, 1), c * DM:(c + 1) * DM].rearrange("p a n -> p (a n)"),
                                           start=False, stop=(c == KC - 1 and a is lo))
                    mm.then_inc(f_done, 1)

                def body(k, n):
                    if is_block(k, n + 1):
                        transpose(k, n + 1)
                    if is_block(k, n):
                        product(k, n)

                blocks(pe, body)


def position_table():
    pos = np.arange(S, dtype=np.float32)[:, None]
    div = np.exp(np.arange(0, DP, 2, dtype=np.float32) * np.float32(-np.log(10000.0) / DP))
    ang = (pos * div).astype(np.float32)
    pe = np.zeros((S, DP), np.float32)
    pe[:, 0::2] = np.sin(ang)
    pe[:, 1::2] = np.cos(ang)
    return np.ascontiguousarray(pe.T)


def route_table():
    p = np.arange(P)
    before = (p[:, None] < p[None, :]).astype(np.float32)
    slot = np.concatenate([PB * np.arange(NR) + i for i in range(PB)])
    place = np.stack([(p // B == i) for i in range(PB)]).astype(np.float32)
    pos = np.concatenate([(h * P + p)[:, None] * place[i][None, :] for h in range(2) for i in range(PB)], axis=1)
    rows = lambda v: np.broadcast_to(np.asarray(v, np.float32)[None, :], (P, len(v)))
    return np.ascontiguousarray(np.concatenate([
        before, np.ones((P, P)), rows(slot), pos, rows(place.reshape(-1)), rows(np.arange(NE) - NE),
        (S * (p % B))[:, None], rows(np.arange(NR))], axis=1), dtype=np.float32)


def pick_table():
    return (np.arange(64)[:, None] % 32 == np.arange(NE)[None, :]).astype(np.float32)


def kernel(**inputs):
    import concourse.bacc as _bacc
    from concourse.bass_utils import run_bass_kernel_spmd as _run

    a = {k: np.asarray(v) for k, v in inputs.items()}
    c = np.ascontiguousarray
    ctx_t = a["ctx_1024"].reshape(B, NBLKS, BK, KC, P).transpose(0, 1, 4, 3, 2)
    mask = a["mask_BxSxS2_bk0"].reshape(B, 2, P, NBLKS, BK).transpose(3, 2, 0, 1, 4)
    pad = a["mask_BxS2_bf1"].reshape(B, 2, P).transpose(2, 0, 1)
    arrays = {
        "x": a["x"].reshape(B * S, DM),
        "ctx_t": ctx_t,
        "mask": mask,
        "pad": pad,
        "wq": a["L0_xattn_Wq"].T, "wk": a["L0_xattn_Wk"].T, "wv": a["L0_xattn_Wv"].T, "wo": a["L0_xattn_Wo"].T,
        "sigs_t": a["L0_ffn_tile_sigs"].T,
        "wf": a["L0_ffn_W"].transpose(0, 2, 1),
        "bf": a["L0_ffn_b"],
        "ident": np.eye(P, dtype=np.float32),
        "route": route_table(),
        "pe_t": position_table(),
        "pick": pick_table(),
    }
    nc = _bacc.Bacc("TRN2", target_bir_lowering=False, num_devices=1)
    feeds, args = {}, []
    for name, v in arrays.items():
        v = c(v)
        feeds[f"in_{name}"] = v
        args.append(nc.dram_tensor(f"in_{name}", v.shape, mybir.dt.from_np(v.dtype), kind="ExternalInput").ap())
    out = nc.dram_tensor("out_0_dram", (B * S, DM), F32, kind="ExternalOutput").ap()
    kernel_program(nc, *args, out)
    r = _run(nc, [feeds], core_ids=[0])
    return r.results[0]["out_0_dram"].reshape(B, S, DM)
```

```python
from contextlib import ExitStack

import numpy as np

import concourse.bass as bass
from concourse import mybir

F32 = mybir.dt.float32
F32R = mybir.dt.float32r
I32 = mybir.dt.int32
U32 = mybir.dt.uint32
U8 = mybir.dt.uint8
ALU = mybir.AluOpType
ACT = mybir.ActivationFunctionType
AX = mybir.AxisListType

P = 128
B, S, DM = 32, 256, 512
H, DH = 16, 32
KC = DM // P
HG = P // DH
BK = 64
NBLKS = S // BK
SCALE = float(DH) ** -0.5
EPS = 1e-5
BIG = 3e38
FLOOR = -1e38
TINY = 1e-30
NE, DP = 8, 32
PB = P // B
NR = (S + NE * (PB - 1)) // PB
OOB = 1 << 20


def wait_alone(eng, sem, value, passed):
    wait(eng, sem, value)
    if not isinstance(value, int):
        eng.sem_inc(passed, 1)


def wait(eng, sem, value):
    if isinstance(value, int) and value <= 0:
        return
    eng.wait_ge(sem, value)


class Drains:

    def __init__(self, lists, bank_of, signals):
        self.lists, self.bank_of, self.signals = lists, bank_of, signals

    def uses(self, names, bank):
        return self.signals * sum(bank in self.bank_of(n) for n in names)

    def before(self, kind, i, name, bank):
        names = self.lists[kind]
        first = self.uses(names[:names.index(name)], bank)
        if kind == "prologue":
            return first
        first = first + self.uses(self.lists["prologue"], bank)
        if kind == "zero":
            return first
        first = first + self.uses(self.lists["zero"], bank)
        return (i - 1) * self.uses(self.lists["step"], bank) + first

    def after(self, kind, i, name, bank):
        return self.before(kind, i, name, bank) + self.signals


def t_banks(name):
    if name.startswith("PT"):
        return (0, 1)
    if name.startswith(("XT", "OT")):
        return (int(name[2]) % 2,)
    return ()


A_BANK = {"PV0": 0, "OP3": 1, "K": 0, "PV1": 1, "OP0": 0, "KT": 1, "Q0": 0, "PV2": 1, "OP1": 0, "Q1": 1,
          "Q2": 0, "Q3": 1, "PV3": 0, "OP2": 1, "V": 0, "OP3z": 0}


def a_banks(name):
    key = name.rstrip("0123456789") if name[0] in "KV" else name
    return (A_BANK[key],) if key in A_BANK else ()


class Form:

    def __init__(self, nb, nbk, depth):
        self.nb, self.nbk, self.depth = nb, nbk, depth
        self.groups = B // nb
        self.c = 2 * nb
        self.slots = nb * nbk
        self.nt = self.slots // 2
        self.first_block = NBLKS - nbk
        c, nt, nbk = self.c, self.nt, self.nbk
        pt = lambda q: [f"PT{q}.{n}" for n in range(nbk)]
        sc = lambda q: [f"S{q}.{n}" for n in range(nbk)]
        kt, vt = [f"K{t}" for t in range(nt)], [f"V{t}" for t in range(nt)]
        ktt = [f"KT{t}" for t in range(nt)]
        if depth == 2:
            lists = {"prologue": kt + ["XT0", "XT1"] + ktt + ["XT2", "XT3", "Q0", "Q1", "Q2", "Q3"] + sc(0) + vt}
            for kind in ("zero", "step", "last"):
                nxt = kind != "last"
                o3 = ["OP3"] if kind != "zero" else []
                lists[kind] = (
                    pt(0) + sc(1) + (["XT0"] if nxt else []) + ["PV0"] + (["XT1"] if nxt else []) + o3 + ["OT0"]
                    + (kt if nxt else [])
                    + pt(1) + sc(2) + (["XT2"] if nxt else []) + ["PV1"] + (["XT3"] if nxt else []) + ["OP0"]
                    + (ktt if nxt else []) + ["OT1"] + (["Q0"] if nxt else [])
                    + pt(2) + sc(3) + ["PV2", "OP1", "OT2"] + (["Q1", "Q2"] if nxt else [])
                    + pt(3) + (["Q3"] + sc(0) if nxt else []) + ["PV3", "OP2", "OT3"] + (vt if nxt else ["OP3z"]))
        else:
            names = [n for pair in zip(kt, ktt) for n in pair] + vt + ["XT0", "XT1", "Q0", "Q1", "Q2", "Q3"]
            for q in range(c):
                names += sc(q) + pt(q) + [f"PV{q}", f"OT{q}", f"OP{q}"]
            lists = {"prologue": [], "zero": names, "step": names, "last": names}
        self.t = Drains(lists, t_banks, 2)
        self.a = Drains(lists, a_banks, 1)

    def place(self, d):
        return self.depth - 1 - d

    def kind(self, i):
        if isinstance(i, int) and i in (0, self.groups - 1):
            return "zero" if i == 0 else "last"
        return "step"

    def output_at(self, i, q):
        if q < 3:
            return i, f"OP{q}"
        return (i, "OP3z") if isinstance(i, int) and i == self.groups - 1 else (i + 1, "OP3")

    def output_read(self, i, q):
        at, name = self.output_at(i, q)
        b = a_banks(name)[0]
        return b, self.a.after(self.kind(at), at, name, b)


def kernel_program(nc, x, ctx_t, mask, pad, wq, wk, wv, wo, sigs_t, wf, bf, ident_d, route_d, pe_t, out):
    x1 = nc.dram_tensor("x1_scratch", (B * S, DM + 2), F32, kind="Internal").ap()
    top = ExitStack()
    with top:
        def sb(name, shape, dt=F32, stack=top):
            return stack.enter_context(nc.sbuf_tensor(name, shape, dt))

        def sem(name):
            return top.enter_context(nc.semaphore(name))

        pS = top.enter_context(nc.psum_tensor("pS", [P, 2, 2 * 512], F32))
        pT = top.enter_context(nc.psum_tensor("pT", [P, 2, 512], F32))
        pA = top.enter_context(nc.psum_tensor("pA", [P, 2, 512], F32))

        ident = sb("ident", [P, P])
        neg_half = sb("neg_half", [P, 1])
        gather_rows = sb("gather_rows", [P, NR], I32)
        scatter_rows = sb("scatter_rows", [P, NR], I32)
        expert_of = sb("expert_of", [1, NR], I32)
        short_flag = sb("short_flag", [1, 1], I32)
        bias_all = sb("bias_all", [P, NE, DM])

        attn_stack = ExitStack()
        w_hi = {n: sb(f"w{n}_hi", [P, KC, DM], F32R, attn_stack) for n in "qkv"}
        w_lo = {n: sb(f"w{n}_lo", [P, KC, DM], F32R, attn_stack) for n in "qkv"}
        w_hi["o"] = sb("wo_hi", [P, KC, DM], F32R, attn_stack)
        w_lo["o"] = sb("wo_lo", [P, KC, DM], F32R, attn_stack)

        prep = ExitStack()
        w_raw = sb("w_raw", [P, 4, KC * DM], F32, prep)
        mask_early = sb("mask_early", [P, NBLKS - 1, B * 2 * BK], U8, prep)
        NROUTE = route_d.shape[1]
        route = sb("route", [P, NROUTE], F32, prep)
        pe_sb = sb("pe_sb", [DP, S], F32, prep)
        sig = sb("sig", [DP, NE], F32, prep)
        sgn = sb("sgn", [DP, 3, NE], F32, prep)
        rt = sb("rt", [P, 2, 8, NE], F32, prep)
        cnt = sb("cnt", [P, 4, NE + 1], F32, prep)
        cnt_i = sb("cnt_i", [P, 2, NE], I32, prep)
        r1 = sb("r1", [P, 2, 4], F32, prep)
        match = sb("match", [P, 2, 2, PB * NR], F32, prep)
        rows_f = sb("rows_f", [P, 2, NR], F32, prep)
        expert_f = sb("expert_f", [1, NR, NE - 1], F32, prep)
        started = sb("started", [1, NR], F32, prep)
        early = sb("early", [P, 1], F32, prep)

        widths = (P, P, PB * NR, PB * P, NE, 1, NR, 2)
        ends = np.cumsum(widths)
        c_before, c_ones, c_slot, c_place, c_expert, c_batch, c_block, c_pos = (
            route[:, int(b) - n:int(b)] for b, n in zip(ends, widths))

        mask_loaded = sem("mask_loaded")
        consts_loaded = sem("consts_loaded")
        w_loaded = [sem(f"w_loaded_{n}") for n in "qkvo"]
        w_hi_ready = sem("w_hi_ready")
        w_lo_ready = [sem(f"w_lo_ready_{n}") for n in "qkvo"]
        half_set = sem("half_set")
        bias_loaded = sem("bias_loaded")
        pool_passed, dve_passed, sync_passed = sem("pool_passed"), sem("dve_passed"), sem("sync_passed")
        early_max = sem("early_max")
        early_sum = sem("early_sum")
        flag_ready = sem("flag_ready")
        rv = sem("route_vector")
        FOUND = 3 + 2 * 6
        MATCHED = FOUND + 4 + NE + 10
        rp = sem("route_product")

        def low(eng, n):
            k = "qkvo"[n]
            eng.wait_ge(w_hi_ready, n + 1)
            eng.tensor_tensor(w_lo[k][:].rearrange("p c n -> p (c n)"), w_raw[:, n, :],
                              w_hi[k][:].rearrange("p c n -> p (c n)").bitcast(F32), ALU.subtract)\
                .then_inc(w_lo_ready[n], 1)

        with nc.Block() as block:
            @block.sync
            def _(sp):
                sp.dma_start(mask_early[:], mask[0:NBLKS - 1].rearrange("k p b q j -> p k (b q j)"))\
                    .then_inc(mask_loaded, 16)
                sp.dma_start(ident[:], ident_d).then_inc(consts_loaded, 16)
                sp.dma_start(route[:], route_d).then_inc(consts_loaded, 16)
                sp.dma_start(pe_sb[:], pe_t).then_inc(consts_loaded, 16)
                sp.dma_start(sig[:], sigs_t).then_inc(consts_loaded, 16)
                for n, w in enumerate((wq, wk, wv, wo)):
                    sp.dma_start(w_raw[:, n, :].rearrange("p (c n) -> p c n", c=KC),
                                 w.rearrange("(c p) n -> p c n", p=P)).then_inc(w_loaded[n], 16)

            @block.gpsimd
            def _(pool):
                pool.memset(neg_half[:], -0.5).then_inc(half_set, 1)
                low(pool, 2)
                low(pool, 3)
                pool.wait_ge(w_lo_ready[3], 1)
                pool.wait_ge(half_set, 1)

            @block.scalar
            def _(act):
                for n, k in enumerate("qkvo"):
                    act.wait_ge(w_loaded[n], 16)
                    act.copy(w_hi[k][:].rearrange("p c n -> p (c n)"), w_raw[:, n, :]).then_inc(w_hi_ready, 1)
                act.wait_ge(w_hi_ready, 4)

            @block.vector
            def _(dve):
                step = [0]

                def done(ins):
                    step[0] += 1
                    ins.then_inc(rv, 1)
                    dve.wait_ge(rv, step[0])

                dve.wait_ge(mask_loaded, 16)
                dve.tensor_reduce(early[:], mask_early[:].rearrange("p k n -> p (k n)").bitcast(U32), AX.X, ALU.max)\
                    .then_inc(early_max, 1)
                dve.wait_ge(consts_loaded, 64)
                done(dve.tensor_scalar(sgn[:, 0, :], sig[:], 0.0, None, ALU.is_gt))
                done(dve.tensor_scalar(sgn[:, 1, :], sig[:], 0.0, None, ALU.is_lt))
                done(dve.tensor_tensor(sgn[:, 2, :], sgn[:, 0, :], sgn[:, 1, :], ALU.subtract))
                dve.wait_ge(rp, 1)
                for h in range(2):
                    sc = pA[:, h, 0:NE]
                    done(dve.tensor_reduce(r1[:, h, 0:1], sc, AX.X, ALU.max))
                    done(dve.tensor_scalar(rt[:, h, 0, :], sc, r1[:, h, 0:1], None, ALU.is_equal))
                    done(dve.scalar_tensor_tensor(rt[:, h, 1, :], rt[:, h, 0, :], -float(NE), c_expert, ALU.mult, ALU.add))
                    done(dve.tensor_scalar(rt[:, h, 1, :], rt[:, h, 1, :], float(NE), None, ALU.add))
                    done(dve.tensor_reduce(r1[:, h, 1:2], rt[:, h, 1, :], AX.X, ALU.min))
                    done(dve.tensor_scalar(rt[:, h, 2, :], c_expert, r1[:, h, 1:2], None, ALU.is_equal))
                low(dve, 0)
                dve.wait_ge(rp, 2)
                done(dve.tensor_scalar(cnt_i[:, 0, :], pA[:, 0, 256:256 + NE], float(PB - 1), None, ALU.add))
                done(dve.tensor_scalar(cnt_i[:, 1, :], cnt_i[:, 0, :], 2, None, ALU.arith_shift_right))
                done(dve.tensor_copy(cnt[:, 0, 0:NE], cnt_i[:, 1, :]))
                done(dve.memset(cnt[:, 1, 0:1], 0.0))
                for t in range(NE):
                    done(dve.tensor_tensor(cnt[:, 1, t + 1:t + 2], cnt[:, 1, t:t + 1], cnt[:, 0, t:t + 1], ALU.add))
                for h in range(2):
                    done(dve.scalar_tensor_tensor(rt[:, h, 3, :], cnt[:, 1, 0:NE], float(PB),
                                                  pA[:, 1, 64 + 64 * h:64 + 64 * h + NE], ALU.mult, ALU.add))
                    done(dve.tensor_tensor(rt[:, h, 4, :], rt[:, h, 3, :], rt[:, h, 2, :], ALU.mult))
                    done(dve.tensor_reduce(r1[:, h, 2:3], rt[:, h, 4, :], AX.X, ALU.add))
                    done(dve.tensor_scalar(match[:, h, 0, :], c_slot, r1[:, h, 2:3], None, ALU.is_equal))
                    done(dve.tensor_scalar(match[:, h, 1, :], match[:, h, 0, :], c_pos[:, h:h + 1], None, ALU.mult))
                done(dve.tensor_tensor(expert_f[:], c_block[0:1, :].unsqueeze(2).broadcast_to([1, NR, NE - 1]),
                                       cnt[0:1, 1:2, 1:NE].broadcast_to([1, NR, NE - 1]), ALU.is_ge))
                done(dve.tensor_reduce(started[:], expert_f[:], AX.X, ALU.add))
                done(dve.tensor_copy(expert_of[:], started[:]))
                low(dve, 1)
                dve.wait_ge(rp, 3)
                done(dve.tensor_scalar(rows_f[:, 0, :], pT[:, 0, NR:2 * NR], c_batch, None, ALU.add))
                done(dve.tensor_scalar(rows_f[:, 1, :], pT[:, 0, 0:NR], -float(OOB), float(OOB), ALU.mult, ALU.add))
                done(dve.tensor_copy(gather_rows[:], rows_f[:, 0, :]))
                done(dve.tensor_tensor(scatter_rows[:], rows_f[:, 0, :], rows_f[:, 1, :], ALU.add))
                dve.wait_ge(early_sum, 1)
                dve.tensor_scalar(short_flag[:], pS[0:1, 0, 0:1], 0.0, None, ALU.is_equal).then_inc(flag_ready, 1)
                for n in range(2):
                    dve.wait_ge(w_lo_ready[n], 1)
                dve.wait_ge(flag_ready, 1)

            @block.tensor
            def _(pe):
                pe.wait_ge(rv, 3)
                pe.wait_ge(consts_loaded, 64)
                for h in range(2):
                    mm = pe.matmul(pA[:, h, 0:NE], pe_sb[:, h * P:(h + 1) * P], sgn[:, 2, :], start=True, stop=True)
                mm.then_inc(rp, 1)
                pe.wait_ge(early_max, 1)
                pe.matmul(pS[0:1, 0, 0:1], early[:], c_ones[:, 0:1], start=True, stop=True).then_inc(early_sum, 1)
                pe.wait_ge(rv, FOUND)
                oh = [rt[:, h, 2, :] for h in range(2)]
                pe.matmul(pA[:, 0, 256:256 + NE], c_ones, oh[0], start=True, stop=False)
                pe.matmul(pA[:, 0, 256:256 + NE], c_ones, oh[1], start=False, stop=True)
                pe.matmul(pA[:, 1, 64:64 + NE], c_before, oh[0], start=True, stop=True)
                pe.matmul(pA[:, 1, 128:128 + NE], c_ones, oh[0], start=True, stop=False)
                pe.matmul(pA[:, 1, 128:128 + NE], c_before, oh[1], start=False, stop=True).then_inc(rp, 1)
                pe.wait_ge(rv, MATCHED)
                for k in range(2 * PB):
                    h, i = divmod(k, PB)
                    mm = pe.matmul(pT[:, 0, 0:2 * NR].rearrange("p (a n) -> p a n", a=2), c_place[:, i * P:(i + 1) * P],
                                   match[:, h, :, i * NR:(i + 1) * NR], start=(k == 0), stop=(k == 2 * PB - 1))
                mm.then_inc(rp, 1)
        prep.close()

        SHORT, FULL = Form(2, 1, 2), Form(1, NBLKS, 1)
        for f, tag in ((SHORT, "s"), (FULL, "f")):
            st = ExitStack()
            d = f.depth
            f.xn = sb(f"xn_{tag}", [P, f.c, DM], F32, st)
            f.xt_hi = sb(f"xt_hi_{tag}", [P, KC, f.c * P], F32R, st)
            f.xt_lo = sb(f"xt_lo_{tag}", [P, KC, f.c * P], F32R, st)
            f.ctx_hi = sb(f"ctx_hi_{tag}", [P, KC, f.slots, BK], F32R, st)
            f.ctx_lo = sb(f"ctx_lo_{tag}", [P, KC, f.slots, BK], F32R, st)
            f.k_sb = sb(f"k_{tag}", [P, DM], F32, st)
            f.ctx_raw = sb(f"ctx_raw_{tag}", [P, f.slots, KC, BK], F32, st)
            f.x_sb = sb(f"x_{tag}", [P, d, f.c, DM], F32, st)
            f.qt = sb(f"qt_{tag}", [P, d, KC, f.c * P], F32, st)
            f.mask_u8 = sb(f"mask_u8_{tag}", [P, f.c, f.nbk, BK], U8, st)
            f.pad_u8 = sb(f"pad_u8_{tag}", [P, f.c], U8, st)
            f.pad_big = sb(f"pad_big_{tag}", [P, f.c], F32, st)
            f.bias = sb(f"bias_{tag}", [P, d, f.c, f.nbk, BK], F32, st)
            f.stat = sb(f"stat_{tag}", [P, f.c, 6], F32, st)
            f.mom = sb(f"mom_{tag}", [P, f.c, 2], F32, st)
            f.rstd = sb(f"rstd_{tag}", [P, f.c, 3], F32, st)
            f.kd = sb(f"kd_{tag}", [P, d, f.slots, KC, HG * BK], F32, st)
            f.vd = sb(f"vd_{tag}", [P, d, f.slots, H // 2, 2 * DH], F32, st)
            f.s_sb = sb(f"s_{tag}", [P, d, f.nbk, H * BK], F32, st)
            f.row = sb(f"row_{tag}", [P, 2, 4, H], F32, st)
            f.pt = sb(f"pt_{tag}", [P, f.nbk, H // 2, P], F32, st)
            f.o_sb = sb(f"o_{tag}", [P, DM], F32, st)
            f.ot_hi = sb(f"ot_hi_{tag}", [P, KC, P], F32R, st)
            f.ot_lo = sb(f"ot_lo_{tag}", [P, KC, P], F32R, st)
            f.y_sb = sb(f"y_{tag}", [P, 2, DM + 2], F32, st)
            f.y_stat = sb(f"y_stat_{tag}", [P, 2, 6], F32, st)
            f.y_mom = sb(f"y_mom_{tag}", [P, 2, 2], F32, st)
            st.close()
        attn_stack.close()
        wf_hl = sb("wf_hl", [P, NE, 2 * KC * DM], F32R)
        EARLY = (0, 1, 2, 4, 5)
        POOL_LOW = EARLY[:4]
        LATE = (6, 7, 3)
        wf_loaded = [sem(f"wf_loaded_{t}") for t in range(NE)]
        wf_hi_ready = [sem(f"wf_hi_ready_{t}") for t in range(NE)]
        wf_lo_pool = sem("wf_lo_pool")
        wf_lo_dve = sem("wf_lo_dve")

        def part_of(t, n):
            return wf_hl[:, t, n * KC * DM:(n + 1) * KC * DM]

        def load_expert(sp, t):
            sp.dma_start(part_of(t, 1).bitcast(F32).rearrange("p (c n) -> p c n", c=KC),
                         wf[t].rearrange("(c p) n -> p c n", p=P)).then_inc(wf_loaded[t], 16)

        def expert_high(act, t):
            act.wait_ge(wf_loaded[t], 16)
            act.copy(part_of(t, 0), part_of(t, 1).bitcast(F32)).then_inc(wf_hi_ready[t], 1)

        def expert_low(eng, t):
            eng.wait_ge(wf_hi_ready[t], 1)
            return eng.tensor_tensor(part_of(t, 1), part_of(t, 1).bitcast(F32), part_of(t, 0).bitcast(F32), ALU.subtract)

        zeroed = sem("zeroed")
        x_loaded = [[sem(f"x_loaded_{d}{q}") for q in range(SHORT.c)] for d in range(2)]
        ctx_loaded = sem("ctx_loaded")
        mask_in = sem("mask_in")
        ctx_hi_ready = sem("ctx_hi_ready")
        ctx_lo_ready = sem("ctx_lo_ready")
        stat_ready = sem("stat_ready")
        mom_ready = sem("mom_ready")
        var_ready = sem("var_ready")
        rstd_ready = sem("rstd_ready")
        shift_ready = sem("shift_ready")
        xn_ready = sem("xn_ready")
        pad_ready = sem("pad_ready")
        bias_ready = sem("bias_ready")
        xt_done = sem("xt_done")
        k_done = sem("k_done")
        kt_done = sem("kt_done")
        v_done = sem("v_done")
        q_done = sem("q_done")
        s_done = sem("s_done")
        s_drained = sem("s_drained")
        max_ready = sem("max_ready")
        shifted = sem("shifted")
        exp_ready = sem("exp_ready")
        sum_ready = sem("sum_ready")
        floored = sem("floored")
        inv_ready = sem("inv_ready")
        pt_done = sem("pt_done")
        pv_done = sem("pv_done")
        ot_done = sem("ot_done")
        ot_hi_ready = sem("ot_hi_ready")
        op_done = sem("op_done")
        y_stat_ready = sem("y_stat_ready")
        y_mom_ready = sem("y_mom_ready")
        y_var_ready = sem("y_var_ready")
        y_ready = sem("y_ready")
        xt_hi_ready = sem("xt_hi_ready")
        t_drained = [sem(f"t_drained_{b}") for b in range(2)]
        a_drained = [sem(f"a_drained_{b}") for b in range(2)]
        y_stored = [sem(f"y_stored_{b}") for b in range(2)]

        def sync_part(sp, f):
            c = f.c

            def load_x(g, d, q):
                row = sp.snap(g * (c * P) + q * P) if not isinstance(g, int) else g * c * P + q * P
                if not (isinstance(g, int) and g < f.depth):
                    b, count = f.output_read(g - f.depth, q)
                    wait(sp, a_drained[b], count)
                sp.dma_start(f.x_sb[:, f.place(d), q, :], x[bass.ds(row, P), :]).then_inc(x_loaded[d][q], 16)

            def first_batch(g):
                return g * f.nb if isinstance(g, int) else sp.snap(g * f.nb)

            def load_bias():
                sp.dma_start(bias_all[:].rearrange("p t n -> p (t n)"),
                             bf.rearrange("(a t) n -> a (t n)", a=1).broadcast_to([P, NE * DM])).then_inc(bias_loaded, 16)

            def load_ctx(g):
                b0 = first_batch(g)
                wait(sp, ctx_lo_ready, g)
                for b in range(f.nb):
                    for n in range(f.nbk):
                        sp.dma_start(f.ctx_raw[:, b * f.nbk + n, :, :],
                                     ctx_t[bass.ds(b0 + b, 1), f.first_block + n].rearrange("a p c k -> (a p) c k"))\
                            .then_inc(ctx_loaded, 16)

            def load_mask(g):
                b0 = first_batch(g)
                wait_alone(sp, bias_ready, g * c, sync_passed)
                for n in range(f.nbk):
                    sp.dma_start(f.mask_u8[:, :, n, :],
                                 mask[f.first_block + n, :, bass.ds(b0, f.nb)].rearrange("p b q k -> p (b q) k"))\
                        .then_inc(mask_in, 16)
                sp.dma_start(f.pad_u8[:], pad[:, bass.ds(b0, f.nb)].rearrange("p b q -> p (b q)")).then_inc(mask_in, 16)

            def store_y(i, q):
                row = sp.snap(i * (c * P) + q * P) if not isinstance(i, int) else i * c * P + q * P
                sp.wait_ge(y_ready, i * c + q + 1)
                sp.dma_start(x1[bass.ds(row, P), :], f.y_sb[:, q % 2, :]).then_inc(y_stored[q % 2], 16)

            def load_projected():
                sp.wait_ge(kt_done, f.groups * f.nt)
                sp.wait_ge(q_done, f.groups * KC)
                sp.wait_ge(v_done, f.groups * f.nt)
                for t in (0, 1, 2, 4, 5):
                    load_expert(sp, t)

            def load_halves():
                for t in (6, 7):
                    load_expert(sp, t)

            def load_last():
                sp.wait_ge(op_done, f.groups * c)
                load_expert(sp, 3)

            def step(i, d, ahead=True, last=False):
                if last:
                    load_projected()
                if not (isinstance(i, int) and i == 0):
                    if not last:
                        load_x(i + 1, 1 - d, 3)
                    store_y(i - 1, 3)
                if last:
                    load_halves()
                if ahead:
                    load_ctx(i + 2)
                for q in range(3):
                    if ahead:
                        load_x(i + 2, d, q)
                    store_y(i, q)
                    if ahead and q == 0:
                        load_mask(i + 2)
                if last:
                    store_y(i, 3)
                    load_last()

            if f.depth == 2:
                load_ctx(0)
                for q in range(c):
                    load_x(0, 0, q)
                load_mask(0)
                for q in range(c):
                    load_x(1, 1, q)
                load_ctx(1)
                load_mask(1)
                load_bias()
                step(0, 0)
                step(1, 1)
                with sp.Fori(1, f.groups // 2 - 1) as j:
                    step(2 * j, 0)
                    step(2 * j + 1, 1)
                step(f.groups - 2, 0, ahead=False)
                step(f.groups - 1, 1, ahead=False, last=True)
            else:
                def group(i):
                    load_ctx(i)
                    load_mask(i)
                    for q in range(c):
                        load_x(i, 0, q)
                    for q in range(c):
                        store_y(i, q)

                group(0)
                load_bias()
                with sp.Fori(1, f.groups) as i:
                    group(i)
                load_projected()
                load_halves()
                load_last()
            for b in range(2):
                sp.wait_ge(y_stored[b], 16 * f.groups * c // 2)

        def gpsimd_part(pool, f):
            c = f.c
            if f.depth == 2:
                pool.memset(f.vd[:, 0], 0.0).then_inc(zeroed, 1)
                pool.memset(f.kd[:, 1], 0.0).then_inc(zeroed, 1)
            def ctx_low(g):
                wait(pool, ctx_hi_ready, g + 1)
                pool.tensor_tensor(f.ctx_lo[:].rearrange("p c s k -> p s c k"), f.ctx_raw[:],
                                   f.ctx_hi[:].bitcast(F32).rearrange("p c s k -> p s c k"), ALU.subtract)\
                    .then_inc(ctx_lo_ready, 1)

            def rstd(g, q):
                n = g * c + q
                wait_alone(pool, mom_ready, n + 1, pool_passed)
                pool.tensor_scalar(f.rstd[:, q, 0:1], f.mom[:, q, 1:2], EPS, None, ALU.add).then_inc(var_ready, 1)
                pool.wait_ge(var_ready, n + 1)
                pool.tensor_tensor(f.rstd[:, q, 1:2], f.rstd[:, q, 0:1], neg_half[:], ALU.pow).then_inc(rstd_ready, 1)
                wait_alone(pool, rstd_ready, n + 1, pool_passed)
                pool.tensor_scalar(f.rstd[:, q, 2:3], f.mom[:, q, 0:1], f.rstd[:, q, 1:2], -1.0,
                                   ALU.mult, ALU.mult).then_inc(shift_ready, 1)

            def y_rstd(i, q):
                n = i * c + q
                y = f.y_sb[:, q % 2, :]
                wait_alone(pool, y_mom_ready, n + 1, pool_passed)
                pool.tensor_copy(y[:, DM:DM + 1], f.y_mom[:, q % 2, 0:1])
                pool.tensor_scalar(f.y_mom[:, q % 2, 1:2], f.y_mom[:, q % 2, 1:2], EPS, None, ALU.add)\
                    .then_inc(y_var_ready, 1)
                pool.wait_ge(y_var_ready, n + 1)
                pool.tensor_tensor(y[:, DM + 1:DM + 2], f.y_mom[:, q % 2, 1:2], neg_half[:], ALU.pow).then_inc(y_ready, 1)

            def mask_bias(g, d):
                wait_alone(pool, mask_in, 16 * (f.nbk + 1) * (g + 1), pool_passed)
                pool.tensor_scalar(f.pad_big[:], f.pad_u8[:], BIG, None, ALU.mult).then_inc(pad_ready, 1)
                wait(pool, s_drained, (g + 1 - f.depth) * (c * f.nbk))
                wait_alone(pool, pad_ready, g + 1, pool_passed)
                for q in range(c):
                    pool.tensor_scalar(f.bias[:, d, q].rearrange("p n k -> p (n k)"),
                                       f.mask_u8[:, q].rearrange("p n k -> p (n k)"),
                                       f.pad_big[:, q:q + 1], -BIG, ALU.mult, ALU.add).then_inc(bias_ready, 1)

            if f.depth == 2:
                def step(i, d, nxt=True, ahead=True):
                    g = i + 1
                    if nxt:
                        ctx_low(g)
                        rstd(g, 2)
                        rstd(g, 3)
                    if not (isinstance(i, int) and i == 0):
                        y_rstd(i - 1, 3)
                    if nxt:
                        mask_bias(g, 1 - d)
                    y_rstd(i, 0)
                    y_rstd(i, 1)
                    if ahead:
                        rstd(g + 1, 0)
                    y_rstd(i, 2)
                    if ahead:
                        rstd(g + 1, 1)

                ctx_low(0)
                for q in range(c):
                    rstd(0, q)
                mask_bias(0, 0)
                rstd(1, 0)
                rstd(1, 1)
                step(0, 0)
                step(1, 1)
                with pool.Fori(1, f.groups // 2 - 1) as j:
                    step(2 * j, 0)
                    step(2 * j + 1, 1)
                step(f.groups - 2, 0, ahead=False)
                y_rstd(f.groups - 2, 3)
                y_rstd(f.groups - 1, 0)
                for t in POOL_LOW[:2]:
                    expert_low(pool, t).then_inc(wf_lo_pool, 1)
                y_rstd(f.groups - 1, 1)
                for t in POOL_LOW[2:]:
                    expert_low(pool, t).then_inc(wf_lo_pool, 1)
                y_rstd(f.groups - 1, 2)
                y_rstd(f.groups - 1, 3)
            else:
                def group(i):
                    ctx_low(i)
                    for q in range(c):
                        rstd(i, q)
                    mask_bias(i, 0)
                    for q in range(c):
                        y_rstd(i, q)

                group(0)
                with pool.Fori(1, f.groups) as i:
                    group(i)
                for t in POOL_LOW:
                    expert_low(pool, t).then_inc(wf_lo_pool, 1)

        def scalar_part(act, f):
            c = f.c

            def ctx_high(g):
                act.wait_ge(ctx_loaded, 16 * f.slots * (g + 1))
                wait(act, v_done, f.nt * g)
                act.copy(f.ctx_hi[:].rearrange("p c s k -> p s c k"), f.ctx_raw[:]).then_inc(ctx_hi_ready, 1)

            def xt_high(g, q):
                act.wait_ge(xt_done, g * c + q + 1)
                act.copy(f.xt_hi[:, :, q * P:(q + 1) * P], pT[:, q % 2, :].rearrange("p (c n) -> p c n", c=KC))\
                    .then_inc(xt_hi_ready, 1)

            def k_copy(g, t):
                act.wait_ge(k_done, g * f.nt + t + 1)
                act.copy(f.k_sb[:], pA[:, a_banks("K0")[0], :]).then_inc(a_drained[a_banks("K0")[0]], 1)

            def kt_copy(g, d, t):
                if isinstance(g, int) and g == 0:
                    act.wait_ge(zeroed, 2 * f.depth)
                b = a_banks("KT0")[0]
                act.wait_ge(kt_done, g * f.nt + t + 1)
                for h in range(HG):
                    r = slice(h * DH, (h + 1) * DH)
                    src = pA[r, b, :].rearrange("p (c s k) -> p c s k", c=KC, s=2)
                    for s in range(2):
                        ins = act.copy(f.kd[r, d, 2 * t + s, :, h * BK:(h + 1) * BK], src[:, :, s, :])
                ins.then_inc(a_drained[b], 1)

            def v_copy(g, d):
                for t in range(f.nt):
                    act.wait_ge(v_done, g * f.nt + t + 1)
                    src = pA[:, a_banks("V0")[0], :].rearrange("p (r e c) -> p r e c", r=H // 2, e=2)
                    for s in range(2):
                        for e in range(2):
                            ins = act.copy(f.vd[e * BK:(e + 1) * BK, d, 2 * t + s, :, e * DH:(e + 1) * DH],
                                           src[s * BK:(s + 1) * BK, :, e, :])
                    ins.then_inc(a_drained[a_banks("V0")[0]], 1)

            def q_copy(g, d, m):
                act.wait_ge(q_done, g * KC + m + 1)
                b = a_banks(f"Q{m}")[0]
                act.copy(f.qt[:, f.place(d), m, :], pA[:, b, 0:c * P]).then_inc(a_drained[b], 1)

            def exps(i, q):
                act.wait_ge(shifted, (i * c + q + 1) * f.nbk)
                t = f.s_sb[:, q % f.depth]
                act.activation(t, t, ACT.Exp, scale=-SCALE).then_inc(exp_ready, 1)

            def pt_copy(i, q):
                for n in range(f.nbk):
                    act.wait_ge(pt_done, (i * c + q) * f.nbk + n + 1)
                    for b in range(2):
                        act.copy(f.pt[:, n, 4 * b:4 * b + 4, :].rearrange("p r n -> p (r n)"), pT[:, b, :])\
                            .then_inc(t_drained[b], 2)

            def normalise(g, d, q):
                n = g * c + q
                wait(act, shift_ready, n + 1)
                wait(act, xt_done, n + 1 - c)
                act.activation(f.xn[:, q, :], f.x_sb[:, f.place(d), q, :], ACT.Identity, bias=f.rstd[:, q, 2:3],
                               scale=f.rstd[:, q, 1:2]).then_inc(xn_ready, 1)

            def ot_high(i, q):
                act.wait_ge(ot_done, i * c + q + 1)
                wait(act, op_done, i * c + q)
                act.copy(f.ot_hi[:].rearrange("p c n -> p (c n)"), pT[:, q % 2, :]).then_inc(ot_hi_ready, 1)

            if f.depth == 2:
                def first():
                    ctx_high(0)
                    for q in range(c):
                        normalise(0, 0, q)
                    k_copy(0, 0)
                    xt_high(0, 0)
                    xt_high(0, 1)
                    kt_copy(0, 0, 0)
                    xt_high(0, 2)
                    xt_high(0, 3)
                    normalise(1, 1, 0)
                    for m in range(KC):
                        q_copy(0, 0, m)
                    exps(0, 0)
                    v_copy(0, 0)

                def step(i, d, nxt=True, ahead=True):
                    g, e = i + 1, 1 - d
                    pt_copy(i, 0)
                    if nxt:
                        normalise(g, e, 1)
                        ctx_high(g)
                        xt_high(g, 0)
                        xt_high(g, 1)
                    exps(i, 1)
                    ot_high(i, 0)
                    if nxt:
                        normalise(g, e, 2)
                        k_copy(g, 0)
                    pt_copy(i, 1)
                    if not nxt:
                        expert_high(act, EARLY[0])
                        expert_high(act, EARLY[1])
                    if nxt:
                        normalise(g, e, 3)
                        xt_high(g, 2)
                        xt_high(g, 3)
                    exps(i, 2)
                    ot_high(i, 1)
                    if nxt:
                        kt_copy(g, e, 0)
                        q_copy(g, e, 0)
                    pt_copy(i, 2)
                    if not nxt:
                        expert_high(act, EARLY[2])
                        expert_high(act, EARLY[3])
                    exps(i, 3)
                    ot_high(i, 2)
                    if nxt:
                        q_copy(g, e, 1)
                    if ahead:
                        normalise(g + 1, d, 0)
                    if nxt:
                        q_copy(g, e, 2)
                    pt_copy(i, 3)
                    if not nxt:
                        expert_high(act, EARLY[4])
                    if nxt:
                        q_copy(g, e, 3)
                        exps(g, 0)
                    ot_high(i, 3)
                    if nxt:
                        v_copy(g, e)

                first()
                step(0, 0)
                step(1, 1)
                with act.Fori(1, f.groups // 2 - 1) as j:
                    step(2 * j, 0)
                    step(2 * j + 1, 1)
                step(f.groups - 2, 0, ahead=False)
                step(f.groups - 1, 1, nxt=False, ahead=False)
            else:
                def group(i):
                    ctx_high(i)
                    for q in range(c):
                        normalise(i, 0, q)
                    for t in range(f.nt):
                        k_copy(i, t)
                        kt_copy(i, 0, t)
                    v_copy(i, 0)
                    for q in range(c):
                        xt_high(i, q)
                    for m in range(KC):
                        q_copy(i, 0, m)
                    for q in range(c):
                        exps(i, q)
                        pt_copy(i, q)
                        ot_high(i, q)

                group(0)
                with act.Fori(1, f.groups) as i:
                    group(i)
                for t in EARLY:
                    expert_high(act, t)

        def vector_part(dve, f):
            c = f.c
            dve.memset(f.kd[:, 0], 0.0).then_inc(zeroed, 1)
            dve.memset(f.vd[:, f.depth - 1], 0.0).then_inc(zeroed, 1)

            def moments(g, d, q):
                n = g * c + q
                dve.wait_ge(x_loaded[d][q], (16 // f.depth) * (g - d) + 16)
                dve.bn_stats(f.stat[:, q, :], f.x_sb[:, f.place(d), q, :]).then_inc(stat_ready, 1)
                wait(dve, xn_ready, n + 1 - c)
                wait_alone(dve, stat_ready, n + 1, dve_passed)
                dve.bn_aggr(f.mom[:, q, :], f.stat[:, q, :]).then_inc(mom_ready, 1)

            def xt_low(g, q):
                dve.wait_ge(xt_hi_ready, g * c + q + 1)
                t = slice(q * P, (q + 1) * P)
                dve.tensor_tensor(f.xt_lo[:, :, t], pT[:, q % 2, :].rearrange("p (c n) -> p c n", c=KC),
                                  f.xt_hi[:, :, t].bitcast(F32), ALU.subtract).then_inc(t_drained[q % 2], 2)

            def mask_scores(i, d, q):
                n = i * c + q
                dve.wait_ge(bias_ready, n + 1)
                wait(dve, pt_done, (n + 1 - f.depth) * f.nbk)
                for k in range(f.nbk):
                    u = n * f.nbk + k
                    dve.wait_ge(s_done, u + 1)
                    ring = (q * f.nbk + k) % 2
                    dve.tensor_tensor(f.s_sb[:, q % f.depth, k, :].rearrange("p (h k) -> p h k", h=H),
                                      pS[:, ring, :].rearrange("p (h k) -> p h k", h=H),
                                      f.bias[:, d, q, k:k + 1, :].broadcast_to([P, H, BK]), ALU.add).then_inc(s_drained, 1)
                dve.wait_ge(s_drained, (n + 1) * f.nbk)
                t = f.s_sb[:, q % f.depth].rearrange("p n (h k) -> p h n k", h=H)
                dve.tensor_reduce(f.row[:, q % 2, 0, :], t, AX.XY, ALU.max).then_inc(max_ready, 1)

            def shift_scores(i, q):
                dve.wait_ge(max_ready, i * c + q + 1)
                for k in range(f.nbk):
                    t = f.s_sb[:, q % f.depth, k, :].rearrange("p (h k) -> p h k", h=H)
                    dve.scalar_tensor_tensor(t, f.row[:, q % 2, 0, :].unsqueeze(2).broadcast_to([P, H, BK]), FLOOR, t,
                                             ALU.max, ALU.subtract).then_inc(shifted, 1)

            def row_sums(i, q):
                n = i * c + q
                dve.wait_ge(exp_ready, n + 1)
                t = f.s_sb[:, q % f.depth].rearrange("p n (h k) -> p h n k", h=H)
                dve.tensor_reduce(f.row[:, q % 2, 1, :], t, AX.XY, ALU.add).then_inc(sum_ready, 1)
                dve.wait_ge(sum_ready, n + 1)
                dve.tensor_scalar(f.row[:, q % 2, 2, :], f.row[:, q % 2, 1, :], TINY, None, ALU.max).then_inc(floored, 1)
                dve.wait_ge(floored, n + 1)
                dve.reciprocal(f.row[:, q % 2, 3, :], f.row[:, q % 2, 2, :]).then_inc(inv_ready, 1)

            def o_scale(i, q):
                n = i * c + q
                b = a_banks(f"PV{q}")[0]
                dve.wait_ge(inv_ready, n + 1)
                dve.wait_ge(pv_done, n + 1)
                wait(dve, ot_done, n)
                dve.tensor_tensor(f.o_sb[:].rearrange("p (h e) -> p h e", h=H),
                                  pA[:, b, :].rearrange("p (h e) -> p h e", h=H),
                                  f.row[:, q % 2, 3, :].unsqueeze(2).broadcast_to([P, H, DH]), ALU.mult)\
                    .then_inc(a_drained[b], 1)

            def ot_low(i, q):
                dve.wait_ge(ot_hi_ready, i * c + q + 1)
                dve.tensor_tensor(f.ot_lo[:].rearrange("p c n -> p (c n)"), pT[:, q % 2, :],
                                  f.ot_hi[:].rearrange("p c n -> p (c n)").bitcast(F32), ALU.subtract)\
                    .then_inc(t_drained[q % 2], 2)

            def residual(i, d, q):
                b, _ = f.output_read(i, q)
                dve.wait_ge(op_done, i * c + q + 1)
                wait(dve, y_stored[q % 2], 16 * (i * (c // 2) + q // 2))
                dve.tensor_tensor(f.y_sb[:, q % 2, 0:DM], pA[:, b, :], f.x_sb[:, f.place(d), q, :], ALU.add)\
                    .then_inc(a_drained[b], 1)

            def y_moments(i, q):
                n = i * c + q
                b, count = f.output_read(i, q)
                dve.wait_ge(a_drained[b], count)
                dve.bn_stats(f.y_stat[:, q % 2, :], f.y_sb[:, q % 2, 0:DM]).then_inc(y_stat_ready, 1)
                wait(dve, y_ready, n - 1)
                wait_alone(dve, y_stat_ready, n + 1, dve_passed)
                dve.bn_aggr(f.y_mom[:, q % 2, :], f.y_stat[:, q % 2, :]).then_inc(y_mom_ready, 1)

            if f.depth == 2:
                def step(i, d, nxt=True, ahead=True):
                    g, e = i + 1, 1 - d
                    row_sums(i, 0)
                    mask_scores(i, d, 1)
                    if nxt:
                        o_scale(i, 0)
                    shift_scores(i, 1)
                    if not nxt:
                        o_scale(i, 0)
                    if nxt:
                        xt_low(g, 0)
                    if not (isinstance(i, int) and i == 0):
                        residual(i - 1, e, 3)
                    if nxt:
                        xt_low(g, 1)
                        moments(g, e, 2)
                    ot_low(i, 0)
                    if nxt:
                        moments(g, e, 3)
                    row_sums(i, 1)
                    mask_scores(i, d, 2)
                    if nxt:
                        o_scale(i, 1)
                        xt_low(g, 2)
                        xt_low(g, 3)
                    shift_scores(i, 2)
                    if not nxt:
                        o_scale(i, 1)
                    residual(i, d, 0)
                    ot_low(i, 1)
                    if not (isinstance(i, int) and i == 0):
                        y_moments(i - 1, 3)
                    y_moments(i, 0)
                    row_sums(i, 2)
                    mask_scores(i, d, 3)
                    if nxt:
                        o_scale(i, 2)
                    shift_scores(i, 3)
                    if not nxt:
                        o_scale(i, 2)
                    residual(i, d, 1)
                    ot_low(i, 2)
                    y_moments(i, 1)
                    if ahead:
                        moments(g + 1, d, 0)
                    row_sums(i, 3)
                    if nxt:
                        mask_scores(g, e, 0)
                    o_scale(i, 3)
                    if nxt:
                        shift_scores(g, 0)
                    residual(i, d, 2)
                    ot_low(i, 3)
                    y_moments(i, 2)
                    if ahead:
                        moments(g + 1, d, 1)

                for q in range(c):
                    moments(0, 0, q)
                moments(1, 1, 0)
                moments(1, 1, 1)
                for q in range(c):
                    xt_low(0, q)
                mask_scores(0, 0, 0)
                shift_scores(0, 0)
                step(0, 0)
                step(1, 1)
                with dve.Fori(1, f.groups // 2 - 1) as j:
                    step(2 * j, 0)
                    step(2 * j + 1, 1)
                step(f.groups - 2, 0, ahead=False)
                step(f.groups - 1, 1, nxt=False, ahead=False)
                residual(f.groups - 1, 1, 3)
                y_moments(f.groups - 1, 3)
                expert_low(dve, 5).then_inc(wf_lo_dve, 1)
            else:
                def group(i):
                    for q in range(c):
                        moments(i, 0, q)
                    for q in range(c):
                        xt_low(i, q)
                    for q in range(c):
                        mask_scores(i, 0, q)
                        shift_scores(i, q)
                        row_sums(i, q)
                        o_scale(i, q)
                        ot_low(i, q)
                        residual(i, 0, q)
                        y_moments(i, q)

                group(0)
                with dve.Fori(1, f.groups) as i:
                    group(i)
                expert_low(dve, 5).then_inc(wf_lo_dve, 1)

        def tensor_part(pe, f):
            c = f.c

            def t_free(kind, i, name, b):
                wait(pe, t_drained[b], f.t.before(kind, i, name, b))

            def a_free(kind, i, name):
                b = a_banks(name)[0]
                wait(pe, a_drained[b], f.a.before(kind, i, name, b))
                return b

            def a_copied(kind, i, name):
                b = a_banks(name)[0]
                pe.wait_ge(a_drained[b], f.a.after(kind, i, name, b))

            def three(dst, lhs, rhs, k, last):
                for n, (a, b) in enumerate(((0, 0), (0, 1), (1, 0))):
                    mm = pe.matmul(dst, lhs[a], rhs[b], start=(k == 0 and n == 0), stop=(last and n == 2))
                return mm

            def transpose_x(kind, i, g, q):
                b = q % 2
                pe.wait_ge(xn_ready, g * c + q + 1)
                t_free(kind, i, f"XT{q}", b)
                for k in range(KC):
                    mm = pe.transpose(pT[:, b, k * P:(k + 1) * P], f.xn[:, q, k * P:(k + 1) * P], ident[:])
                mm.then_inc(xt_done, 1)

            def project_k(kind, i, g, t):
                pe.wait_ge(ctx_lo_ready, g + 1)
                b = a_free(kind, i, f"K{t}")
                s = slice(2 * t, 2 * t + 2)
                for k in range(KC):
                    mm = three(pA[:, b, :], (f.ctx_hi[:, k, s, :].rearrange("p s k -> p (s k)"),
                                             f.ctx_lo[:, k, s, :].rearrange("p s k -> p (s k)")),
                               (w_hi["k"][:, k, :], w_lo["k"][:, k, :]), k, k == KC - 1)
                mm.then_inc(k_done, 1)

            def transpose_k(kind, i, g, t):
                b = a_free(kind, i, f"KT{t}")
                a_copied(kind, i, f"K{t}")
                for m in range(KC):
                    mm = pe.transpose(pA[:, b, m * P:(m + 1) * P], f.k_sb[:, m * P:(m + 1) * P], ident[:])
                mm.then_inc(kt_done, 1)

            def project_v(kind, i, g):
                for t in range(f.nt):
                    b = a_free(kind, i, f"V{t}")
                    s = slice(2 * t, 2 * t + 2)
                    for k in range(KC):
                        mm = three(pA[:, b, :], (f.ctx_hi[:, k, s, :].rearrange("p s k -> p (s k)"),
                                                 f.ctx_lo[:, k, s, :].rearrange("p s k -> p (s k)")),
                                   (w_hi["v"][:, k, :], w_lo["v"][:, k, :]), k, k == KC - 1)
                    mm.then_inc(v_done, 1)

            def project_q(kind, i, m):
                if m == 0:
                    for q in range(c):
                        if q >= c - 2:
                            pe.wait_ge(t_drained[q % 2], f.t.after(kind, i, f"XT{q}", q % 2))
                b = a_free(kind, i, f"Q{m}")
                for k in range(KC):
                    mm = three(pA[:, b, 0:c * P], (w_hi["q"][:, k, m * P:(m + 1) * P], w_lo["q"][:, k, m * P:(m + 1) * P]),
                               (f.xt_hi[:, k, :], f.xt_lo[:, k, :]), k, k == KC - 1)
                mm.then_inc(q_done, 1)

            def scores(kind, i, g, d, q):
                for n in range(f.nbk):
                    u = (g * c + q) * f.nbk + n
                    ring = (q * f.nbk + n) % 2
                    wait(pe, s_drained, u - 1)
                    for m in range(KC):
                        if q == 0 and n == 0:
                            a_copied(kind, i, f"Q{m}")
                        if q == 0 and n == 0 and m == 0:
                            a_copied(kind, i, f"KT{f.nt - 1}")
                        mm = pe.matmul(pS[:, ring, m * 256:(m + 1) * 256], f.qt[:, f.place(d), m, q * P:(q + 1) * P],
                                       f.kd[:, d, (q // 2) * f.nbk + n, m, :], start=True, stop=True)
                    mm.then_inc(s_done, 1)

            def transpose_p(kind, i, q):
                pe.wait_ge(exp_ready, i * c + q + 1)
                for n in range(f.nbk):
                    for b in range(2):
                        t_free(kind, i, f"PT{q}.{n}", b)
                        for r in range(4):
                            k = 4 * b + r
                            mm = pe.transpose(pT[:, b, r * P:(r + 1) * P],
                                              f.s_sb[:, q % f.depth, n, k * P:(k + 1) * P], ident[:])
                    mm.then_inc(pt_done, 1)

            def weigh_v(kind, i, d, q):
                b = a_free(kind, i, f"PV{q}")
                if q == 0 and f.depth == 1:
                    a_copied(kind, i, f"V{f.nt - 1}")
                for h in range(2):
                    pe.wait_ge(t_drained[h], f.t.after(kind, i, f"PT{q}.{f.nbk - 1}", h))
                for r in range(H // 2):
                    for n in range(f.nbk):
                        mm = pe.matmul(pA[:, b, r * 2 * DH:(r + 1) * 2 * DH], f.pt[:, n, r, :],
                                       f.vd[:, d, (q // 2) * f.nbk + n, r, :], start=(n == 0), stop=(n == f.nbk - 1))
                mm.then_inc(pv_done, 1)

            def transpose_o(kind, i, q):
                b = q % 2
                t_free(kind, i, f"OT{q}", b)
                v = a_banks(f"PV{q}")[0]
                pe.wait_ge(a_drained[v], f.a.after(kind, i, f"PV{q}", v))
                for k in range(KC):
                    mm = pe.transpose(pT[:, b, k * P:(k + 1) * P], f.o_sb[:, k * P:(k + 1) * P], ident[:])
                mm.then_inc(ot_done, 1)

            def project_o(i, q):
                at, name = f.output_at(i, q)
                b = a_free(f.kind(at), at, name)
                pe.wait_ge(t_drained[q % 2], f.t.after(f.kind(i), i, f"OT{q}", q % 2))
                for k in range(KC):
                    mm = three(pA[:, b, :], (f.ot_hi[:, k, :], f.ot_lo[:, k, :]), (w_hi["o"][:, k, :], w_lo["o"][:, k, :]),
                               k, k == KC - 1)
                mm.then_inc(op_done, 1)

            if f.depth == 2:
                def first():
                    k = "prologue"
                    project_k(k, 0, 0, 0)
                    transpose_x(k, 0, 0, 0)
                    transpose_x(k, 0, 0, 1)
                    transpose_k(k, 0, 0, 0)
                    transpose_x(k, 0, 0, 2)
                    transpose_x(k, 0, 0, 3)
                    for m in range(KC):
                        project_q(k, 0, m)
                    scores(k, 0, 0, 0, 0)
                    project_v(k, 0, 0)

                def step(i, d):
                    k = f.kind(i)
                    nxt = k != "last"
                    g, e = i + 1, 1 - d
                    if not nxt:
                        scores(k, i, i, d, 1)
                    transpose_p(k, i, 0)
                    scores(k, i, i, d, 1 if nxt else 2)
                    if nxt:
                        transpose_x(k, i, g, 0)
                    weigh_v(k, i, d, 0)
                    if nxt:
                        transpose_x(k, i, g, 1)
                    if k != "zero":
                        project_o(i - 1, 3)
                    transpose_o(k, i, 0)
                    if nxt:
                        project_k(k, i, g, 0)
                    transpose_p(k, i, 1)
                    scores(k, i, i, d, 2 if nxt else 3)
                    if nxt:
                        transpose_x(k, i, g, 2)
                    weigh_v(k, i, d, 1)
                    if nxt:
                        transpose_x(k, i, g, 3)
                    project_o(i, 0)
                    if nxt:
                        transpose_k(k, i, g, 0)
                    transpose_o(k, i, 1)
                    if nxt:
                        project_q(k, i, 0)
                    transpose_p(k, i, 2)
                    if nxt:
                        scores(k, i, i, d, 3)
                    weigh_v(k, i, d, 2)
                    project_o(i, 1)
                    transpose_o(k, i, 2)
                    if nxt:
                        project_q(k, i, 1)
                        project_q(k, i, 2)
                    transpose_p(k, i, 3)
                    if nxt:
                        project_q(k, i, 3)
                        scores(k, i, g, e, 0)
                    weigh_v(k, i, d, 3)
                    project_o(i, 2)
                    transpose_o(k, i, 3)
                    if nxt:
                        project_v(k, i, g)

                first()
                step(0, 0)
                step(1, 1)
                with pe.Fori(1, f.groups // 2 - 1) as j:
                    step(2 * j, 0)
                    step(2 * j + 1, 1)
                step(f.groups - 2, 0)
                step(f.groups - 1, 1)
                project_o(f.groups - 1, 3)
            else:
                def group(i, kind):
                    for t in range(f.nt):
                        project_k(kind, i, i, t)
                        transpose_k(kind, i, i, t)
                    project_v(kind, i, i)
                    for q in range(c):
                        transpose_x(kind, i, i, q)
                    for m in range(KC):
                        project_q(kind, i, m)
                    for q in range(c):
                        scores(kind, i, i, 0, q)
                        transpose_p(kind, i, q)
                        weigh_v(kind, i, 0, q)
                        transpose_o(kind, i, q)
                        project_o(i, q)

                group(0, "zero")
                with pe.Fori(1, f.groups) as i:
                    group(i, "step")

        with nc.Block() as block:
            def either(eng, part):
                short = eng.value_load(short_flag[0:1, 0:1], min_val=0, max_val=1)
                with eng.If(short == 1):
                    part(eng, SHORT)
                with eng.Else():
                    part(eng, FULL)

            @block.sync
            def _(sp):
                either(sp, sync_part)

            @block.gpsimd
            def _(pool):
                either(pool, gpsimd_part)

            @block.scalar
            def _(act):
                either(act, scalar_part)

            @block.vector
            def _(dve):
                either(dve, vector_part)

            @block.tensor
            def _(pe):
                either(pe, tensor_part)

        R = 6
        g_row = sb("g_row", [P, R], I32)
        s_row = sb("s_row", [P, R], I32)
        xg = sb("xg", [P, R, DM + 2])
        xb = sb("xb", [P, 2, DM])
        xn2 = sb("xn2", [P, 2, DM])
        x2_hi = sb("x2_hi", [P, 2, DM], F32R)
        x2_lo = sb("x2_lo", [P, 2, DM], F32R)
        y2 = sb("y2", [P, 3, DM])

        wf_lo_ready = sem("wf_lo_ready")
        xb_ready = sem("xb_ready")
        g_row_ready = sem("g_row_ready")
        s_row_ready = sem("s_row_ready")
        gathered = [sem(f"gathered_{r}") for r in range(R)]
        xn2_ready = sem("xn2_ready")
        x2t_done = sem("x2t_done")
        x2_hi_ready = sem("x2_hi_ready")
        x2_lo_ready = sem("x2_lo_ready")
        f_done = sem("f_done")
        y2_ready = sem("y2_ready")
        scattered = [sem(f"scattered_{r}") for r in range(R)]

        def at(k, n):
            return R * k + n, n % R, k + n // R

        def blocks(eng, body):
            turns = (NR - 5 - 1) // R
            for n in range(-5, R):
                body(0, n)
            with eng.Fori(1, turns) as k:
                for n in range(R):
                    body(k, n)
            for n in range(NR + 1 - R * turns):
                body(turns, n)

        def is_block(k, n):
            return not isinstance(k, int) or 0 <= R * k + n < NR

        with nc.Block() as block:
            @block.gpsimd
            def _(pool):
                last_row = pool.to_reg(B * S - 1)

                def gather(k, n):
                    j, r, turn = at(k, n)
                    wait(pool, y2_ready, j + 1 - R)
                    pool.tensor_copy(g_row[:, r:r + 1], gather_rows[:, bass.ds(j, 1)]).then_inc(g_row_ready, 1)
                    wait_alone(pool, g_row_ready, j + 1, pool_passed)
                    pool.indirect_dma_start(xg[:, r, :], None, x1, bass.IndirectOffsetOnAxis(ap=g_row[:, r:r + 1], axis=0))\
                        .then_inc(gathered[r], 16)

                def scatter(k, n):
                    j, r, turn = at(k, n)
                    pool.wait_ge(y2_ready, j + 1)
                    pool.tensor_copy(s_row[:, r:r + 1], scatter_rows[:, bass.ds(j, 1)]).then_inc(s_row_ready, 1)
                    wait_alone(pool, s_row_ready, j + 1, pool_passed)
                    pool.indirect_dma_start(out, bass.IndirectOffsetOnAxis(ap=s_row[:, r:r + 1], axis=0), y2[:, r % 3, :], None,
                                            bounds_check=last_row, oob_is_err=False).then_inc(scattered[r], 16)

                def body(k, n):
                    if is_block(k, n - 1):
                        scatter(k, n - 1)
                    if is_block(k, n + 5):
                        gather(k, n + 5)

                blocks(pool, body)
                for r in range(R):
                    pool.wait_ge(scattered[r], 16 * len(range(r, NR, R)))

            @block.scalar
            def _(act):
                def high(k, n):
                    j, r, turn = at(k, n)
                    act.wait_ge(x2t_done, j + 1)
                    wait(act, f_done, j - 1)
                    act.copy(x2_hi[:, r % 2, :], pT[:, r % 2, :]).then_inc(x2_hi_ready, 1)

                def body(k, n):
                    if is_block(k, n + 1):
                        high(k, n + 1)

                for t in LATE:
                    expert_high(act, t)
                blocks(act, body)

            @block.vector
            def _(dve):
                def add_bias(k, n):
                    j, r, turn = at(k, n)
                    e = dve.value_load(expert_of[0:1, bass.ds(j, 1)], min_val=0, max_val=NE - 1)
                    dve.tensor_tensor(xb[:, r % 2, :], xg[:, r, 0:DM],
                                      bias_all[:, bass.ds(e, 1), :].rearrange("p a n -> p (a n)"), ALU.add)\
                        .then_inc(xb_ready, 1)

                def normalise(k, n):
                    j, r, turn = at(k, n)
                    wait(dve, x2t_done, j - 1)
                    dve.wait_ge(gathered[r], 16 * turn + 16)
                    dve.tensor_scalar(xn2[:, r % 2, :], xg[:, r, 0:DM], xg[:, r, DM:DM + 1], xg[:, r, DM + 1:DM + 2],
                                      ALU.subtract, ALU.mult).then_inc(xn2_ready, 1)

                def low(k, n):
                    j, r, turn = at(k, n)
                    dve.wait_ge(x2_hi_ready, j + 1)
                    dve.tensor_tensor(x2_lo[:, r % 2, :], pT[:, r % 2, :], x2_hi[:, r % 2, :].bitcast(F32), ALU.subtract)\
                        .then_inc(x2_lo_ready, 1)

                def finish(k, n):
                    j, r, turn = at(k, n)
                    dve.wait_ge(f_done, j + 1)
                    if is_block(k, n - 3):
                        _, r3, turn3 = at(k, n - 3)
                        dve.wait_ge(scattered[r3], 16 * turn3 + 16)
                    dve.wait_ge(xb_ready, j + 1)
                    dve.tensor_tensor(y2[:, r % 3, :], pA[:, r % 2, :], xb[:, r % 2, :], ALU.add).then_inc(y2_ready, 1)

                def body(k, n):
                    if is_block(k, n + 1):
                        low(k, n + 1)
                    if is_block(k, n + 2):
                        normalise(k, n + 2)
                    if isinstance(k, int) and R * k + n == 0:
                        expert_low(dve, LATE[1])
                        expert_low(dve, LATE[2]).then_inc(wf_lo_ready, NE - 3)
                    if is_block(k, n):
                        finish(k, n)
                    if is_block(k, n + 1):
                        add_bias(k, n + 1)

                dve.wait_ge(bias_loaded, 16)
                dve.wait_ge(wf_lo_pool, 4)
                dve.sem_inc(wf_lo_ready, 3)
                dve.wait_ge(wf_lo_dve, 1)
                expert_low(dve, LATE[0])
                blocks(dve, body)

            @block.tensor
            def _(pe):
                def transpose(k, n):
                    j, r, turn = at(k, n)
                    pe.wait_ge(xn2_ready, j + 1)
                    wait(pe, x2_lo_ready, j - 1)
                    for c in range(KC):
                        mm = pe.transpose(pT[:, r % 2, c * P:(c + 1) * P], xn2[:, r % 2, c * P:(c + 1) * P], ident[:])
                    mm.then_inc(x2t_done, 1)

                def expert(k, n):
                    j, r, turn = at(k, n)
                    e = pe.value_load(expert_of[0:1, bass.ds(j, 1)], min_val=0, max_val=NE - 1)
                    pe.wait_ge(wf_lo_ready, e + 1)
                    return e

                def product(k, n, e):
                    j, r, turn = at(k, n)
                    wait(pe, y2_ready, j - 1)
                    pe.wait_ge(x2_lo_ready, j + 1)
                    hi, lo = x2_hi[:, r % 2, :], x2_lo[:, r % 2, :]
                    for c in range(KC):
                        for m, (a, part) in enumerate(((hi, 0), (hi, 1), (lo, 0))):
                            o = (part * KC + c) * DM
                            w = wf_hl[:, bass.ds(e, 1), o:o + DM].rearrange("p a n -> p (a n)")
                            mm = pe.matmul(pA[:, r % 2, :], a[:, c * P:(c + 1) * P], w,
                                           start=(c == 0 and m == 0), stop=(c == KC - 1 and m == 2))
                    mm.then_inc(f_done, 1)

                def body(k, n):
                    first = isinstance(k, int) and R * k + n == 0
                    if first:
                        transpose(k, n + 1)
                    if is_block(k, n):
                        e = expert(k, n)
                    if is_block(k, n + 1) and not first:
                        transpose(k, n + 1)
                    if is_block(k, n):
                        product(k, n, e)

                blocks(pe, body)


def position_table():
    pos = np.arange(S, dtype=np.float32)[:, None]
    div = np.exp(np.arange(0, DP, 2, dtype=np.float32) * np.float32(-np.log(10000.0) / DP))
    ang = (pos * div).astype(np.float32)
    pe = np.zeros((S, DP), np.float32)
    pe[:, 0::2] = np.sin(ang)
    pe[:, 1::2] = np.cos(ang)
    return np.ascontiguousarray(pe.T)


def route_table():
    p = np.arange(P)
    before = (p[:, None] < p[None, :]).astype(np.float32)
    slot = np.concatenate([PB * np.arange(NR) + i for i in range(PB)])
    place = np.stack([(p // B == i) for i in range(PB)]).astype(np.float32)
    rows = lambda v: np.broadcast_to(np.asarray(v, np.float32)[None, :], (P, len(v)))
    return np.ascontiguousarray(np.concatenate([
        before, np.ones((P, P)), rows(slot), rows(place.reshape(-1)), rows(np.arange(NE) - NE),
        (S * (p % B))[:, None], rows(np.arange(NR)), np.stack([p, P + p], axis=1)], axis=1), dtype=np.float32)


def kernel(**inputs):
    import concourse.bacc as _bacc
    from concourse.bass_utils import run_bass_kernel_spmd as _run

    a = {k: np.asarray(v) for k, v in inputs.items()}
    c = np.ascontiguousarray
    ctx_t = a["ctx_1024"].reshape(B, NBLKS, BK, KC, P).transpose(0, 1, 4, 3, 2)
    mask = a["mask_BxSxS2_bk0"].reshape(B, 2, P, NBLKS, BK).transpose(3, 2, 0, 1, 4)
    pad = a["mask_BxS2_bf1"].reshape(B, 2, P).transpose(2, 0, 1)
    arrays = {
        "x": a["x"].reshape(B * S, DM),
        "ctx_t": ctx_t,
        "mask": mask,
        "pad": pad,
        "wq": a["L0_xattn_Wq"].T, "wk": a["L0_xattn_Wk"].T, "wv": a["L0_xattn_Wv"].T, "wo": a["L0_xattn_Wo"].T,
        "sigs_t": a["L0_ffn_tile_sigs"].T,
        "wf": a["L0_ffn_W"].transpose(0, 2, 1),
        "bf": a["L0_ffn_b"],
        "ident": np.eye(P, dtype=np.float32),
        "route": route_table(),
        "pe_t": position_table(),
    }
    nc = _bacc.Bacc("TRN2", target_bir_lowering=False, num_devices=1)
    feeds, args = {}, []
    for name, v in arrays.items():
        v = c(v)
        feeds[f"in_{name}"] = v
        args.append(nc.dram_tensor(f"in_{name}", v.shape, mybir.dt.from_np(v.dtype), kind="ExternalInput").ap())
    out = nc.dram_tensor("out_0_dram", (B * S, DM), F32, kind="ExternalOutput").ap()
    kernel_program(nc, *args, out)
    r = _run(nc, [feeds], core_ids=[0])
    return r.results[0]["out_0_dram"].reshape(B, S, DM)
```
